# Optimizing a Trainium2 kernel written in Bass

```python
import numpy as np
import jax
import jax.numpy as jnp

def _softmax(x, axis=-1):
    return jax.nn.softmax(x, axis=axis)

def _gelu(x):
    return jax.nn.gelu(x, approximate=True)

def _silu(x):
    return jax.nn.silu(x)

def _sigmoid(x):
    return jax.nn.sigmoid(x)

def _layernorm(x, axis=-1, eps=1e-05):
    m = jnp.mean(x, axis=axis, keepdims=True)
    v = jnp.var(x, axis=axis, keepdims=True)
    return (x - m) / jnp.sqrt(v + eps)

def _scatter_add(tgt, idx, src, axis=0):
    return tgt.at[idx].add(src)

def _segment_sum(src, seg, n):
    return jax.ops.segment_sum(src, seg, n)
kernel_name = 'mk_perceiver_d1_seqx_r4_9c0083'

def setup_inputs(seed: int=0):
    np.random.seed(seed)
    _w = jnp.asarray

    def _rec_inputs():
        import jax
        import jax.numpy as jnp
        _rk = jax.random.key(seed)
        x = -0.0002928 + 1 * jax.random.normal(jax.random.fold_in(_rk, 1), (2, 256, 256), jnp.float32)
        _lenS = 256 - jax.random.randint(jax.random.fold_in(_rk, 7), (2,), 0, max(1, 256 // 4) + 1, jnp.int32)
        _lenS2 = 4096 - jax.random.randint(jax.random.fold_in(_rk, 8), (2,), 0, max(1, 4096 // 4) + 1, jnp.int32)
        _ctx_1024P = jax.random.normal(jax.random.fold_in(_rk, 11), (2, 16, 256), jnp.float32)
        _ctx_1024c = jax.random.dirichlet(jax.random.fold_in(_rk, 511), 0.3 * jnp.ones((16,), jnp.float32), (2, 4096))
        _ctx_1024t = jnp.einsum('bsk,bkd->bsd', _ctx_1024c, _ctx_1024P)
        _ctx_1024t = _ctx_1024t * jax.lax.rsqrt(jnp.mean(jnp.square(_ctx_1024t)) + 1e-12) * 0.953939
        ctx_1024 = 4.13588e-05 + 0.999923 * (_ctx_1024t + 0.3 * jax.random.normal(jax.random.fold_in(_rk, 611), (2, 4096, 256), jnp.float32))
        return (x, ctx_1024)
    x, ctx_1024 = _rec_inputs()

    def _L0_xattn_setup():
        import jax, jax.numpy as jnp
        import numpy as np
        HIDDEN = 256
        HEADS = 16
        HEAD_DIM = 64
        key = jax.random.key(seed)
        ks = jax.random.split(key, 7)
        B, Q, K = (2, 512, 1024)
        s = 1.0 / np.sqrt(HIDDEN)
        return {'query': jax.random.normal(ks[0], (B, Q, HIDDEN), dtype=jnp.float32), 'key': jax.random.normal(ks[1], (B, K, HIDDEN), dtype=jnp.float32), 'value': jax.random.normal(ks[2], (B, K, HIDDEN), dtype=jnp.float32), 'w_q': jax.random.normal(ks[3], (HIDDEN, HEADS * HEAD_DIM), dtype=jnp.float32) * s, 'w_k': jax.random.normal(ks[4], (HIDDEN, HEADS * HEAD_DIM), dtype=jnp.float32) * s, 'w_v': jax.random.normal(ks[5], (HIDDEN, HEADS * HEAD_DIM), dtype=jnp.float32) * s, 'w_o': jax.random.normal(ks[6], (HEADS * HEAD_DIM, HIDDEN), dtype=jnp.float32) * s}
    _L0_xattn_all = _L0_xattn_setup()
    _L0_xattn_in = {k: v for k, v in _L0_xattn_all.items() if k in ('w_q', 'w_k', 'w_v', 'w_o')}
    del _L0_xattn_all

    def _L0_attn_setup():
        import jax, jax.numpy as jnp
        import numpy as np
        D_MODEL = 256
        N_HEADS = 16
        DIM_HEAD = 64
        NUM_MEM_KV = 16
        INNER = N_HEADS * DIM_HEAD
        key = jax.random.key(seed)
        ks = jax.random.split(key, 8)
        s = 0.02
        x = jax.random.normal(ks[0], (2, 512, D_MODEL), dtype=jnp.float32)
        Wq = jax.random.normal(ks[1], (D_MODEL, INNER), dtype=jnp.float32) * s
        Wkv = jax.random.normal(ks[2], (D_MODEL, 2 * INNER), dtype=jnp.float32) * s
        Wo = jax.random.normal(ks[3], (INNER, D_MODEL), dtype=jnp.float32) * s
        pre_proj = jax.random.normal(ks[4], (N_HEADS, N_HEADS), dtype=jnp.float32)
        post_proj = jax.random.normal(ks[5], (N_HEADS, N_HEADS), dtype=jnp.float32)
        mem_k = jax.random.normal(ks[6], (N_HEADS, NUM_MEM_KV, DIM_HEAD), dtype=jnp.float32)
        mem_v = jax.random.normal(ks[7], (N_HEADS, NUM_MEM_KV, DIM_HEAD), dtype=jnp.float32)
        return {'x': x, 'Wq': Wq, 'Wkv': Wkv, 'Wo': Wo, 'pre_proj': pre_proj, 'post_proj': post_proj, 'mem_k': mem_k, 'mem_v': mem_v}
    _L0_attn_all = _L0_attn_setup()
    _L0_attn_in = {k: v for k, v in _L0_attn_all.items() if k in ('Wq', 'Wkv', 'Wo', 'pre_proj', 'post_proj', 'mem_k', 'mem_v')}
    del _L0_attn_all

    def _L0_ffn_setup():
        import jax, jax.numpy as jnp
        import numpy as np
        BLOCK = 32
        W_BITS = 4
        ACT_BITS = 16

        def act_qdq(x):
            qmax = 2.0 ** (ACT_BITS - 1) - 1.0
            scale = jnp.maximum(jnp.max(jnp.abs(x)) / qmax, 1e-12)
            return jnp.clip(jnp.round(x / scale), -qmax - 1.0, qmax) * scale

        def fixed_qdq_u16(x):
            scale = 1.0 / 65536.0
            return jnp.clip(jnp.round(x / scale), 0.0, 65535.0) * scale

        def lpbq_dequant(w):
            O, I = w.shape
            qmax = 2.0 ** (W_BITS - 1) - 1.0
            wb = w.reshape(O, I // BLOCK, BLOCK)
            s = jnp.maximum(jnp.max(jnp.abs(wb), axis=-1, keepdims=True) / qmax, 1e-12)
            wq = jnp.clip(jnp.round(wb / s), -qmax - 1.0, qmax) * s
            return wq.reshape(O, I)
        key = jax.random.key(seed)
        k1, k2, k3, k4 = jax.random.split(key, 4)
        B, S, H, I = (2, 1024, 256, 768)
        x = jax.random.normal(k1, (B, S, H), jnp.float32)
        w_gate = jax.random.normal(k2, (I, H), jnp.float32) * 0.02
        w_up = jax.random.normal(k3, (I, H), jnp.float32) * 0.02
        w_down = jax.random.normal(k4, (H, I), jnp.float32) * 0.02
        return {'x': x, 'w_gate': w_gate, 'w_up': w_up, 'w_down': w_down}
    _L0_ffn_all = _L0_ffn_setup()
    _L0_ffn_in = {k: v for k, v in _L0_ffn_all.items() if k in ('w_gate', 'w_up', 'w_down')}
    del _L0_ffn_all
    return {'x': x, 'ctx_1024': ctx_1024, 'L0_xattn_w_q': _L0_xattn_in['w_q'], 'L0_xattn_w_k': _L0_xattn_in['w_k'], 'L0_xattn_w_v': _L0_xattn_in['w_v'], 'L0_xattn_w_o': _L0_xattn_in['w_o'], 'L0_attn_Wq': _L0_attn_in['Wq'], 'L0_attn_Wkv': _L0_attn_in['Wkv'], 'L0_attn_Wo': _L0_attn_in['Wo'], 'L0_attn_pre_proj': _L0_attn_in['pre_proj'], 'L0_attn_post_proj': _L0_attn_in['post_proj'], 'L0_attn_mem_k': _L0_attn_in['mem_k'], 'L0_attn_mem_v': _L0_attn_in['mem_v'], 'L0_ffn_w_gate': _L0_ffn_in['w_gate'], 'L0_ffn_w_up': _L0_ffn_in['w_up'], 'L0_ffn_w_down': _L0_ffn_in['w_down']}

def reference(x, ctx_1024, L0_xattn_w_q, L0_xattn_w_k, L0_xattn_w_v, L0_xattn_w_o, L0_attn_Wq, L0_attn_Wkv, L0_attn_Wo, L0_attn_pre_proj, L0_attn_post_proj, L0_attn_mem_k, L0_attn_mem_v, L0_ffn_w_gate, L0_ffn_w_up, L0_ffn_w_down):
    import jax
    import jax.numpy as jnp

    def _L0_xattn_ref(query, key, value, w_q, w_k, w_v, w_o):
        import jax, jax.numpy as jnp
        import numpy as np
        HIDDEN = 256
        HEADS = 16
        HEAD_DIM = 64
        B, Q, _ = query.shape
        Kl = key.shape[1]
        scale = HEAD_DIM ** (-0.5)
        q = (query @ w_q).reshape(B, Q, HEADS, HEAD_DIM).transpose(0, 2, 1, 3)
        k = (key @ w_k).reshape(B, Kl, HEADS, HEAD_DIM).transpose(0, 2, 1, 3)
        v = (value @ w_v).reshape(B, Kl, HEADS, HEAD_DIM).transpose(0, 2, 1, 3)
        scores = jnp.einsum('bhqd,bhkd->bhqk', q, k) * scale
        attn = jax.nn.softmax(scores, axis=-1)
        out = jnp.einsum('bhqk,bhkd->bhqd', attn, v)
        out = out.transpose(0, 2, 1, 3).reshape(B, Q, HEADS * HEAD_DIM)
        return out @ w_o

    def _L0_attn_ref(x, Wq, Wkv, Wo, pre_proj, post_proj, mem_k, mem_v):
        import jax, jax.numpy as jnp
        import numpy as np
        D_MODEL = 256
        N_HEADS = 16
        DIM_HEAD = 64
        NUM_MEM_KV = 16
        INNER = N_HEADS * DIM_HEAD
        b, n, _ = x.shape
        scale = DIM_HEAD ** (-0.5)
        q = x @ Wq
        kv = x @ Wkv
        k, v = jnp.split(kv, 2, axis=-1)
        split_heads = lambda t: t.reshape(b, n, N_HEADS, DIM_HEAD).transpose(0, 2, 1, 3)
        q, k, v = (split_heads(q), split_heads(k), split_heads(v))
        mk = jnp.broadcast_to(mem_k[None], (b, N_HEADS, NUM_MEM_KV, DIM_HEAD))
        mv = jnp.broadcast_to(mem_v[None], (b, N_HEADS, NUM_MEM_KV, DIM_HEAD))
        k = jnp.concatenate([mk, k], axis=2)
        v = jnp.concatenate([mv, v], axis=2)
        dots = jnp.einsum('bhid,bhjd->bhij', q, k) * scale
        dots = jnp.einsum('bhij,hk->bkij', dots, pre_proj)
        i, j = (dots.shape[-2], dots.shape[-1])
        causal = jnp.triu(jnp.ones((i, j), dtype=bool), k=j - i + 1)
        mask_value = jnp.finfo(dots.dtype).min
        dots = jnp.where(causal[None, None], mask_value, dots)
        attn = jax.nn.softmax(dots, axis=-1)
        attn = jnp.einsum('bhij,hk->bkij', attn, post_proj)
        out = jnp.einsum('bhij,bhjd->bhid', attn, v)
        out = out.transpose(0, 2, 1, 3).reshape(b, n, INNER)
        return out @ Wo

    def _L0_ffn_ref(x, w_gate, w_up, w_down):
        import jax, jax.numpy as jnp
        import numpy as np
        BLOCK = 32
        W_BITS = 4
        ACT_BITS = 16

        def act_qdq(x):
            qmax = 2.0 ** (ACT_BITS - 1) - 1.0
            scale = jnp.maximum(jnp.max(jnp.abs(x)) / qmax, 1e-12)
            return jnp.clip(jnp.round(x / scale), -qmax - 1.0, qmax) * scale

        def fixed_qdq_u16(x):
            scale = 1.0 / 65536.0
            return jnp.clip(jnp.round(x / scale), 0.0, 65535.0) * scale

        def lpbq_dequant(w):
            O, I = w.shape
            qmax = 2.0 ** (W_BITS - 1) - 1.0
            wb = w.reshape(O, I // BLOCK, BLOCK)
            s = jnp.maximum(jnp.max(jnp.abs(wb), axis=-1, keepdims=True) / qmax, 1e-12)
            wq = jnp.clip(jnp.round(wb / s), -qmax - 1.0, qmax) * s
            return wq.reshape(O, I)
        x = act_qdq(x)
        up = act_qdq(x @ lpbq_dequant(w_up).T)
        gate = act_qdq(x @ lpbq_dequant(w_gate).T)
        sig = fixed_qdq_u16(jax.nn.sigmoid(gate))
        gate = act_qdq(gate * sig)
        o = act_qdq(gate * up)
        return o @ lpbq_dequant(w_down).T
    x = x + _L0_xattn_ref(_layernorm(x, axis=-1), ctx_1024, ctx_1024, L0_xattn_w_q, L0_xattn_w_k, L0_xattn_w_v, L0_xattn_w_o)
    x = x + _L0_attn_ref(_layernorm(x, axis=-1), L0_attn_Wq, L0_attn_Wkv, L0_attn_Wo, L0_attn_pre_proj, L0_attn_post_proj, L0_attn_mem_k, L0_attn_mem_v)
    x = x + _L0_ffn_ref(_layernorm(x, axis=-1), L0_ffn_w_gate, L0_ffn_w_up, L0_ffn_w_down)
    return x

_drawn_inputs = setup_inputs


def setup_inputs(seed=0):
    import zlib

    import numpy as np

    out = dict(_drawn_inputs(seed))
    spreads = {}
    factors = {'L0_ffn_w_gate': 2.694}
    for name, (base, spread) in spreads.items():
        noise = np.random.default_rng([zlib.crc32(name.encode()), seed]).standard_normal(out[name].shape)
        drawn = base * np.exp(spread * noise) if base else spread * noise
        out[name] = jnp.asarray(drawn.astype(out[name].dtype))
    for name, factor in factors.items():
        out[name] = (out[name] * factor).astype(out[name].dtype)
    return out
```

```python
from contextlib import ExitStack

import concourse.bass as bass
from concourse import mybir

F32 = mybir.dt.float32
F32R = mybir.dt.float32r
ALU = mybir.AluOpType
ACT = mybir.ActivationFunctionType
X = mybir.AxisListType.X

P = 128
BATCH, SEQ, D = 2, 256, 256
CTX = 4096
HEADS, DH = 16, 64
INNER = HEADS * DH
TOK_TILES = BATCH * SEQ // P
QT = SEQ // P
DC = D // P
PAIRS = HEADS // 2
SCALE = DH ** -0.5
EPS = 1e-5


class Resources:

    def __init__(self, nc, stack):
        self.nc, self.stack = nc, stack

    def sbuf(self, name, shape, dtype=F32):
        return self.stack.enter_context(self.nc.sbuf_tensor(name, shape, dtype))

    def psum(self, name, shape, dtype=F32):
        return self.stack.enter_context(self.nc.psum_tensor(name, shape, dtype))

    def sem(self, name):
        return self.stack.enter_context(self.nc.semaphore(name))


def wait_past(eng, sem, value):
    if not isinstance(value, int) or value > 0:
        eng.wait_ge(sem, value)


NORMALISED = 3 * TOK_TILES


def normalise_rows(dve, x, out, stats, moments, chain, inverse_std):
    n = 0
    for t in range(TOK_TILES):
        dve.bn_stats(stats[:, t, :], x[:, t, :]).then_inc(chain, 1)
    n += TOK_TILES
    dve.wait_ge(chain, n)
    for t in range(TOK_TILES):
        dve.bn_aggr(moments[:, t, :], stats[:, t, :]).then_inc(chain, 1)
    n += TOK_TILES
    dve.wait_ge(inverse_std, 3)
    for t in range(TOK_TILES):
        dve.tensor_scalar(out[:, t, :], x[:, t, :], moments[:, t, 0:1], moments[:, t, 1:2],
                          ALU.subtract, ALU.mult).then_inc(chain, 1)
    assert n + TOK_TILES == NORMALISED


def invert_std(pool, moments, power, chain, inverse_std):
    pool.memset(power[:, :], -0.5).then_inc(inverse_std, 1)
    pool.wait_ge(chain, 2 * TOK_TILES)
    pool.tensor_scalar(moments[:, :, 1], moments[:, :, 1], EPS, None, ALU.add).then_inc(inverse_std, 1)
    pool.wait_ge(inverse_std, 2)
    pool.tensor_tensor(moments[:, :, 1], moments[:, :, 1], power[:, :], ALU.pow).then_inc(inverse_std, 1)


def cross_attention(nc, x, ctx_in, w_q, w_k, w_v, w_o, x_res, ident):
    CHUNK = 512
    STEPS = CTX // CHUNK
    KT = CHUNK // P
    LOAD = 4
    LOADS = CTX // P // LOAD
    GROUP = 4
    GROUPS = CTX // P // GROUP
    A, B = 0, 1

    with ExitStack() as stack:
        r = Resources(nc, stack)
        ctx_rows = r.sbuf("ctx_rows", [P, 2, LOAD, D])
        ctxT_hi = r.sbuf("ctxT_hi", [P, DC, CTX], F32R)
        ctxT_lo = r.sbuf("ctxT_lo", [P, DC, CTX], F32R)
        k_split = r.sbuf("k_split", [P, 2, CTX], F32R)
        k_ones = r.sbuf("k_ones", [P, 2, CTX], F32R)
        v_rows = r.sbuf("v_rows", [P, CTX // P, 2 * DH])
        q_twice = r.sbuf("q_twice", [P, 2, SEQ], F32R)
        q_low_max = r.sbuf("q_low_max", [P, 2, SEQ], F32R)
        probs = r.sbuf("probs", [P, 2, 2, KT * SEQ])
        prob_sum = r.sbuf("prob_sum", [P, 2, KT * SEQ])
        xn = prob_sum[:, 0, :].rearrange("p (t d) -> p t d", t=TOK_TILES)
        xnT = r.sbuf("xnT", [P, DC, BATCH * SEQ])
        stats = r.sbuf("stats", [P, TOK_TILES, 6])
        moments = r.sbuf("moments", [P, TOK_TILES, 2])
        power = r.sbuf("power", [P, TOK_TILES])
        w_raw = r.sbuf("w_raw", [P, 3, DC, 2 * DH])
        w_hi = r.sbuf("w_hi", [P, 2, DC, 2 * DH], F32R)
        w_lo = r.sbuf("w_lo", [P, 2, DC, 2 * DH], F32R)
        wq_pair = r.sbuf("wq_pair", [P, DC, 2 * DH])
        wo_pair = r.sbuf("wo_pair", [P, D])
        step_max = r.sbuf("step_max", [P, QT, 2, STEPS])
        row_max = r.sbuf("row_max", [P, QT, 2])
        neg_max = r.sbuf("neg_max", [P, QT, P])
        recip = r.sbuf("recip", [P, SEQ])
        outT = r.sbuf("outT", [P, SEQ])
        ones = r.sbuf("ones", [P, DH])

        scores = [r.psum("scores_a", [P, 2, CHUNK]), r.psum("scores_b", [P, 2, CHUNK])]
        k_ps = [r.psum("k_ps0", [P, CHUNK]), r.psum("k_ps1", [P, CHUNK])]
        v_ps = r.psum("v_ps", [P, CHUNK])
        out_ps = r.psum("out_ps", [P, CHUNK])
        flat_scores = [s[:, :, :].rearrange("p a b -> p (a b)") for s in scores]

        x_loaded = r.sem("x_loaded")
        ctx_loaded = [r.sem("ctx_loaded0"), r.sem("ctx_loaded1")]
        w_loaded = r.sem("w_loaded")
        wo_loaded = r.sem("wo_loaded")
        consts_ready = r.sem("consts_ready")
        norm_chain = r.sem("norm_chain")
        inverse_std = r.sem("inverse_std")
        xT_made = r.sem("xT_made")
        xT_copied = r.sem("xT_copied")
        ctxT_made = r.sem("ctxT_made")
        ctx_high = r.sem("ctx_high")
        ctx_low = r.sem("ctx_low")
        w_high = r.sem("w_high")
        w_low = r.sem("w_low")
        wq_copied = r.sem("wq_copied")
        q_made = r.sem("q_made")
        q_high = r.sem("q_high")
        q_low = r.sem("q_low")
        k_made = r.sem("k_made")
        k_high = r.sem("k_high")
        k_low = r.sem("k_low")
        k_copied = r.sem("k_copied")
        v_made = r.sem("v_made")
        v_copied = r.sem("v_copied")
        pre_made = r.sem("pre_made")
        max_done = r.sem("max_done")
        max_chain = r.sem("max_chain")
        maxT_made = r.sem("maxT_made")
        max_ready = r.sem("max_ready")
        scores_made = r.sem("scores_made")
        exp_done = r.sem("exp_done")
        sum_done = r.sem("sum_done")
        fold_done = r.sem("fold_done")
        pv_done = r.sem("pv_done")
        den_made = r.sem("den_made")
        recip_done = r.sem("recip_done")
        outT_ready = r.sem("outT_ready")
        y_made = r.sem("y_made")
        y_added = r.sem("y_added")

        def pairs_of_batch(eng, b, body):
            body(b * PAIRS, b, 0)
            with eng.Fori(1, PAIRS) as i:
                body(b * PAIRS + i, b, i)

        def act_context(act, b):
            for g in range(GROUPS):
                n = b * GROUPS + g
                act.wait_ge(ctxT_made, n + 1)
                act.activation(ctxT_hi[:, :, g * CHUNK:(g + 1) * CHUNK], scores[n % 2][:, :, :], ACT.Copy
                               ).then_inc(ctx_high, 1)

        x_tiles = x.rearrange("b (t p) d -> p (b t) d", p=P)
        ctx_tiles = ctx_in.rearrange("b (p t) d -> b p t d", p=P)
        block = stack.enter_context(nc.Block())

        @block.sync
        def _(sp):
            sp.dma_start(x_res[:, :, :], x_tiles).then_inc(x_loaded, 16)
            for b in range(BATCH):
                for n in range(LOADS):
                    at = b * LOADS + n
                    if at >= 2:
                        sp.wait_ge(ctxT_made, (at - 1) * LOAD // GROUP)
                    sp.dma_start(ctx_rows[:, at % 2, :, :],
                                 ctx_tiles[b, :, n * LOAD:(n + 1) * LOAD, :]).then_inc(ctx_loaded[at % 2], 16)

                def body(it, b, i):
                    wait_past(sp, w_low, it)
                    wait_past(sp, wq_copied, it)
                    cols = bass.ds(i * 2 * DH, 2 * DH)
                    for n, w in enumerate((w_q, w_k, w_v)):
                        sp.dma_start(w_raw[:, n, :, :], w[:, cols].rearrange("(c p) n -> p c n", p=P)
                                     ).then_inc(w_loaded, 16)
                    wait_past(sp, y_made, it)
                    sp.dma_start(wo_pair[:, :], w_o[bass.ds(i * P, P), :]).then_inc(wo_loaded, 16)
                pairs_of_batch(sp, b, body)

        @block.gpsimd
        def _(pool):
            for s in (0, 1):
                pool.memset(k_ones[:, s, :].bitcast(F32), 0.0).then_inc(consts_ready, 1)
            pool.memset(neg_max[:, :, :], 0.0).then_inc(consts_ready, 1)
            pool.memset(ones[:, :], 1.0).then_inc(consts_ready, 1)
            pool.wait_ge(consts_ready, 4)
            pool.memset(k_ones[DH:DH + 1, A, :].bitcast(F32), 1.0).then_inc(consts_ready, 1)
            pool.memset(k_ones[0:1, B, :].bitcast(F32), 1.0).then_inc(consts_ready, 1)
            pool.wait_ge(consts_ready, 6)
            invert_std(pool, moments, power, norm_chain, inverse_std)

            def body(it, b, i):
                pool.wait_ge(w_high, it + 1)
                pool.tensor_tensor(w_lo[:, :, :, :], w_raw[:, 1:3, :, :], w_hi[:, :, :, :].bitcast(F32),
                                   ALU.subtract).then_inc(w_low, 1)
            for b in range(BATCH):
                pairs_of_batch(pool, b, body)

        @block.scalar
        def _(act):
            act.wait_ge(consts_ready, 6)

            def body(it, b, i):
                act.wait_ge(w_loaded, 48 * it + 48)
                wait_past(act, v_made, STEPS * it)
                act.activation(w_hi[:, :, :, :], w_raw[:, 1:3, :, :], ACT.Copy).then_inc(w_high, 1)
                act.activation(wq_pair[:, :, :], w_raw[:, 0, :, :], ACT.Copy).then_inc(wq_copied, 1)
                act.wait_ge(q_made, it + 1)
                for h in (A, B):
                    for half in (0, DH):
                        act.activation(q_twice[half:half + DH, h, :], out_ps[h * DH:(h + 1) * DH, 0:SEQ],
                                       ACT.Copy).then_inc(q_high, 1)
                for j in range(STEPS):
                    keys = slice(j * CHUNK, (j + 1) * CHUNK)
                    n = STEPS * it + j
                    act.wait_ge(k_made, n + 1)
                    ps = k_ps[j % 2]
                    act.activation(k_split[0:DH, A, keys], ps[0:DH, :], ACT.Copy).then_inc(k_high, 1)
                    act.activation(k_split[DH:P, B, keys], ps[DH:P, :], ACT.Copy).then_inc(k_high, 1)
                    act.wait_ge(v_made, n + 1)
                    act.wait_ge(k_high, 2 * n + 2)
                    act.activation(v_rows[:, j * KT:(j + 1) * KT, :], v_ps[:, :].rearrange("p (t d) -> p t d", t=KT),
                                   ACT.Copy).then_inc(v_copied, 1)
                    act.activation(k_ones[0:DH, A, keys], k_split[0:DH, A, keys].bitcast(F32), ACT.Copy
                                   ).then_inc(k_copied, 1)
                    act.activation(k_ones[DH:P, B, keys], k_split[DH:P, B, keys].bitcast(F32), ACT.Copy
                                   ).then_inc(k_copied, 1)
                act.wait_ge(maxT_made, it + 1)
                act.activation(q_low_max[DH:P, A, :], v_ps[DH:P, 0:SEQ], ACT.Copy).then_inc(max_ready, 1)
                act.activation(q_low_max[0:DH, B, :], v_ps[0:DH, 0:SEQ], ACT.Copy).then_inc(max_ready, 1)
                for j in range(STEPS):
                    for h in (A, B):
                        n = 2 * (STEPS * it + j) + h
                        act.wait_ge(scores_made, n + 1)
                        if j >= 2 or not (b == 0 and isinstance(i, int)):
                            act.wait_ge(sum_done, n - 3)
                            act.wait_ge(pv_done, STEPS * it + j - 1)
                        act.activation(probs[:, j % 2, h, :], flat_scores[h], ACT.Exp, scale=SCALE
                                       ).then_inc(exp_done, 1)
            for b in range(BATCH):
                act_context(act, b)
                pairs_of_batch(act, b, body)

        @block.vector
        def _(dve):
            dve.wait_ge(x_loaded, 16)
            normalise_rows(dve, x_res, xn, stats, moments, norm_chain, inverse_std)

            def divide(before):
                dve.wait_ge(den_made, before + 1)
                dve.reciprocal(recip[:, :], k_ps[1][:, 0:SEQ]).then_inc(recip_done, 1)
                dve.wait_ge(recip_done, before + 1)
                wait_past(dve, y_made, before)
                dve.tensor_tensor(outT[:, :], out_ps[:, SEQ:2 * SEQ], recip[:, :], ALU.mult).then_inc(outT_ready, 1)

            def add_output(before, b):
                dve.wait_ge(y_made, before + 1)
                dst = x_res[:, b * QT:(b + 1) * QT, :]
                dve.tensor_tensor(dst, dst, k_ps[0][:, :].rearrange("p (t d) -> p t d", t=QT), ALU.add
                                  ).then_inc(y_added, 1)

            def body(it, b, i):
                dve.wait_ge(q_high, 4 * it + 4)
                dve.tensor_tensor(q_low_max[0:DH, A, :], out_ps[0:DH, 0:SEQ], q_twice[0:DH, A, :].bitcast(F32),
                                  ALU.subtract).then_inc(q_low, 1)
                dve.tensor_tensor(q_low_max[DH:P, B, :], out_ps[DH:P, 0:SEQ], q_twice[DH:P, B, :].bitcast(F32),
                                  ALU.subtract).then_inc(q_low, 1)
                for j in range(STEPS + 1):
                    if j < STEPS:
                        keys = slice(j * CHUNK, (j + 1) * CHUNK)
                        n = STEPS * it + j
                        ps = k_ps[j % 2]
                        dve.wait_ge(k_high, 2 * n + 2)
                        dve.tensor_tensor(k_split[DH:P, A, keys], ps[0:DH, :], k_split[0:DH, A, keys].bitcast(F32),
                                          ALU.subtract).then_inc(k_low, 1)
                        dve.tensor_tensor(k_split[0:DH, B, keys], ps[DH:P, :], k_split[DH:P, B, keys].bitcast(F32),
                                          ALU.subtract).then_inc(k_low, 1)
                    if j > 0:
                        for h in (A, B):
                            dve.wait_ge(pre_made, 2 * (STEPS * it + j - 1) + h + 1)
                            dve.tensor_reduce(step_max[:, :, 1 - h, j - 1], scores[h][:, :, :], X, ALU.max
                                              ).then_inc(max_done, 1)
                dve.wait_ge(max_done, 2 * STEPS * (it + 1))
                dve.tensor_reduce(row_max[:, :, :], step_max[:, :, :, :], X, ALU.max).then_inc(max_chain, 1)
                dve.wait_ge(max_chain, 2 * it + 1)
                dve.tensor_scalar(neg_max[:, :, 0:P:DH], row_max[:, :, :], -1.0, None, ALU.mult
                                  ).then_inc(max_chain, 1)
                for j in range(STEPS):
                    for h in (A, B):
                        n = 2 * (STEPS * it + j) + h
                        dve.wait_ge(exp_done, n + 1)
                        if j == 0:
                            dve.tensor_copy(prob_sum[:, h, :], probs[:, 0, h, :]).then_inc(sum_done, 1)
                        else:
                            dve.wait_ge(sum_done, n - 1)
                            dve.tensor_tensor(prob_sum[:, h, :], prob_sum[:, h, :], probs[:, j % 2, h, :], ALU.add
                                              ).then_inc(sum_done, 1)
                dve.wait_ge(sum_done, 2 * STEPS * (it + 1))
                half = KT * SEQ // 2
                dve.tensor_tensor(prob_sum[:, :, 0:half], prob_sum[:, :, 0:half], prob_sum[:, :, half:2 * half],
                                  ALU.add).then_inc(fold_done, 1)
                dve.wait_ge(fold_done, 2 * it + 1)
                dve.tensor_tensor(prob_sum[:, :, 0:SEQ], prob_sum[:, :, 0:SEQ], prob_sum[:, :, SEQ:2 * SEQ],
                                  ALU.add).then_inc(fold_done, 1)
                divide(it)
                add_output(it, b)
            for b in range(BATCH):
                for g in range(GROUPS):
                    n = b * GROUPS + g
                    dve.wait_ge(ctx_high, n + 1)
                    cols = slice(g * CHUNK, (g + 1) * CHUNK)
                    dve.tensor_tensor(ctxT_lo[:, :, cols], scores[n % 2][:, :, :], ctxT_hi[:, :, cols].bitcast(F32),
                                      ALU.subtract).then_inc(ctx_low, 1)
                    if n == 3:
                        for c in range(DC):
                            dve.wait_ge(xT_made, c + 1)
                            dve.tensor_copy(xnT[:, c, :], k_ps[c][:, :]).then_inc(xT_copied, 1)
                pairs_of_batch(dve, b, body)

        @block.tensor
        def _(pe):
            mm = pe.matmul

            def transpose_context(b, g):
                n = b * GROUPS + g
                if g % (LOAD // GROUP) == 0:
                    load = n * GROUP // LOAD
                    pe.wait_ge(ctx_loaded[load % 2], 16 * (load // 2 + 1))
                if n >= 2:
                    pe.wait_ge(ctx_low, n - 1)
                for t in range(GROUP):
                    tile = g * GROUP + t
                    slot = (b * LOADS + tile // LOAD) % 2
                    for c in range(DC):
                        last = pe.transpose(scores[n % 2][:, c, t * P:(t + 1) * P],
                                            ctx_rows[:, slot, tile % LOAD, c * P:(c + 1) * P], ident[:, :])
                last.then_inc(ctxT_made, 1)

            def transpose_x():
                pe.wait_ge(norm_chain, NORMALISED)
                for c in range(DC):
                    for t in range(TOK_TILES):
                        last = pe.transpose(k_ps[c][:, t * P:(t + 1) * P], xn[:, t, c * P:(c + 1) * P], ident[:, :])
                    last.then_inc(xT_made, 1)

            def project_q(it, b):
                pe.wait_ge(wq_copied, it + 1)
                for c in range(DC):
                    last = mm(out_ps[:, 0:SEQ], wq_pair[:, c, :], xnT[:, c, b * SEQ:(b + 1) * SEQ],
                              start=(c == 0), stop=(c == DC - 1))
                last.then_inc(q_made, 1)

            def project_k(it, j):
                keys = slice(j * CHUNK, (j + 1) * CHUNK)
                passes = [(w, s, c) for w, s in ((w_hi, ctxT_lo), (w_lo, ctxT_hi), (w_hi, ctxT_hi)) for c in range(DC)]
                for n, (w, s, c) in enumerate(passes):
                    last = mm(k_ps[j % 2][:, :], w[:, 0, c, :], s[:, c, keys], start=(n == 0),
                              stop=(n == len(passes) - 1))
                last.then_inc(k_made, 1)

            def project_v(it, j):
                for t in range(KT):
                    keys = slice((j * KT + t) * P, (j * KT + t + 1) * P)
                    passes = [(s, w, c) for c in range(DC) for s, w in ((ctxT_lo, w_hi), (ctxT_hi, w_lo), (ctxT_hi, w_hi))]
                    for n, (s, w, c) in enumerate(passes):
                        last = mm(v_ps[:, t * P:(t + 1) * P], s[:, c, keys], w[:, 1, c, :], start=(n == 0),
                                  stop=(n == len(passes) - 1))
                last.then_inc(v_made, 1)

            def scores_for_max(it, j, b, i):
                keys = slice(j * CHUNK, (j + 1) * CHUNK)
                pe.wait_ge(k_low, 2 * (STEPS * it + j + 1))
                for h in (A, B):
                    if j > 0:
                        pe.wait_ge(max_done, 2 * (STEPS * it + j - 1) + h + 1)
                    else:
                        wait_past(pe, exp_done, 2 * STEPS * it)
                    for qt in range(QT):
                        last = mm(scores[h][:, qt, :], q_twice[:, h, qt * P:(qt + 1) * P], k_split[:, h, keys],
                                  start=True, stop=True)
                    last.then_inc(pre_made, 1)

            def scores_by_keys(it, j, h):
                if j > 0:
                    pe.wait_ge(exp_done, 2 * (STEPS * it + j - 1) + h + 1)
                for t in range(KT):
                    keys = slice((j * KT + t) * P, (j * KT + t + 1) * P)
                    out = flat_scores[h][:, t * SEQ:(t + 1) * SEQ]
                    mm(out, k_split[:, h, keys], q_twice[:, h, :], start=True, stop=False)
                    last = mm(out, k_ones[:, h, keys], q_low_max[:, h, :], start=False, stop=True)
                last.then_inc(scores_made, 1)

            def product_with_v(it, j):
                pe.wait_ge(exp_done, 2 * (STEPS * it + j) + 2)
                for t in range(KT):
                    for h in (A, B):
                        last = mm(out_ps[h * DH:(h + 1) * DH, SEQ:2 * SEQ],
                                  v_rows[:, j * KT + t, h * DH:(h + 1) * DH],
                                  probs[:, j % 2, h, t * SEQ:(t + 1) * SEQ],
                                  start=(j == 0 and t == 0), stop=(j == STEPS - 1 and t == KT - 1))
                last.then_inc(pv_done, 1)

            def body(it, b, i):
                project_q(it, b)
                pe.wait_ge(w_low, it + 1)
                for j in range(STEPS):
                    if j >= 2:
                        pe.wait_ge(k_low, 2 * (STEPS * it + j - 1))
                    elif j == 0:
                        wait_past(pe, y_added, it)
                    project_k(it, j)
                    if j > 0:
                        scores_for_max(it, j - 1, b, i)
                        wait_past(pe, v_copied, STEPS * it + j - 1)
                        project_v(it, j - 1)
                scores_for_max(it, STEPS - 1, b, i)
                pe.wait_ge(v_copied, STEPS * it + STEPS - 1)
                project_v(it, STEPS - 1)
                pe.wait_ge(max_chain, 2 * it + 2)
                pe.wait_ge(v_copied, STEPS * it + STEPS)
                for qt in range(QT):
                    last = pe.transpose(v_ps[:, qt * P:(qt + 1) * P], neg_max[:, qt, :], ident[:, :])
                last.then_inc(maxT_made, 1)
                pe.wait_ge(q_low, 2 * it + 2)
                pe.wait_ge(max_ready, 2 * it + 2)
                pe.wait_ge(k_copied, 2 * STEPS * (it + 1))
                for j in range(STEPS):
                    for h in (A, B):
                        scores_by_keys(it, j, h)
                    if j > 0:
                        product_with_v(it, j - 1)
                product_with_v(it, STEPS - 1)
                pe.wait_ge(fold_done, 2 * it + 2)
                for h in (A, B):
                    last = mm(k_ps[1][h * DH:(h + 1) * DH, 0:SEQ], ones[:, :], prob_sum[:, h, 0:SEQ],
                              start=True, stop=True)
                last.then_inc(den_made, 1)
                pe.wait_ge(outT_ready, it + 1)
                pe.wait_ge(wo_loaded, 16 * (it + 1))
                for qt in range(QT):
                    last = mm(k_ps[0][:, qt * D:(qt + 1) * D], outT[:, qt * P:(qt + 1) * P], wo_pair[:, :],
                              start=True, stop=True)
                last.then_inc(y_made, 1)

            pe.wait_ge(consts_ready, 6)
            for b in range(BATCH):
                for g in range(GROUPS):
                    transpose_context(b, g)
                    if b == 0 and g == 2:
                        transpose_x()
                if b == 0:
                    pe.wait_ge(xT_copied, DC)
                pe.wait_ge(ctx_low, (b + 1) * GROUPS)
                pairs_of_batch(pe, b, body)



MEM = 16
KEYS = MEM + SEQ
ROWS = P // HEADS
GPS = 2
STEP_ROWS = GPS * ROWS
SA_STEPS = SEQ // STEP_ROWS
LOW = -3.0e38


def self_attention(nc, w_q, w_kv, w_o, pre_proj, post_proj, mem_k, mem_v, x_res, ident):
    with ExitStack() as stack:
        r = Resources(nc, stack)
        shared = r.sbuf("shared", [P, 2 * HEADS * SEQ])
        wq_sb = shared[:, 0:DC * INNER].rearrange("p (c n) -> p c n", c=DC)
        wkv_sb = shared[:, DC * INNER:3 * DC * INNER].rearrange("p (c n) -> p c n", c=DC)
        mixed = [shared[:, n * HEADS * SEQ:(n + 1) * HEADS * SEQ].rearrange("p (k i) -> p k i", k=HEADS)
                 for n in range(2)]
        mixed_mem = r.sbuf("mixed_mem", [MEM, HEADS, SEQ])
        wo_sb = r.sbuf("wo_sb", [P, PAIRS, D])
        xn = r.sbuf("xn2", [P, TOK_TILES, D])
        xnT = r.sbuf("xnT2", [P, DC, BATCH * SEQ])
        stats = r.sbuf("stats2", [P, TOK_TILES, 6])
        moments = r.sbuf("moments2", [P, TOK_TILES, 2])
        power = r.sbuf("power2", [P, TOK_TILES])
        q_padded = r.sbuf("q_padded", [P, HEADS, BATCH * SEQ])
        kT = r.sbuf("kT", [P, PAIRS, BATCH, KEYS])
        v_sb = r.sbuf("v_sb", [P, TOK_TILES, INNER])
        memk_sb = r.sbuf("memk_sb", [P, 2, DH])
        memv_sb = r.sbuf("memv_sb", [MEM, HEADS, DH])
        dots_sb = r.sbuf("dots_sb", [P, HEADS, KEYS])
        grouped = r.sbuf("grouped", [P, 2, P // ROWS, KEYS])
        expd = r.sbuf("expd", [P, 2, GPS, KEYS])
        proj_sb = r.sbuf("proj_sb", [HEADS, 2, HEADS])
        spread = r.sbuf("spread", [HEADS, P])
        same_row = r.sbuf("same_row", [P, ROWS])
        rep = r.sbuf("rep", [P, 2, HEADS])
        kron = r.sbuf("kron", [P, 2, HEADS, ROWS])
        kron_scaled = r.sbuf("kron_scaled", [P, 2, GPS, P])
        row_of = r.sbuf("row_of", [P, 1])
        columns = r.sbuf("columns", [P, GPS, STEP_ROWS])
        weighted = r.sbuf("weighted", [P, ROWS])
        causal = r.sbuf("causal", [P, GPS, STEP_ROWS])
        top = r.sbuf("top", [P, 2, GPS])
        neg_top = r.sbuf("neg_top", [P, 2, GPS])
        total = r.sbuf("total", [P, 2, GPS])
        inv_total = r.sbuf("inv_total", [P, 2, GPS])
        outT = r.sbuf("outT2", [P, PAIRS, SEQ])

        bank = [r.psum(f"bank{n}", [P, 2, 512]) for n in range(4)]

        w_in = r.sem("w_in")
        small_in = r.sem("small_in")
        norm_chain = r.sem("norm_chain2")
        inverse_std = r.sem("inverse_std2")
        xT_made = r.sem("xT_made2")
        xT_copied = r.sem("xT_copied2")
        consts = r.sem("consts")
        zeroed = r.sem("zeroed")
        kron_made = r.sem("kron_made")
        kron_chain = r.sem("kron_chain")
        memk_made = r.sem("memk_made")
        memk_copied = r.sem("memk_copied")
        proj_made = r.sem("proj_made")
        proj_copied = [r.sem("proj_by_act"), r.sem("proj_by_dve")]
        dots_made = r.sem("dots_made")
        dots_copied = [r.sem("dots_by_act"), r.sem("dots_by_dve")]
        regrouped = r.sem("regrouped")
        mix_made = r.sem("mix_made")
        masked = r.sem("masked")
        top_done = r.sem("top_done")
        neg_done = r.sem("neg_done")
        exp_done = r.sem("exp_done2")
        tail_zero = r.sem("tail_zero")
        inv_done = r.sem("inv_done")
        kron_done = r.sem("kron_done")
        post_made = r.sem("post_made")
        mixed_by_act = r.sem("mixed_by_act")
        mixed_by_dve = r.sem("mixed_by_dve")
        out_made = r.sem("out_made")
        out_copied = r.sem("out_copied")
        y_made = r.sem("y_made2")
        y_added = r.sem("y_added2")

        Q, K, V = range(3)
        projections = [(kind, n) for n in range(PAIRS) for kind in (Q, K)] + [(V, n) for n in range(2 * TOK_TILES)]
        NPROJ = len(projections)
        DOT_STEPS = BATCH * QT * PAIRS

        def dot_keys(t):
            return MEM + (t + 1) * P

        def step_keys(s):
            return MEM + (s + 1) * STEP_ROWS

        block = stack.enter_context(nc.Block())

        @block.sync
        def _(sp):
            sp.dma_start(wq_sb, w_q.rearrange("(c p) n -> p c n", p=P)).then_inc(w_in, 16)
            sp.dma_start(wkv_sb, w_kv.rearrange("(c p) n -> p c n", p=P)).then_inc(w_in, 16)
            sp.dma_start(wo_sb[:, :, :], w_o.rearrange("(c p) n -> p c n", p=P)).then_inc(w_in, 16)
            sp.dma_start(proj_sb[:, 0, :], pre_proj).then_inc(small_in, 16)
            sp.dma_start(proj_sb[:, 1, :], post_proj).then_inc(small_in, 16)
            sp.dma_start(memv_sb[:, :, :], mem_v.rearrange("h m d -> m h d")).then_inc(small_in, 16)
            for pair in range(PAIRS):
                sp.dma_start(memk_sb[pair * MEM:(pair + 1) * MEM, :, :],
                             mem_k[2 * pair:2 * pair + 2].rearrange("h m d -> m h d")).then_inc(small_in, 16)
            for b in range(BATCH):
                for t in range(QT):
                    if b > 0:
                        sp.wait_ge(mix_made, (b - 1) * SA_STEPS + (t + 1) * SA_STEPS // QT)
                    for h in range(HEADS):
                        n = (b * QT + t) * PAIRS + h // 2
                        sp.wait_ge(dots_copied[n % 2], n // 2 + 1)
                        keys = dot_keys(t)
                        sp.dma_start(grouped[h * ROWS:(h + 1) * ROWS, t, :, 0:keys],
                                     dots_sb[:, h, 0:keys]).then_inc(regrouped, 16)

        @block.gpsimd
        def _(pool):
            pool.memset(q_padded[:, :, :], 0.0).then_inc(zeroed, 1)
            pool.memset(spread[:, :], 1.0).then_inc(consts, 1)
            for n in range(GPS):
                for c in range(STEP_ROWS):
                    pool.memset(columns[:, n, c:c + 1], float(c - n * ROWS)).then_inc(consts, 1)
            pool.wait_ge(consts, 1 + GPS * STEP_ROWS)
            pool.affine_select(out=spread[:, :], in_=spread[:, :], compare_op=ALU.is_ge, fill=0.0, base=0,
                               pattern=[[1, P]], channel_multiplier=-ROWS).then_inc(consts, 1)
            pool.wait_ge(consts, 2 + GPS * STEP_ROWS)
            pool.affine_select(out=spread[:, :], in_=spread[:, :], compare_op=ALU.is_ge, fill=0.0, base=ROWS - 1,
                               pattern=[[-1, P]], channel_multiplier=ROWS).then_inc(consts, 1)
            invert_std(pool, moments, power, norm_chain, inverse_std)
            for n in range(BATCH * SA_STEPS):
                s = n % SA_STEPS
                keys = step_keys(s)
                if n >= 2:
                    pool.wait_ge(post_made, n - 1)
                if keys < KEYS:
                    pool.memset(expd[:, n % 2, :, keys:KEYS], 0.0).then_inc(tail_zero, 1)
                pool.wait_ge(inv_done, n + 1)
                for g in range(GPS):
                    pool.tensor_scalar(kron_scaled[:, n % 2, g, :], kron[:, 1, :, :], inv_total[:, n % 2, g:g + 1],
                                       None, ALU.mult).then_inc(kron_done, 1)

        def copy_projection(copy, n):
            kind, m = projections[n]
            src = bank[n % 4][:, 0, :]
            if kind == Q:
                queries = src.rearrange("p (t g r) -> p t g r", g=P // ROWS, r=ROWS)
                for half in range(2):
                    rows = slice(half * DH, (half + 1) * DH)
                    place = q_padded[rows, 2 * m + half, :].rearrange("p (t r g) -> p t g r", g=P // ROWS, r=ROWS)
                    ins = copy(place, queries[rows])
            elif kind == K:
                ins = copy(kT[:, m, :, MEM:KEYS], src.rearrange("p (b n) -> p b n", b=BATCH))
            else:
                ins = copy(v_sb[:, m // 2, (m % 2) * 512:(m % 2 + 1) * 512], src)
            ins.then_inc(proj_copied[n % 2], 1)

        def copy_dots(eng, scaled_copy, n):
            t = n // PAIRS % QT
            pair = n % PAIRS
            keys = dot_keys(t)
            eng.wait_ge(dots_made, n + 1)
            if n >= PAIRS:
                eng.wait_ge(regrouped, 16 * HEADS * (n // PAIRS))
            scaled_copy(dots_sb[:, 2 * pair:2 * pair + 2, 0:keys], bank[n % 2][:, :, 0:keys]
                        ).then_inc(dots_copied[n % 2], 1)

        def mixed_place(n, to):
            i = n % SA_STEPS * STEP_ROWS
            return to[:, :, i:i + STEP_ROWS].rearrange("p k (g r) -> p g k r", g=GPS)

        def mixed_source(n, rows, half, at):
            return bank[n % 2][0:rows, half, at:at + GPS * P].rearrange("p (g k r) -> p g k r", g=GPS, k=HEADS)

        @block.scalar
        def _(act):
            def copy(out, src):
                return act.activation(out, src, ACT.Copy)

            def scaled_copy(out, src):
                return act.activation(out, src, ACT.Copy, scale=SCALE)

            act.wait_ge(zeroed, 1)
            for n in range(0, NPROJ, 2):
                act.wait_ge(proj_made, n + 1)
                copy_projection(copy, n)

            def exponentials(n):
                keys = step_keys(n % SA_STEPS)
                act.wait_ge(neg_done, n + 1)
                if n >= 2:
                    act.wait_ge(post_made, n - 1)
                    act.wait_ge(inv_done, n - 1)
                for g in range(GPS):
                    act.activation(expd[:, n % 2, g, 0:keys], bank[2 + n % 2][:, g, 0:keys], ACT.Exp,
                                   bias=neg_top[:, n % 2, g:g + 1], accum_out=total[:, n % 2, g:g + 1]
                                   ).then_inc(exp_done, 1)

            def copy_mixed(n):
                act.wait_ge(post_made, n + 1)
                copy(mixed_place(n, mixed[0]), mixed_source(n, P, 0, 0)).then_inc(mixed_by_act, 1)

            for b in range(BATCH):
                for n in range(b * QT * PAIRS, (b + 1) * QT * PAIRS, 2):
                    copy_dots(act, scaled_copy, n)
                first = b * SA_STEPS
                for n in range(first, first + SA_STEPS):
                    exponentials(n)
                    if n >= first + 2:
                        copy_mixed(n - 2)
                copy_mixed(first + SA_STEPS - 2)
                copy_mixed(first + SA_STEPS - 1)
                for n in range(b * PAIRS, (b + 1) * PAIRS):
                    act.wait_ge(out_made, n + 1)
                    copy(outT[:, n % PAIRS, :], bank[2 + n % 2][:, 0, 0:SEQ]).then_inc(out_copied, 1)

        @block.vector
        def _(dve):
            normalise_rows(dve, x_res, xn, stats, moments, norm_chain, inverse_std)
            for c in range(DC):
                dve.wait_ge(xT_made, c + 1)
                dve.tensor_copy(xnT[:, c, :], bank[0][:, c, :]).then_inc(xT_copied, 1)
            dve.tensor_reduce(same_row[:, :], ident[:, :].rearrange("p (h r) -> p r h", r=ROWS), X, ALU.add
                              ).then_inc(kron_chain, 1)
            dve.wait_ge(kron_made, 1)
            dve.tensor_copy(rep[:, :, :].rearrange("p a k -> p (a k)"), bank[3][:, 0, 0:2 * HEADS]
                            ).then_inc(kron_chain, 1)
            dve.wait_ge(kron_chain, 2)
            for n in range(2):
                dve.tensor_tensor(kron[:, n, :, :], rep[:, n, :].unsqueeze(2).to_broadcast([P, HEADS, ROWS]),
                                  same_row[:, :].unsqueeze(1).to_broadcast([P, HEADS, ROWS]), ALU.mult
                                  ).then_inc(kron_chain, 1)
            dve.wait_ge(consts, 3 + GPS * STEP_ROWS)
            dve.tensor_tensor(weighted[:, :], same_row[:, :], columns[:, 0, 0:ROWS], ALU.mult).then_inc(kron_chain, 1)
            dve.wait_ge(kron_chain, 5)
            dve.tensor_reduce(row_of[:, :], weighted[:, :], X, ALU.add).then_inc(kron_chain, 1)
            dve.wait_ge(kron_chain, 6)
            dve.tensor_scalar(causal[:, :, :], columns[:, :, :], row_of[:, 0:1], LOW, ALU.is_gt, ALU.mult
                              ).then_inc(kron_chain, 1)
            dve.wait_ge(kron_chain, 7)
            dve.wait_ge(memk_made, 1)
            for b in range(BATCH):
                dve.tensor_copy(kT[:, :, b, 0:MEM], bank[3][:, 1, 0:P].rearrange("p (k m) -> p k m", m=MEM)
                                ).then_inc(memk_copied, 1)
            for n in range(1, NPROJ, 2):
                dve.wait_ge(proj_made, n + 1)
                copy_projection(dve.tensor_copy, n)

            def scaled_copy(out, src):
                return dve.tensor_scalar(out, src, SCALE, None, ALU.mult)

            def maximum(n):
                keys = step_keys(n % SA_STEPS)
                ps = bank[2 + n % 2]
                dve.wait_ge(mix_made, n + 1)
                last = ps[:, :, keys - STEP_ROWS:keys]
                dve.tensor_tensor(last, last, causal[:, :, :], ALU.add).then_inc(masked, 1)
                dve.wait_ge(masked, n + 1)
                dve.tensor_reduce(top[:, n % 2, :], ps[:, :, 0:keys], X, ALU.max).then_inc(top_done, 1)
                dve.wait_ge(top_done, n + 1)
                if n >= 2:
                    dve.wait_ge(exp_done, GPS * (n - 1))
                dve.tensor_scalar(neg_top[:, n % 2, :], top[:, n % 2, :], -1.0, None, ALU.mult).then_inc(neg_done, 1)

            def invert(n):
                dve.wait_ge(exp_done, GPS * (n + 1))
                if n >= 2:
                    dve.wait_ge(kron_done, GPS * (n - 1))
                dve.reciprocal(inv_total[:, n % 2, :], total[:, n % 2, :]).then_inc(inv_done, 1)

            def copy_mixed(n):
                dve.wait_ge(post_made, n + 1)
                ins = dve.tensor_copy(mixed_place(n, mixed_mem), mixed_source(n, MEM, 1, GPS * P))
                if n % SA_STEPS >= SA_STEPS // QT:
                    ins = dve.tensor_copy(mixed_place(n, mixed[1]), mixed_source(n, P, 1, 0))
                ins.then_inc(mixed_by_dve, 1)

            for b in range(BATCH):
                for n in range(b * QT * PAIRS + 1, (b + 1) * QT * PAIRS, 2):
                    copy_dots(dve, scaled_copy, n)
                first = b * SA_STEPS
                for n in range(first, first + SA_STEPS):
                    maximum(n)
                    if n >= first + 1:
                        invert(n - 1)
                    if n >= first + 2:
                        copy_mixed(n - 2)
                invert(first + SA_STEPS - 1)
                copy_mixed(first + SA_STEPS - 2)
                copy_mixed(first + SA_STEPS - 1)
                for n in range(b * QT, (b + 1) * QT):
                    dve.wait_ge(y_made, n + 1)
                    dve.tensor_tensor(x_res[:, n, :], x_res[:, n, :], bank[n % 2][:, 0, 0:D], ALU.add
                                      ).then_inc(y_added, 1)

        @block.tensor
        def _(pe):
            mm = pe.matmul
            pe.wait_ge(small_in, 16 * (3 + PAIRS))
            pe.wait_ge(consts, 3 + GPS * STEP_ROWS)
            mm(bank[3][:, 0, 0:2 * HEADS], spread[:, :], proj_sb[:, :, :].rearrange("p a k -> p (a k)"),
               start=True, stop=True).then_inc(kron_made, 1)
            pe.transpose(bank[3][:, 1, 0:P], memk_sb[:, :, :].rearrange("p a d -> p (a d)"), ident[:, :]
                         ).then_inc(memk_made, 1)
            pe.wait_ge(norm_chain, NORMALISED)
            for c in range(DC):
                for t in range(TOK_TILES):
                    last = pe.transpose(bank[0][:, c, t * P:(t + 1) * P], xn[:, t, c * P:(c + 1) * P], ident[:, :])
                last.then_inc(xT_made, 1)
            pe.wait_ge(xT_copied, DC)
            pe.wait_ge(w_in, 48)
            pe.wait_ge(memk_copied, BATCH)
            for n, (kind, m) in enumerate(projections):
                if n >= 4:
                    pe.wait_ge(proj_copied[n % 2], (n - 4) // 2 + 1)
                for c in range(DC):
                    if kind == Q:
                        w, a = wq_sb[:, c, m * P:(m + 1) * P], xnT[:, c, :]
                    elif kind == K:
                        w, a = wkv_sb[:, c, m * P:(m + 1) * P], xnT[:, c, :]
                    else:
                        at = INNER + (m % 2) * 512
                        w, a = xnT[:, c, (m // 2) * P:(m // 2 + 1) * P], wkv_sb[:, c, at:at + 512]
                    last = mm(bank[n % 4][:, 0, :], w, a, start=(c == 0), stop=(c == DC - 1))
                last.then_inc(proj_made, 1)

            def dots(n):
                t, b, pair = n // PAIRS % QT, n // PAIRS // QT, n % PAIRS
                keys = dot_keys(t)
                if n >= 2:
                    pe.wait_ge(dots_copied[n % 2], (n - 2) // 2 + 1)
                for half in range(2):
                    tokens = (b * QT + t) * P
                    last = mm(bank[n % 2][:, half, 0:keys], q_padded[:, 2 * pair + half, tokens:tokens + P],
                              kT[:, pair, b, 0:keys], start=True, stop=True)
                last.then_inc(dots_made, 1)

            def mix(n):
                b, s = n // SA_STEPS, n % SA_STEPS
                keys = step_keys(s)
                pe.wait_ge(regrouped, 16 * HEADS * (b * QT + s // (SA_STEPS // QT) + 1))
                if n >= 2:
                    pe.wait_ge(exp_done, GPS * (n - 1))
                for g in range(GPS):
                    group = s * GPS + g
                    last = mm(bank[2 + n % 2][:, g, 0:keys], kron[:, 0, :, :].rearrange("p k r -> p (k r)"),
                              grouped[:, group // (P // ROWS), group % (P // ROWS), 0:keys], start=True, stop=True)
                last.then_inc(mix_made, 1)

            def post(n):
                b, s = n // SA_STEPS, n % SA_STEPS
                pe.wait_ge(kron_done, GPS * (n + 1))
                pe.wait_ge(tail_zero, b * (SA_STEPS - 1) + min(s + 1, SA_STEPS - 1))
                if n >= 2:
                    pe.wait_ge(mixed_by_act, n - 1)
                    pe.wait_ge(mixed_by_dve, n - 1)
                for g in range(GPS):
                    e, k = expd[:, n % 2, g, :], kron_scaled[:, n % 2, g, :]
                    mm(bank[n % 2][0:MEM, 1, (GPS + g) * P:(GPS + g + 1) * P], e[:, 0:MEM], k, start=True, stop=True)
                    last = mm(bank[n % 2][:, 0, g * P:(g + 1) * P], e[:, MEM:MEM + P], k, start=True, stop=True)
                    if s >= SA_STEPS // QT:
                        last = mm(bank[n % 2][:, 1, g * P:(g + 1) * P], e[:, MEM + P:KEYS], k, start=True, stop=True)
                last.then_inc(post_made, 1)

            def product_with_v(n):
                b, pair = n // PAIRS, n % PAIRS
                if n % PAIRS >= 2 :
                    pe.wait_ge(out_copied, n - 1)
                for half in range(2):
                    k = 2 * pair + half
                    out = bank[2 + n % 2][half * DH:(half + 1) * DH, 0, :]
                    mm(out[:, 0:SEQ], memv_sb[:, k, :], mixed_mem[:, k, :], start=True, stop=False)
                    mm(out[:, 0:SEQ], v_sb[:, b * QT, k * DH:(k + 1) * DH], mixed[0][:, k, :], start=False, stop=False)
                    last = mm(out[:, P:SEQ], v_sb[:, b * QT + 1, k * DH:(k + 1) * DH], mixed[1][:, k, P:SEQ],
                              start=False, stop=True)
                last.then_inc(out_made, 1)

            def output(n):
                for pair in range(PAIRS):
                    last = mm(bank[n % 2][:, 0, 0:D], outT[:, pair, n % QT * P:(n % QT + 1) * P], wo_sb[:, pair, :],
                              start=(pair == 0), stop=(pair == PAIRS - 1))
                last.then_inc(y_made, 1)

            for eng in range(2):
                pe.wait_ge(proj_copied[eng], NPROJ // 2)
            for b in range(BATCH):
                if b > 0:
                    pe.wait_ge(y_added, b * QT)
                for n in range(b * QT * PAIRS, (b + 1) * QT * PAIRS):
                    dots(n)
                first = b * SA_STEPS
                for eng in range(2):
                    pe.wait_ge(dots_copied[eng], (b + 1) * QT * PAIRS // 2)
                mix(first)
                for n in range(first + 1, first + SA_STEPS):
                    mix(n)
                    post(n - 1)
                post(first + SA_STEPS - 1)
                pe.wait_ge(mixed_by_act, first + SA_STEPS)
                pe.wait_ge(mixed_by_dve, first + SA_STEPS)
                for n in range(b * PAIRS, (b + 1) * PAIRS):
                    product_with_v(n)
                pe.wait_ge(out_copied, (b + 1) * PAIRS)
                for n in range(b * QT, (b + 1) * QT):
                    output(n)


FF = 768
FC = FF // P
BLOCK = 32
W_MAX = 2.0 ** 3 - 1.0
A_MAX = 2.0 ** 15 - 1.0
U_STEPS = 65536.0
ROUND = 1.5 * 2.0 ** 23
TINY = 1e-12


def gated_ffn(nc, w_gate, w_up, w_down, x_res, out, ident):
    with ExitStack() as stack:
        r = Resources(nc, stack)
        NB = FF * D // P // BLOCK
        UP, GATE, DOWN = range(3)
        w_sb = [r.sbuf(f"w_sb{n}", [P, NB, BLOCK]) for n in range(3)]
        w_top = r.sbuf("w_top", [P, 3, NB])
        w_bottom = r.sbuf("w_bottom", [P, 3, NB])
        w_scale = r.sbuf("w_scale", [P, 3, NB])
        w_inverse = r.sbuf("w_inverse", [P, 3, NB])
        wT = [r.sbuf(f"wT{n}", [P, FF * D // P]) for n in range(3)]
        upT, gateT = (wT[n][:, :].rearrange("p (c f) -> p c f", c=DC) for n in (UP, GATE))
        downT = wT[DOWN][:, :].rearrange("p (c d) -> p c d", c=FC)
        xn = r.sbuf("xn3", [P, TOK_TILES, D])
        xqT = r.sbuf("xqT", [P, DC, BATCH * SEQ])
        stats = r.sbuf("stats3", [P, TOK_TILES, 6])
        moments = r.sbuf("moments3", [P, TOK_TILES, 2])
        power = r.sbuf("power3", [P, TOK_TILES])
        up = r.sbuf("up", [P, FC, BATCH * SEQ])
        gate = r.sbuf("gate", [P, FC, BATCH * SEQ])
        sig = r.sbuf("sig", [P, FC, BATCH * SEQ])
        limits = r.sbuf("limits", [P, 5, 8])
        bank = [r.psum(f"ffn_bank{n}", [P, 512]) for n in range(8)]

        w_in = r.sem("w_in3")
        norm_chain = r.sem("norm_chain3")
        inverse_std = r.sem("inverse_std3")
        w_chain = r.sem("w_chain")
        q_chain = r.sem("q_chain")
        peak = r.sem("peak")
        xq_ready = r.sem("xq_ready")
        xqT_made = r.sem("xqT_made")
        xqT_copied = r.sem("xqT_copied")
        wT_made = r.sem("wT_made")
        wT_copied = r.sem("wT_copied")
        hidden_made = r.sem("hidden_made")
        hidden_copied = r.sem("hidden_copied")
        sig_ready = r.sem("sig_ready")
        product_ready = r.sem("product_ready")
        y_made = r.sem("y_made3")
        y_added = r.sem("y_added3")
        stored = r.sem("stored")
        Q_OPS = 8
        WT_BANKS = FF * D // P // 512
        block = stack.enter_context(nc.Block())

        @block.sync
        def _(sp):
            for n, w in ((UP, w_up), (GATE, w_gate), (DOWN, w_down)):
                t = w.shape[0] // P
                sp.dma_start(w_sb[n][:, :, :].rearrange("p b k -> p (b k)").rearrange("p (t i) -> p t i", t=t),
                             w.rearrange("(t p) i -> p t i", p=P)).then_inc(w_in, 16)
            for t in range(TOK_TILES):
                sp.wait_ge(y_added, t + 1)
                sp.dma_start(out.rearrange("b (t p) d -> p (b t) d", p=P)[:, t, :], x_res[:, t, :]).then_inc(stored, 16)
            sp.wait_ge(stored, 16 * TOK_TILES)

        @block.gpsimd
        def _(pool):
            invert_std(pool, moments, power, norm_chain, inverse_std)
            for n in range(5):
                pool.wait_ge(q_chain, Q_OPS * n + 3)
                pool.partition_all_reduce(limits[:, n, 3:4], limits[:, n, 2:3], P, bass.bass_isa.ReduceOp.max
                                          ).then_inc(peak, 1)

        @block.scalar
        def _(act):
            for n in range(3 * WT_BANKS):
                m, c = n // WT_BANKS, n % WT_BANKS
                act.wait_ge(wT_made, n + 1)
                act.activation(wT[m][:, c * 512:(c + 1) * 512], bank[n % 4][:, :], ACT.Copy).then_inc(wT_copied, 1)
            for n in range(2 * FC):
                act.wait_ge(hidden_made, n + 1)
                act.activation((up if n < FC else gate)[:, n % FC, :], bank[n % 8][:, :], ACT.Copy
                               ).then_inc(hidden_copied, 1)
            act.wait_ge(q_chain, 3 * Q_OPS)
            act.activation(sig[:, :, :], gate[:, :, :], ACT.Sigmoid).then_inc(sig_ready, 1)

        @block.vector
        def _(dve):
            def quantise(n, t):
                a = limits[:, n, :]
                base = Q_OPS * n
                dve.tensor_reduce(a[:, 0:1], t, X, ALU.max).then_inc(q_chain, 1)
                dve.tensor_reduce(a[:, 1:2], t, X, ALU.min).then_inc(q_chain, 1)
                dve.wait_ge(q_chain, base + 2)
                dve.scalar_tensor_tensor(a[:, 2:3], a[:, 1:2], -1.0, a[:, 0:1], ALU.mult, ALU.max).then_inc(q_chain, 1)
                dve.wait_ge(peak, n + 1)
                dve.tensor_scalar(a[:, 4:5], a[:, 3:4], 1.0 / A_MAX, TINY, ALU.mult, ALU.max).then_inc(q_chain, 1)
                dve.wait_ge(q_chain, base + 4)
                dve.reciprocal(a[:, 5:6], a[:, 4:5]).then_inc(q_chain, 1)
                dve.wait_ge(q_chain, base + 5)
                dve.tensor_scalar(t, t, a[:, 5:6], ROUND, ALU.mult, ALU.add).then_inc(q_chain, 1)
                dve.wait_ge(q_chain, base + 6)
                dve.tensor_scalar(t, t, ROUND, A_MAX, ALU.subtract, ALU.min).then_inc(q_chain, 1)
                dve.wait_ge(q_chain, base + 7)
                dve.tensor_scalar(t, t, -A_MAX - 1.0, a[:, 4:5], ALU.max, ALU.mult).then_inc(q_chain, 1)
                dve.wait_ge(q_chain, base + Q_OPS)

            normalise_rows(dve, x_res, xn, stats, moments, norm_chain, inverse_std)
            dve.wait_ge(norm_chain, NORMALISED)
            xflat = xn[:, :, :].rearrange("p t d -> p (t d)")
            quantise(0, xflat)
            dve.wait_ge(w_in, 48)
            for n in range(3):
                w = w_sb[n]
                base = 9 * n
                blocks = [P, NB, BLOCK]
                dve.tensor_reduce(w_top[:, n, :], w[:, :, :], X, ALU.max).then_inc(w_chain, 1)
                dve.tensor_reduce(w_bottom[:, n, :], w[:, :, :], X, ALU.min).then_inc(w_chain, 1)
                dve.wait_ge(w_chain, base + 2)
                dve.scalar_tensor_tensor(w_top[:, n, :], w_bottom[:, n, :], -1.0, w_top[:, n, :], ALU.mult, ALU.max
                                         ).then_inc(w_chain, 1)
                dve.wait_ge(w_chain, base + 3)
                dve.tensor_scalar(w_scale[:, n, :], w_top[:, n, :], 1.0 / W_MAX, TINY, ALU.mult, ALU.max
                                  ).then_inc(w_chain, 1)
                dve.wait_ge(w_chain, base + 4)
                dve.reciprocal(w_inverse[:, n, :], w_scale[:, n, :]).then_inc(w_chain, 1)
                dve.wait_ge(w_chain, base + 5)
                dve.tensor_tensor(w[:, :, :], w[:, :, :], w_inverse[:, n, :].unsqueeze(2).to_broadcast(blocks),
                                  ALU.mult).then_inc(w_chain, 1)
                dve.wait_ge(w_chain, base + 6)
                dve.tensor_scalar(w[:, :, :], w[:, :, :], ROUND, ROUND, ALU.add, ALU.subtract).then_inc(w_chain, 1)
                dve.wait_ge(w_chain, base + 7)
                dve.tensor_scalar(w[:, :, :], w[:, :, :], W_MAX, -W_MAX - 1.0, ALU.min, ALU.max).then_inc(w_chain, 1)
                dve.wait_ge(w_chain, base + 8)
                dve.tensor_tensor(w[:, :, :], w[:, :, :], w_scale[:, n, :].unsqueeze(2).to_broadcast(blocks),
                                  ALU.mult).then_inc(w_chain, 1)
            for c in range(DC):
                dve.wait_ge(xqT_made, c + 1)
                dve.tensor_copy(xqT[:, c, :], bank[6 + c][:, :]).then_inc(xqT_copied, 1)

            def flat(t):
                return t[:, :, :].rearrange("p c n -> p (c n)")
            dve.wait_ge(hidden_copied, FC)
            quantise(1, flat(up))
            dve.wait_ge(hidden_copied, 2 * FC)
            quantise(2, flat(gate))
            dve.wait_ge(sig_ready, 1)
            s = flat(sig)
            dve.tensor_scalar(s, s, U_STEPS, ROUND, ALU.mult, ALU.add).then_inc(product_ready, 1)
            dve.wait_ge(product_ready, 1)
            dve.tensor_scalar(s, s, ROUND, U_STEPS - 1.0, ALU.subtract, ALU.min).then_inc(product_ready, 1)
            dve.wait_ge(product_ready, 2)
            dve.tensor_scalar(s, s, 0.0, 1.0 / U_STEPS, ALU.max, ALU.mult).then_inc(product_ready, 1)
            dve.wait_ge(product_ready, 3)
            dve.tensor_tensor(s, s, flat(gate), ALU.mult).then_inc(product_ready, 1)
            dve.wait_ge(product_ready, 4)
            quantise(3, s)
            dve.tensor_tensor(s, s, flat(up), ALU.mult).then_inc(product_ready, 1)
            dve.wait_ge(product_ready, 5)
            quantise(4, s)
            for t in range(TOK_TILES):
                dve.wait_ge(y_made, t + 1)
                dve.tensor_tensor(x_res[:, t, :], x_res[:, t, :], bank[t][:, 0:D], ALU.add).then_inc(y_added, 1)

        @block.tensor
        def _(pe):
            mm = pe.matmul
            pe.wait_ge(q_chain, Q_OPS)
            for c in range(DC):
                for t in range(TOK_TILES):
                    last = pe.transpose(bank[6 + c][:, t * P:(t + 1) * P], xn[:, t, c * P:(c + 1) * P], ident[:, :])
                last.then_inc(xqT_made, 1)
            for n in range(3):
                pe.wait_ge(w_chain, 9 * (n + 1))
                w = w_sb[n][:, :, :].rearrange("p b k -> p (b k)")
                tiles = 2 if n == DOWN else FC
                width = FF * D // P // tiles
                for k in range(FF * D // P // P):
                    at = n * WT_BANKS + k // 4
                    if k % 4 == 0 and at >= 4:
                        pe.wait_ge(wT_copied, at - 3)
                    c, t = k // tiles, k % tiles
                    last = pe.transpose(bank[at % 4][:, k % 4 * P:(k % 4 + 1) * P],
                                        w[:, t * width + c * P:t * width + (c + 1) * P], ident[:, :])
                    if k % 4 == 3:
                        last.then_inc(wT_made, 1)
            pe.wait_ge(wT_copied, 3 * WT_BANKS)
            pe.wait_ge(xqT_copied, DC)
            for n in range(2 * FC):
                if n >= 8:
                    pe.wait_ge(hidden_copied, n - 7)
                w = upT if n < FC else gateT
                for c in range(DC):
                    last = mm(bank[n % 8][:, :], w[:, c, n % FC * P:(n % FC + 1) * P], xqT[:, c, :],
                              start=(c == 0), stop=(c == DC - 1))
                last.then_inc(hidden_made, 1)
            pe.wait_ge(hidden_copied, 2 * FC)
            pe.wait_ge(q_chain, 5 * Q_OPS)
            for t in range(TOK_TILES):
                for c in range(FC):
                    last = mm(bank[t][:, 0:D], sig[:, c, t * P:(t + 1) * P], downT[:, c, :],
                              start=(c == 0), stop=(c == FC - 1))
                last.then_inc(y_made, 1)


def load_identity(nc, ident):
    with ExitStack() as stack:
        r = Resources(nc, stack)
        cleared = r.sem("cleared")
        block = stack.enter_context(nc.Block())

        @block.gpsimd
        def _(pool):
            pool.memset(ident[:, :], 0.0).then_inc(cleared, 1)
            pool.wait_ge(cleared, 1)
            pool.affine_select(out=ident[:, :], in_=ident[:, :], compare_op=ALU.not_equal, fill=1.0, base=0,
                               pattern=[[-1, P]], channel_multiplier=1).then_inc(cleared, 1)
            pool.wait_ge(cleared, 2)


def perceiver_layer(nc, x, ctx_1024, x_w_q, x_w_k, x_w_v, x_w_o, a_w_q, a_w_kv, a_w_o, pre_proj, post_proj,
                    mem_k, mem_v, w_gate, w_up, w_down, out):
    with ExitStack() as stack:
        r = Resources(nc, stack)
        ident = r.sbuf("ident", [P, P])
        x_res = r.sbuf("x_res", [P, TOK_TILES, D])
        load_identity(nc, ident)
        cross_attention(nc, x, ctx_1024, x_w_q, x_w_k, x_w_v, x_w_o, x_res, ident)
        self_attention(nc, a_w_q, a_w_kv, a_w_o, pre_proj, post_proj, mem_k, mem_v, x_res, ident)
        gated_ffn(nc, w_gate, w_up, w_down, x_res, out, ident)


_INS = ['x', 'ctx_1024', 'L0_xattn_w_q', 'L0_xattn_w_k', 'L0_xattn_w_v', 'L0_xattn_w_o', 'L0_attn_Wq',
        'L0_attn_Wkv', 'L0_attn_Wo', 'L0_attn_pre_proj', 'L0_attn_post_proj', 'L0_attn_mem_k', 'L0_attn_mem_v',
        'L0_ffn_w_gate', 'L0_ffn_w_up', 'L0_ffn_w_down']
_OUTS = [((2, 256, 256), 'float32')]


def kernel(**inputs):
    import numpy as _np
    import concourse.bacc as _bacc
    from concourse import mybir as _mybir
    from concourse.bass_utils import run_bass_kernel_spmd as _run

    nc = _bacc.Bacc("TRN2", target_bir_lowering=False, num_devices=1)
    arrays, args = {}, []
    for name in _INS:
        a = _np.ascontiguousarray(inputs[name])
        arrays[f"in_{name}_dram"] = a
        args.append(nc.dram_tensor(f"in_{name}_dram", a.shape, _mybir.dt.from_np(a.dtype), kind="ExternalInput").ap())
    for i, (shape, dtype) in enumerate(_OUTS):
        dt = _mybir.dt.from_np(_np.dtype(dtype))
        args.append(nc.dram_tensor(f"out_{i}_dram", shape, dt, kind="ExternalOutput").ap())
    perceiver_layer(nc, *args)
    r = _run(nc, [arrays], core_ids=[0])
    got = tuple(r.results[0][f"out_{i}_dram"] for i in range(len(_OUTS)))
    return got[0]
```

```python
from contextlib import ExitStack

import concourse.bass as bass
from concourse import mybir

F32 = mybir.dt.float32
F32R = mybir.dt.float32r
ALU = mybir.AluOpType
ACT = mybir.ActivationFunctionType
X = mybir.AxisListType.X

P = 128
BATCH, SEQ, D = 2, 256, 256
CTX = 4096
HEADS, DH = 16, 64
INNER = HEADS * DH
TOK_TILES = BATCH * SEQ // P
QT = SEQ // P
DC = D // P
PAIRS = HEADS // 2
SCALE = DH ** -0.5
EPS = 1e-5


class Resources:

    def __init__(self, nc, stack):
        self.nc, self.stack = nc, stack

    def sbuf(self, name, shape, dtype=F32):
        return self.stack.enter_context(self.nc.sbuf_tensor(name, shape, dtype))

    def psum(self, name, shape, dtype=F32):
        return self.stack.enter_context(self.nc.psum_tensor(name, shape, dtype))

    def sem(self, name):
        return self.stack.enter_context(self.nc.semaphore(name))


def wait_past(eng, sem, value):
    if not isinstance(value, int) or value > 0:
        eng.wait_ge(sem, value)


NORMALISED = 3 * TOK_TILES


def normalise_rows(dve, x, out, stats, moments, chain, inverse_std):
    n = 0
    for t in range(TOK_TILES):
        dve.bn_stats(stats[:, t, :], x[:, t, :]).then_inc(chain, 1)
    n += TOK_TILES
    dve.wait_ge(chain, n)
    for t in range(TOK_TILES):
        dve.bn_aggr(moments[:, t, :], stats[:, t, :]).then_inc(chain, 1)
    n += TOK_TILES
    dve.wait_ge(inverse_std, 3)
    for t in range(TOK_TILES):
        dve.tensor_scalar(out[:, t, :], x[:, t, :], moments[:, t, 0:1], moments[:, t, 1:2],
                          ALU.subtract, ALU.mult).then_inc(chain, 1)
    assert n + TOK_TILES == NORMALISED


def invert_std(pool, moments, power, chain, inverse_std):
    pool.memset(power[:, :], -0.5).then_inc(inverse_std, 1)
    pool.wait_ge(chain, 2 * TOK_TILES)
    pool.tensor_scalar(moments[:, :, 1], moments[:, :, 1], EPS, None, ALU.add).then_inc(inverse_std, 1)
    pool.wait_ge(inverse_std, 2)
    pool.tensor_tensor(moments[:, :, 1], moments[:, :, 1], power[:, :], ALU.pow).then_inc(inverse_std, 1)


def cross_attention(nc, x, ctx_in, w_q, w_k, w_v, w_o, x_res, ident):
    CHUNK = 512
    STEPS = CTX // CHUNK
    KT = CHUNK // P
    LOAD = 4
    LOADS = CTX // P // LOAD
    GROUP = 4
    GROUPS = CTX // P // GROUP
    A, B = 0, 1

    with ExitStack() as stack:
        r = Resources(nc, stack)
        ctx_rows = r.sbuf("ctx_rows", [P, 2, LOAD, D])
        ctxT_hi = r.sbuf("ctxT_hi", [P, DC, CTX], F32R)
        ctxT_lo = r.sbuf("ctxT_lo", [P, DC, CTX], F32R)
        k_split = r.sbuf("k_split", [P, 2, CTX], F32R)
        k_ones = r.sbuf("k_ones", [P, 2, CTX], F32R)
        v_rows = r.sbuf("v_rows", [P, CTX // P, 2 * DH])
        q_twice = r.sbuf("q_twice", [P, 2, SEQ], F32R)
        q_low_max = r.sbuf("q_low_max", [P, 2, SEQ], F32R)
        probs = r.sbuf("probs", [P, 2, 2, KT * SEQ])
        vT_sb = [probs[:, n, A, 0:CHUNK] for n in range(2)]
        prob_sum = r.sbuf("prob_sum", [P, 2, KT * SEQ])
        xn = prob_sum[:, 0, :].rearrange("p (t d) -> p t d", t=TOK_TILES)
        xnT = r.sbuf("xnT", [P, DC, BATCH * SEQ])
        stats = r.sbuf("stats", [P, TOK_TILES, 6])
        moments = r.sbuf("moments", [P, TOK_TILES, 2])
        power = r.sbuf("power", [P, TOK_TILES])
        w_raw = r.sbuf("w_raw", [P, 3, DC, 2 * DH])
        w_hi = r.sbuf("w_hi", [P, 2, DC, 2 * DH], F32R)
        w_lo = r.sbuf("w_lo", [P, 2, DC, 2 * DH], F32R)
        wq_pair = r.sbuf("wq_pair", [P, DC, 2 * DH])
        wo_pair = r.sbuf("wo_pair", [P, D])
        step_max = r.sbuf("step_max", [P, QT, 2, STEPS])
        row_max = r.sbuf("row_max", [P, QT, 2])
        neg_max = r.sbuf("neg_max", [P, QT, P])
        recip = r.sbuf("recip", [P, SEQ])
        outT = r.sbuf("outT", [P, SEQ])
        ones = r.sbuf("ones", [P, DH])

        scores = [r.psum("scores_a", [P, 2, CHUNK]), r.psum("scores_b", [P, 2, CHUNK])]
        k_ps = [r.psum("k_ps0", [P, CHUNK]), r.psum("k_ps1", [P, CHUNK])]
        v_ps = r.psum("v_ps", [P, CHUNK])
        out_ps = r.psum("out_ps", [P, CHUNK])
        flat_scores = [s[:, :, :].rearrange("p a b -> p (a b)") for s in scores]

        x_loaded = r.sem("x_loaded")
        ctx_loaded = [r.sem("ctx_loaded0"), r.sem("ctx_loaded1")]
        w_loaded = r.sem("w_loaded")
        wo_loaded = r.sem("wo_loaded")
        consts_ready = r.sem("consts_ready")
        norm_chain = r.sem("norm_chain")
        inverse_std = r.sem("inverse_std")
        xT_made = r.sem("xT_made")
        xT_copied = r.sem("xT_copied")
        ctxT_made = r.sem("ctxT_made")
        ctx_high = r.sem("ctx_high")
        ctx_low = r.sem("ctx_low")
        w_high = r.sem("w_high")
        w_low = r.sem("w_low")
        wq_copied = r.sem("wq_copied")
        q_made = r.sem("q_made")
        q_high = r.sem("q_high")
        q_low = r.sem("q_low")
        k_made = r.sem("k_made")
        k_high = r.sem("k_high")
        k_low = r.sem("k_low")
        k_copied = r.sem("k_copied")
        vT_made = r.sem("vT_made")
        vT_copied = r.sem("vT_copied")
        v_made = r.sem("v_made")
        v_copied = r.sem("v_copied")
        pre_made = r.sem("pre_made")
        max_done = r.sem("max_done")
        max_chain = r.sem("max_chain")
        maxT_made = r.sem("maxT_made")
        max_ready = r.sem("max_ready")
        scores_made = r.sem("scores_made")
        exp_done = r.sem("exp_done")
        sum_done = r.sem("sum_done")
        fold_done = r.sem("fold_done")
        pv_done = r.sem("pv_done")
        den_made = r.sem("den_made")
        recip_done = r.sem("recip_done")
        outT_ready = r.sem("outT_ready")
        y_made = r.sem("y_made")
        y_added = r.sem("y_added")

        def vT_bank(j):
            return k_ps[1] if j == STEPS - 2 else out_ps

        def v_bank(j):
            return k_ps[1] if j == STEPS - 1 else v_ps

        def pairs_of_batch(eng, b, body):
            body(b * PAIRS, b, 0)
            with eng.Fori(1, PAIRS) as i:
                body(b * PAIRS + i, b, i)

        def act_context(act, b):
            for g in range(GROUPS):
                n = b * GROUPS + g
                act.wait_ge(ctxT_made, n + 1)
                act.activation(ctxT_hi[:, :, g * CHUNK:(g + 1) * CHUNK], scores[n % 2][:, :, :], ACT.Copy
                               ).then_inc(ctx_high, 1)

        def is_first(it):
            return isinstance(it, int) and it == 0

        def last_batch(b, i):
            return b - 1 if isinstance(i, int) else b

        x_tiles = x.rearrange("b (t p) d -> p (b t) d", p=P)
        ctx_tiles = ctx_in.rearrange("b (p t) d -> b p t d", p=P)
        block = stack.enter_context(nc.Block())

        @block.sync
        def _(sp):
            sp.dma_start(x_res[:, :, :], x_tiles).then_inc(x_loaded, 16)
            for b in range(BATCH):
                for n in range(LOADS):
                    at = b * LOADS + n
                    if at >= 2:
                        sp.wait_ge(ctxT_made, (at - 1) * LOAD // GROUP)
                    sp.dma_start(ctx_rows[:, at % 2, :, :],
                                 ctx_tiles[b, :, n * LOAD:(n + 1) * LOAD, :]).then_inc(ctx_loaded[at % 2], 16)

                def body(it, b, i):
                    wait_past(sp, w_low, it)
                    wait_past(sp, wq_copied, it)
                    cols = bass.ds(i * 2 * DH, 2 * DH)
                    for n, w in enumerate((w_q, w_k, w_v)):
                        sp.dma_start(w_raw[:, n, :, :], w[:, cols].rearrange("(c p) n -> p c n", p=P)
                                     ).then_inc(w_loaded, 16)
                    wait_past(sp, y_made, it)
                    sp.dma_start(wo_pair[:, :], w_o[bass.ds(i * P, P), :]).then_inc(wo_loaded, 16)
                pairs_of_batch(sp, b, body)

        @block.gpsimd
        def _(pool):
            pool.memset(neg_max[:, :, :], 0.0).then_inc(consts_ready, 1)
            pool.memset(ones[:, :], 1.0).then_inc(consts_ready, 1)
            invert_std(pool, moments, power, norm_chain, inverse_std)
            for s in (0, 1):
                pool.memset(k_ones[:, s, :].bitcast(F32), 0.0).then_inc(consts_ready, 1)
            pool.wait_ge(consts_ready, 4)
            pool.memset(k_ones[DH:DH + 1, A, :].bitcast(F32), 1.0).then_inc(consts_ready, 1)
            pool.memset(k_ones[0:1, B, :].bitcast(F32), 1.0).then_inc(consts_ready, 1)

            def body(it, b, i):
                pool.wait_ge(w_high, it + 1)
                pool.tensor_tensor(w_lo[:, :, :, :], w_raw[:, 1:3, :, :], w_hi[:, :, :, :].bitcast(F32),
                                   ALU.subtract).then_inc(w_low, 1)
            for b in range(BATCH):
                pairs_of_batch(pool, b, body)

        @block.scalar
        def _(act):
            def copy_vT(it, j):
                act.wait_ge(vT_made, STEPS * it + j + 1)
                act.activation(vT_sb[j % 2], vT_bank(j)[:, :], ACT.Copy).then_inc(vT_copied, 1)

            def copy_v(it, j):
                act.wait_ge(v_made, STEPS * it + j + 1)
                act.activation(v_rows[:, j * KT:(j + 1) * KT, :], v_bank(j)[:, :].rearrange("p (t d) -> p t d", t=KT),
                               ACT.Copy).then_inc(v_copied, 1)

            def body(it, b, i):
                act.wait_ge(w_loaded, 48 * it + 48)
                wait_past(act, v_made, STEPS * it)
                act.activation(w_hi[:, :, :, :], w_raw[:, 1:3, :, :], ACT.Copy).then_inc(w_high, 1)
                act.activation(wq_pair[:, :, :], w_raw[:, 0, :, :], ACT.Copy).then_inc(wq_copied, 1)
                act.wait_ge(q_made, it + 1)
                for h in (A, B):
                    for half in (0, DH):
                        act.activation(q_twice[half:half + DH, h, :], v_ps[h * DH:(h + 1) * DH, 0:SEQ],
                                       ACT.Copy).then_inc(q_high, 1)
                for j in range(STEPS + 2):
                    if j < STEPS:
                        keys = slice(j * CHUNK, (j + 1) * CHUNK)
                        act.wait_ge(k_made, STEPS * it + j + 1)
                        ps = k_ps[j % 2]
                        act.activation(k_split[0:DH, A, keys], ps[0:DH, :], ACT.Copy).then_inc(k_high, 1)
                        act.activation(k_split[DH:P, B, keys], ps[DH:P, :], ACT.Copy).then_inc(k_high, 1)
                    if 0 < j <= STEPS:
                        keys = slice((j - 1) * CHUNK, j * CHUNK)
                        act.wait_ge(k_high, 2 * (STEPS * it + j))
                        act.activation(k_ones[0:DH, A, keys], k_split[0:DH, A, keys].bitcast(F32), ACT.Copy
                                       ).then_inc(k_copied, 1)
                        act.activation(k_ones[DH:P, B, keys], k_split[DH:P, B, keys].bitcast(F32), ACT.Copy
                                       ).then_inc(k_copied, 1)
                    if j > 2:
                        copy_vT(it, j - 3)
                    if j > 3:
                        copy_v(it, j - 4)
                copy_vT(it, STEPS - 1)
                act.wait_ge(maxT_made, it + 1)
                act.activation(q_low_max[DH:P, A, :], k_ps[0][DH:P, 0:SEQ], ACT.Copy).then_inc(max_ready, 1)
                copy_v(it, STEPS - 2)
                copy_v(it, STEPS - 1)
                for j in range(STEPS):
                    for h in (A, B):
                        n = 2 * (STEPS * it + j) + h
                        act.wait_ge(scores_made, n + 1)
                        if j >= 2 or not (b == 0 and isinstance(i, int)):
                            act.wait_ge(sum_done, n - 3)
                            act.wait_ge(pv_done, STEPS * it + j - 1)
                        act.activation(probs[:, j % 2, h, :], flat_scores[h], ACT.Exp, scale=SCALE
                                       ).then_inc(exp_done, 1)
            for b in range(BATCH):
                act_context(act, b)
                if b == 0:
                    act.wait_ge(consts_ready, 6)
                pairs_of_batch(act, b, body)

        @block.vector
        def _(dve):
            dve.wait_ge(x_loaded, 16)
            normalise_rows(dve, x_res, xn, stats, moments, norm_chain, inverse_std)

            def divide(before):
                dve.wait_ge(den_made, before + 1)
                dve.reciprocal(recip[:, :], out_ps[:, 0:SEQ]).then_inc(recip_done, 1)
                dve.wait_ge(recip_done, before + 1)
                wait_past(dve, y_made, before)
                dve.tensor_tensor(outT[:, :], out_ps[:, SEQ:2 * SEQ], recip[:, :], ALU.mult).then_inc(outT_ready, 1)

            def add_output(before, b):
                dve.wait_ge(y_made, before + 1)
                dst = x_res[:, b * QT:(b + 1) * QT, :]
                dve.tensor_tensor(dst, dst, out_ps[:, :].rearrange("p (t d) -> p t d", t=QT), ALU.add
                                  ).then_inc(y_added, 1)

            def body(it, b, i):
                def low_queries():
                    dve.wait_ge(q_high, 4 * it + 4)
                    dve.tensor_tensor(q_low_max[0:DH, A, :], v_ps[0:DH, 0:SEQ], q_twice[0:DH, A, :].bitcast(F32),
                                      ALU.subtract).then_inc(q_low, 1)
                    dve.tensor_tensor(q_low_max[DH:P, B, :], v_ps[DH:P, 0:SEQ], q_twice[DH:P, B, :].bitcast(F32),
                                      ALU.subtract).then_inc(q_low, 1)
                for j in range(STEPS + 1):
                    if j < STEPS:
                        keys = slice(j * CHUNK, (j + 1) * CHUNK)
                        n = STEPS * it + j
                        ps = k_ps[j % 2]
                        dve.wait_ge(k_high, 2 * n + 1)
                        dve.tensor_tensor(k_split[DH:P, A, keys], ps[0:DH, :], k_split[0:DH, A, keys].bitcast(F32),
                                          ALU.subtract).then_inc(k_low, 1)
                        dve.wait_ge(k_high, 2 * n + 2)
                        dve.tensor_tensor(k_split[0:DH, B, keys], ps[DH:P, :], k_split[DH:P, B, keys].bitcast(F32),
                                          ALU.subtract).then_inc(k_low, 1)
                        if j == 0:
                            low_queries()
                    if not is_first(it):
                        if j == 0:
                            divide(it - 1)
                        if j == 1:
                            add_output(it - 1, last_batch(b, i))
                    if j > 0:
                        for h in (A, B):
                            dve.wait_ge(pre_made, 2 * (STEPS * it + j - 1) + h + 1)
                            dve.tensor_reduce(step_max[:, :, 1 - h, j - 1], scores[h][:, :, :], X, ALU.max
                                              ).then_inc(max_done, 1)
                dve.wait_ge(max_done, 2 * STEPS * (it + 1))
                dve.tensor_reduce(row_max[:, :, :], step_max[:, :, :, :], X, ALU.max).then_inc(max_chain, 1)
                dve.wait_ge(max_chain, 2 * it + 1)
                dve.tensor_scalar(neg_max[:, :, 0:P:DH], row_max[:, :, :], -1.0, None, ALU.mult
                                  ).then_inc(max_chain, 1)
                dve.wait_ge(maxT_made, it + 1)
                dve.tensor_copy(q_low_max[0:DH, B, :], k_ps[0][0:DH, 0:SEQ]).then_inc(max_ready, 1)
                for j in range(STEPS):
                    for h in (A, B):
                        n = 2 * (STEPS * it + j) + h
                        dve.wait_ge(exp_done, n + 1)
                        if j == 0:
                            dve.tensor_copy(prob_sum[:, h, :], probs[:, 0, h, :]).then_inc(sum_done, 1)
                        else:
                            dve.wait_ge(sum_done, n - 1)
                            dve.tensor_tensor(prob_sum[:, h, :], prob_sum[:, h, :], probs[:, j % 2, h, :], ALU.add
                                              ).then_inc(sum_done, 1)
                dve.wait_ge(sum_done, 2 * STEPS * (it + 1))
                half = KT * SEQ // 2
                dve.tensor_tensor(prob_sum[:, :, 0:half], prob_sum[:, :, 0:half], prob_sum[:, :, half:2 * half],
                                  ALU.add).then_inc(fold_done, 1)
                dve.wait_ge(fold_done, 2 * it + 1)
                dve.tensor_tensor(prob_sum[:, :, 0:SEQ], prob_sum[:, :, 0:SEQ], prob_sum[:, :, SEQ:2 * SEQ],
                                  ALU.add).then_inc(fold_done, 1)
            for b in range(BATCH):
                for g in range(GROUPS):
                    n = b * GROUPS + g
                    dve.wait_ge(ctx_high, n + 1)
                    cols = slice(g * CHUNK, (g + 1) * CHUNK)
                    dve.tensor_tensor(ctxT_lo[:, :, cols], scores[n % 2][:, :, :], ctxT_hi[:, :, cols].bitcast(F32),
                                      ALU.subtract).then_inc(ctx_low, 1)
                    if n == 3:
                        for c in range(DC):
                            dve.wait_ge(xT_made, c + 1)
                            dve.tensor_copy(xnT[:, c, :], k_ps[c][:, :]).then_inc(xT_copied, 1)
                pairs_of_batch(dve, b, body)
            divide(BATCH * PAIRS - 1)
            add_output(BATCH * PAIRS - 1, BATCH - 1)

        @block.tensor
        def _(pe):
            mm = pe.matmul

            def transpose_context(b, g):
                n = b * GROUPS + g
                if g % (LOAD // GROUP) == 0:
                    load = n * GROUP // LOAD
                    pe.wait_ge(ctx_loaded[load % 2], 16 * (load // 2 + 1))
                if n >= 2:
                    pe.wait_ge(ctx_low, n - 1)
                for t in range(GROUP):
                    tile = g * GROUP + t
                    slot = (b * LOADS + tile // LOAD) % 2
                    for c in range(DC):
                        last = pe.transpose(scores[n % 2][:, c, t * P:(t + 1) * P],
                                            ctx_rows[:, slot, tile % LOAD, c * P:(c + 1) * P], ident[:, :])
                last.then_inc(ctxT_made, 1)

            def transpose_x():
                pe.wait_ge(norm_chain, NORMALISED)
                for c in range(DC):
                    for t in range(TOK_TILES):
                        last = pe.transpose(k_ps[c][:, t * P:(t + 1) * P], xn[:, t, c * P:(c + 1) * P], ident[:, :])
                    last.then_inc(xT_made, 1)

            def project_q(it, b):
                pe.wait_ge(wq_copied, it + 1)
                for c in range(DC):
                    last = mm(v_ps[:, 0:SEQ], wq_pair[:, c, :], xnT[:, c, b * SEQ:(b + 1) * SEQ],
                              start=(c == 0), stop=(c == DC - 1))
                last.then_inc(q_made, 1)

            def project(out, kind, keys):
                passes = [(w, s, c) for w, s in ((w_hi, ctxT_lo), (w_lo, ctxT_hi), (w_hi, ctxT_hi)) for c in range(DC)]
                for n, (w, s, c) in enumerate(passes):
                    last = mm(out, w[:, kind, c, :], s[:, c, keys], start=(n == 0), stop=(n == len(passes) - 1))
                return last

            def project_k(it, j):
                project(k_ps[j % 2][:, :], 0, slice(j * CHUNK, (j + 1) * CHUNK)).then_inc(k_made, 1)

            def project_vT(it, j):
                if j == 0:
                    wait_past(pe, y_added, it)
                elif vT_bank(j) is vT_bank(j - 1):
                    pe.wait_ge(vT_copied, STEPS * it + j)
                else:
                    pe.wait_ge(vT_copied, STEPS * it + j - 1)
                project(vT_bank(j)[:, :], 1, slice(j * CHUNK, (j + 1) * CHUNK)).then_inc(vT_made, 1)

            def transpose_v(it, j):
                pe.wait_ge(vT_copied, STEPS * it + j + 1)
                if j == 0:
                    pe.wait_ge(q_low, 2 * it + 2)
                elif j < STEPS - 1:
                    pe.wait_ge(v_copied, STEPS * it + j)
                for t in range(KT):
                    last = pe.transpose(v_bank(j)[:, t * P:(t + 1) * P], vT_sb[j % 2][:, t * P:(t + 1) * P], ident[:, :])
                last.then_inc(v_made, 1)

            def scores_for_max(it, j):
                keys = slice(j * CHUNK, (j + 1) * CHUNK)
                for h in (A, B):
                    pe.wait_ge(k_low, 2 * (STEPS * it + j) + h + 1)
                    if j > 0:
                        pe.wait_ge(max_done, 2 * (STEPS * it + j - 1) + h + 1)
                    else:
                        wait_past(pe, exp_done, 2 * STEPS * it)
                    for qt in range(QT):
                        last = mm(scores[h][:, qt, :], q_twice[:, h, qt * P:(qt + 1) * P], k_split[:, h, keys],
                                  start=True, stop=True)
                    last.then_inc(pre_made, 1)

            def scores_by_keys(it, j, h):
                if j > 0:
                    pe.wait_ge(exp_done, 2 * (STEPS * it + j - 1) + h + 1)
                for t in range(KT):
                    keys = slice((j * KT + t) * P, (j * KT + t + 1) * P)
                    out = flat_scores[h][:, t * SEQ:(t + 1) * SEQ]
                    mm(out, k_split[:, h, keys], q_twice[:, h, :], start=True, stop=False)
                    last = mm(out, k_ones[:, h, keys], q_low_max[:, h, :], start=False, stop=True)
                last.then_inc(scores_made, 1)

            def product_with_v(it, j):
                if j == 0:
                    pe.wait_ge(v_copied, STEPS * (it + 1))
                pe.wait_ge(exp_done, 2 * (STEPS * it + j) + 2)
                for t in range(KT):
                    for h in (A, B):
                        last = mm(out_ps[h * DH:(h + 1) * DH, SEQ:2 * SEQ],
                                  v_rows[:, j * KT + t, h * DH:(h + 1) * DH],
                                  probs[:, j % 2, h, t * SEQ:(t + 1) * SEQ],
                                  start=(j == 0 and t == 0), stop=(j == STEPS - 1 and t == KT - 1))
                last.then_inc(pv_done, 1)

            def sum_over_keys(it):
                pe.wait_ge(fold_done, 2 * it + 2)
                for h in (A, B):
                    last = mm(out_ps[h * DH:(h + 1) * DH, 0:SEQ], ones[:, :], prob_sum[:, h, 0:SEQ],
                              start=True, stop=True)
                last.then_inc(den_made, 1)

            def project_output(it):
                pe.wait_ge(outT_ready, it + 1)
                pe.wait_ge(wo_loaded, 16 * (it + 1))
                for qt in range(QT):
                    last = mm(out_ps[:, qt * D:(qt + 1) * D], outT[:, qt * P:(qt + 1) * P], wo_pair[:, :],
                              start=True, stop=True)
                last.then_inc(y_made, 1)

            def body(it, b, i):
                project_q(it, b)
                pe.wait_ge(w_low, it + 1)
                for j in range(STEPS):
                    if j >= 2:
                        pe.wait_ge(k_low, 2 * (STEPS * it + j - 1))
                    project_k(it, j)
                    if not is_first(it):
                        if j == 0:
                            sum_over_keys(it - 1)
                    if j > 1:
                        scores_for_max(it, j - 2)
                    if j == 2 and not is_first(it):
                        project_output(it - 1)
                    if j > 2:
                        project_vT(it, j - 3)
                    if j > 3:
                        transpose_v(it, j - 4)
                scores_for_max(it, STEPS - 2)
                project_vT(it, STEPS - 3)
                transpose_v(it, STEPS - 4)
                scores_for_max(it, STEPS - 1)
                for j in (STEPS - 2, STEPS - 1):
                    project_vT(it, j)
                    transpose_v(it, j - 1)
                pe.wait_ge(max_chain, 2 * it + 2)
                for qt in range(QT):
                    last = pe.transpose(k_ps[0][:, qt * P:(qt + 1) * P], neg_max[:, qt, :], ident[:, :])
                last.then_inc(maxT_made, 1)
                transpose_v(it, STEPS - 1)
                pe.wait_ge(q_low, 2 * it + 2)
                pe.wait_ge(max_ready, 2 * it + 2)
                pe.wait_ge(k_copied, 2 * STEPS * (it + 1))
                for j in range(STEPS):
                    for h in (A, B):
                        scores_by_keys(it, j, h)
                    if j > 0:
                        product_with_v(it, j - 1)
                product_with_v(it, STEPS - 1)

            for b in range(BATCH):
                for g in range(GROUPS):
                    transpose_context(b, g)
                    if b == 0 and g == 2:
                        transpose_x()
                if b == 0:
                    pe.wait_ge(xT_copied, DC)
                    pe.wait_ge(consts_ready, 6)
                pe.wait_ge(ctx_low, (b + 1) * GROUPS)
                pairs_of_batch(pe, b, body)
            sum_over_keys(BATCH * PAIRS - 1)
            project_output(BATCH * PAIRS - 1)



MEM = 16
KEYS = MEM + SEQ
ROWS = P // HEADS
GPS = 2
STEP_ROWS = GPS * ROWS
SA_STEPS = SEQ // STEP_ROWS
RING = 3
LOW = -3.0e38


def self_attention(nc, w_q, w_kv, w_o, pre_proj, post_proj, mem_k, mem_v, x_res, ident):
    with ExitStack() as stack:
        r = Resources(nc, stack)
        shared = r.sbuf("shared", [P, 2 * HEADS * SEQ])
        wq_sb = shared[:, 0:DC * INNER].rearrange("p (c n) -> p c n", c=DC)
        wkv_sb = shared[:, DC * INNER:3 * DC * INNER].rearrange("p (c n) -> p c n", c=DC)
        mixed = [shared[:, n * HEADS * SEQ:(n + 1) * HEADS * SEQ].rearrange("p (k i) -> p k i", k=HEADS)
                 for n in range(2)]
        mixed_mem = r.sbuf("mixed_mem", [MEM, HEADS, SEQ])
        wo_sb = r.sbuf("wo_sb", [P, PAIRS, D])
        normed = r.sbuf("normed", [P, PAIRS * SEQ])
        xn = normed[:, 0:TOK_TILES * D].rearrange("p (t d) -> p t d", t=TOK_TILES)
        xnT = normed[:, TOK_TILES * D:].rearrange("p (c n) -> p c n", c=DC)
        outT = normed[:, :].rearrange("p (k i) -> p k i", k=PAIRS)
        stats = r.sbuf("stats2", [P, TOK_TILES, 6])
        moments = r.sbuf("moments2", [P, TOK_TILES, 2])
        power = r.sbuf("power2", [P, TOK_TILES])
        q_padded = r.sbuf("q_padded", [P, HEADS, BATCH * SEQ])
        kT = r.sbuf("kT", [P, PAIRS, BATCH, KEYS])
        v_sb = r.sbuf("v_sb", [P, TOK_TILES, INNER])
        memk_sb = r.sbuf("memk_sb", [P, 2, DH])
        memv_sb = r.sbuf("memv_sb", [MEM, HEADS, DH])
        dots_sb = r.sbuf("dots_sb", [P, HEADS, KEYS])
        grouped = r.sbuf("grouped", [P, 2, P // ROWS, KEYS])
        expd = r.sbuf("expd", [P, RING, GPS, KEYS])
        proj_sb = r.sbuf("proj_sb", [HEADS, 2, HEADS])
        spread = r.sbuf("spread", [HEADS, P])
        same_row = r.sbuf("same_row", [P, ROWS])
        rep = r.sbuf("rep", [P, 2, HEADS])
        kron = r.sbuf("kron", [P, 2, HEADS, ROWS])
        kron_scaled = r.sbuf("kron_scaled", [P, RING, GPS, P])
        row_of = r.sbuf("row_of", [P, 1])
        columns = r.sbuf("columns", [P, GPS, STEP_ROWS])
        weighted = r.sbuf("weighted", [P, ROWS])
        causal = r.sbuf("causal", [P, GPS, STEP_ROWS])
        top = r.sbuf("top", [P, RING, GPS])
        neg_top = r.sbuf("neg_top", [P, RING, GPS])
        total = r.sbuf("total", [P, RING, GPS])
        inv_total = r.sbuf("inv_total", [P, RING, GPS])

        bank = [r.psum(f"bank{n}", [P, 2, 512]) for n in range(4)]

        w_in = r.sem("w_in")
        small_in = r.sem("small_in")
        norm_chain = r.sem("norm_chain2")
        inverse_std = r.sem("inverse_std2")
        xT_made = r.sem("xT_made2")
        xT_copied = r.sem("xT_copied2")
        consts = r.sem("consts")
        zeroed = r.sem("zeroed")
        kron_made = r.sem("kron_made")
        kron_chain = r.sem("kron_chain")
        memk_made = r.sem("memk_made")
        memk_copied = r.sem("memk_copied")
        proj_made = r.sem("proj_made")
        proj_copied = [r.sem("proj_by_act"), r.sem("proj_by_dve")]
        dots_made = r.sem("dots_made")
        dots_copied = [r.sem("dots_by_act"), r.sem("dots_by_dve")]
        regrouped = r.sem("regrouped")
        mix_made = r.sem("mix_made")
        masked = r.sem("masked")
        top_done = r.sem("top_done")
        neg_done = r.sem("neg_done")
        exp_done = r.sem("exp_done2")
        tail_zero = r.sem("tail_zero")
        inv_done = r.sem("inv_done")
        kron_done = r.sem("kron_done")
        post_made = r.sem("post_made")
        mixed_by_act = r.sem("mixed_by_act")
        mixed_by_dve = r.sem("mixed_by_dve")
        out_made = r.sem("out_made")
        out_copied = r.sem("out_copied")
        y_made = r.sem("y_made2")
        y_added = r.sem("y_added2")

        Q, K, V = range(3)
        projections = [(kind, n) for n in range(PAIRS) for kind in (Q, K)] + [(V, n) for n in range(2 * TOK_TILES)]
        NPROJ = len(projections)
        DOT_STEPS = BATCH * QT * PAIRS

        def dot_keys(t):
            return MEM + (t + 1) * P

        def step_keys(s):
            return MEM + (s + 1) * STEP_ROWS

        block = stack.enter_context(nc.Block())

        @block.sync
        def _(sp):
            sp.dma_start(wq_sb, w_q.rearrange("(c p) n -> p c n", p=P)).then_inc(w_in, 16)
            sp.dma_start(wkv_sb, w_kv.rearrange("(c p) n -> p c n", p=P)).then_inc(w_in, 16)
            sp.dma_start(wo_sb[:, :, :], w_o.rearrange("(c p) n -> p c n", p=P)).then_inc(w_in, 16)
            sp.dma_start(proj_sb[:, 0, :], pre_proj).then_inc(small_in, 16)
            sp.dma_start(proj_sb[:, 1, :], post_proj).then_inc(small_in, 16)
            sp.dma_start(memv_sb[:, :, :], mem_v.rearrange("h m d -> m h d")).then_inc(small_in, 16)
            for pair in range(PAIRS):
                sp.dma_start(memk_sb[pair * MEM:(pair + 1) * MEM, :, :],
                             mem_k[2 * pair:2 * pair + 2].rearrange("h m d -> m h d")).then_inc(small_in, 16)
            for b in range(BATCH):
                for t in range(QT):
                    if b > 0:
                        sp.wait_ge(mix_made, (b - 1) * SA_STEPS + (t + 1) * SA_STEPS // QT)
                    for h in range(HEADS):
                        n = (b * QT + t) * PAIRS + h // 2
                        sp.wait_ge(dots_copied[n % 2], n // 2 + 1)
                        keys = dot_keys(t)
                        sp.dma_start(grouped[h * ROWS:(h + 1) * ROWS, t, :, 0:keys],
                                     dots_sb[:, h, 0:keys]).then_inc(regrouped, 16)

        @block.gpsimd
        def _(pool):
            pool.memset(q_padded[:, :, :], 0.0).then_inc(zeroed, 1)
            pool.memset(spread[:, :], 1.0).then_inc(consts, 1)
            for n in range(GPS):
                for c in range(STEP_ROWS):
                    pool.memset(columns[:, n, c:c + 1], float(c - n * ROWS)).then_inc(consts, 1)
            pool.wait_ge(consts, 1 + GPS * STEP_ROWS)
            pool.affine_select(out=spread[:, :], in_=spread[:, :], compare_op=ALU.is_ge, fill=0.0, base=0,
                               pattern=[[1, P]], channel_multiplier=-ROWS).then_inc(consts, 1)
            pool.wait_ge(consts, 2 + GPS * STEP_ROWS)
            pool.affine_select(out=spread[:, :], in_=spread[:, :], compare_op=ALU.is_ge, fill=0.0, base=ROWS - 1,
                               pattern=[[-1, P]], channel_multiplier=ROWS).then_inc(consts, 1)
            invert_std(pool, moments, power, norm_chain, inverse_std)
            for n in range(BATCH * SA_STEPS):
                s = n % SA_STEPS
                keys = step_keys(s)
                if n >= RING:
                    pool.wait_ge(post_made, n - RING + 1)
                if s < RING:
                    pool.memset(expd[:, n % RING, :, keys:KEYS], 0.0).then_inc(tail_zero, 1)
                pool.wait_ge(inv_done, n + 1)
                for g in range(GPS):
                    pool.tensor_scalar(kron_scaled[:, n % RING, g, :], kron[:, 1, :, :], inv_total[:, n % RING, g:g + 1],
                                       None, ALU.mult).then_inc(kron_done, 1)

        def copy_projection(copy, n):
            kind, m = projections[n]
            src = bank[n % 4][:, 0, :]
            if kind == Q:
                queries = src.rearrange("p (t g r) -> p t g r", g=P // ROWS, r=ROWS)
                for half in range(2):
                    rows = slice(half * DH, (half + 1) * DH)
                    place = q_padded[rows, 2 * m + half, :].rearrange("p (t r g) -> p t g r", g=P // ROWS, r=ROWS)
                    ins = copy(place, queries[rows])
            elif kind == K:
                ins = copy(kT[:, m, :, MEM:KEYS], src.rearrange("p (b n) -> p b n", b=BATCH))
            else:
                ins = copy(v_sb[:, m // 2, (m % 2) * 512:(m % 2 + 1) * 512], src)
            ins.then_inc(proj_copied[n % 2], 1)

        def copy_dots(eng, scaled_copy, n):
            t = n // PAIRS % QT
            pair = n % PAIRS
            keys = dot_keys(t)
            eng.wait_ge(dots_made, n + 1)
            if n >= PAIRS:
                eng.wait_ge(regrouped, 16 * HEADS * (n // PAIRS))
            scaled_copy(dots_sb[:, 2 * pair:2 * pair + 2, 0:keys], bank[n % 2][:, :, 0:keys]
                        ).then_inc(dots_copied[n % 2], 1)

        def mixed_place(n, to):
            i = n % SA_STEPS * STEP_ROWS
            return to[:, :, i:i + STEP_ROWS].rearrange("p k (g r) -> p g k r", g=GPS)

        def mixed_source(n, rows, half, at):
            return bank[0][0:rows, half, at:at + GPS * P].rearrange("p (g k r) -> p g k r", g=GPS, k=HEADS)

        @block.scalar
        def _(act):
            def copy(out, src):
                return act.activation(out, src, ACT.Copy)

            def scaled_copy(out, src):
                return act.activation(out, src, ACT.Copy, scale=SCALE)

            act.wait_ge(zeroed, 1)
            for n in range(0, NPROJ, 2):
                act.wait_ge(proj_made, n + 1)
                copy_projection(copy, n)

            def exponentials(n):
                keys = step_keys(n % SA_STEPS)
                act.wait_ge(neg_done, n + 1)
                if n >= RING:
                    act.wait_ge(post_made, n - RING + 1)
                    act.wait_ge(inv_done, n - RING + 1)
                for g in range(GPS):
                    act.activation(expd[:, n % RING, g, 0:keys], bank[1 + n % RING][:, g, 0:keys], ACT.Exp,
                                   bias=neg_top[:, n % RING, g:g + 1], accum_out=total[:, n % RING, g:g + 1]
                                   ).then_inc(exp_done, 1)

            def copy_mixed(n):
                act.wait_ge(post_made, n + 1)
                copy(mixed_place(n, mixed[0]), mixed_source(n, P, 0, 0)).then_inc(mixed_by_act, 1)

            def copy_scores(b):
                for n in range(b * QT * PAIRS, (b + 1) * QT * PAIRS, 2):
                    copy_dots(act, scaled_copy, n)

            copy_scores(0)
            for b in range(BATCH):
                first = b * SA_STEPS
                for n in range(first, first + SA_STEPS):
                    exponentials(n)
                    if n >= first + 2:
                        copy_mixed(n - 2)
                copy_mixed(first + SA_STEPS - 2)
                copy_mixed(first + SA_STEPS - 1)
                if b < BATCH - 1:
                    copy_scores(b + 1)
                for n in range(b * PAIRS, (b + 1) * PAIRS):
                    act.wait_ge(out_made, n + 1)
                    copy(outT[:, n % PAIRS, :], bank[2 + n % 2][:, 0, 0:SEQ]).then_inc(out_copied, 1)

        @block.vector
        def _(dve):
            normalise_rows(dve, x_res, xn, stats, moments, norm_chain, inverse_std)
            for c in range(DC):
                dve.wait_ge(xT_made, c + 1)
                dve.tensor_copy(xnT[:, c, :], bank[0][:, c, :]).then_inc(xT_copied, 1)
            dve.tensor_reduce(same_row[:, :], ident[:, :].rearrange("p (h r) -> p r h", r=ROWS), X, ALU.add
                              ).then_inc(kron_chain, 1)
            dve.wait_ge(kron_made, 1)
            dve.tensor_copy(rep[:, :, :].rearrange("p a k -> p (a k)"), bank[3][:, 0, 0:2 * HEADS]
                            ).then_inc(kron_chain, 1)
            dve.wait_ge(kron_chain, 2)
            for n in range(2):
                dve.tensor_tensor(kron[:, n, :, :], rep[:, n, :].unsqueeze(2).to_broadcast([P, HEADS, ROWS]),
                                  same_row[:, :].unsqueeze(1).to_broadcast([P, HEADS, ROWS]), ALU.mult
                                  ).then_inc(kron_chain, 1)
            dve.wait_ge(consts, 3 + GPS * STEP_ROWS)
            dve.tensor_tensor(weighted[:, :], same_row[:, :], columns[:, 0, 0:ROWS], ALU.mult).then_inc(kron_chain, 1)
            dve.wait_ge(kron_chain, 5)
            dve.tensor_reduce(row_of[:, :], weighted[:, :], X, ALU.add).then_inc(kron_chain, 1)
            dve.wait_ge(kron_chain, 6)
            dve.tensor_scalar(causal[:, :, :], columns[:, :, :], row_of[:, 0:1], LOW, ALU.is_gt, ALU.mult
                              ).then_inc(kron_chain, 1)
            dve.wait_ge(kron_chain, 7)
            dve.wait_ge(memk_made, 1)
            for b in range(BATCH):
                dve.tensor_copy(kT[:, :, b, 0:MEM], bank[3][:, 1, 0:P].rearrange("p (k m) -> p k m", m=MEM)
                                ).then_inc(memk_copied, 1)
            for n in range(1, NPROJ, 2):
                dve.wait_ge(proj_made, n + 1)
                copy_projection(dve.tensor_copy, n)

            def scaled_copy(out, src):
                return dve.tensor_scalar(out, src, SCALE, None, ALU.mult)

            def maximum(n):
                keys = step_keys(n % SA_STEPS)
                ps = bank[1 + n % RING]
                dve.wait_ge(mix_made, n + 1)
                last = ps[:, :, keys - STEP_ROWS:keys]
                dve.tensor_tensor(last, last, causal[:, :, :], ALU.add).then_inc(masked, 1)
                dve.wait_ge(masked, n + 1)
                dve.tensor_reduce(top[:, n % RING, :], ps[:, :, 0:keys], X, ALU.max).then_inc(top_done, 1)
                dve.wait_ge(top_done, n + 1)
                if n >= RING:
                    dve.wait_ge(exp_done, GPS * (n - RING + 1))
                dve.tensor_scalar(neg_top[:, n % RING, :], top[:, n % RING, :], -1.0, None, ALU.mult).then_inc(neg_done, 1)

            def invert(n):
                dve.wait_ge(exp_done, GPS * (n + 1))
                if n >= RING:
                    dve.wait_ge(kron_done, GPS * (n - RING + 1))
                dve.reciprocal(inv_total[:, n % RING, :], total[:, n % RING, :]).then_inc(inv_done, 1)

            def copy_mixed(n):
                dve.wait_ge(post_made, n + 1)
                ins = dve.tensor_copy(mixed_place(n, mixed_mem), mixed_source(n, MEM, 1, GPS * P))
                if n % SA_STEPS >= SA_STEPS // QT:
                    ins = dve.tensor_copy(mixed_place(n, mixed[1]), mixed_source(n, P, 1, 0))
                ins.then_inc(mixed_by_dve, 1)

            def copy_scores(b):
                for n in range(b * QT * PAIRS + 1, (b + 1) * QT * PAIRS, 2):
                    copy_dots(dve, scaled_copy, n)

            copy_scores(0)
            for b in range(BATCH):
                first = b * SA_STEPS
                for n in range(first, first + SA_STEPS):
                    maximum(n)
                    if n >= first + 1:
                        invert(n - 1)
                    if n >= first + 2:
                        copy_mixed(n - 2)
                invert(first + SA_STEPS - 1)
                copy_mixed(first + SA_STEPS - 2)
                copy_mixed(first + SA_STEPS - 1)
                if b < BATCH - 1:
                    copy_scores(b + 1)
                for n in range(b * QT, (b + 1) * QT):
                    dve.wait_ge(y_made, n + 1)
                    dve.tensor_tensor(x_res[:, n, :], x_res[:, n, :], bank[2 + n % 2][:, 1, 0:D], ALU.add
                                      ).then_inc(y_added, 1)

        @block.tensor
        def _(pe):
            mm = pe.matmul
            pe.wait_ge(small_in, 16 * (3 + PAIRS))
            pe.wait_ge(consts, 3 + GPS * STEP_ROWS)
            mm(bank[3][:, 0, 0:2 * HEADS], spread[:, :], proj_sb[:, :, :].rearrange("p a k -> p (a k)"),
               start=True, stop=True).then_inc(kron_made, 1)
            pe.transpose(bank[3][:, 1, 0:P], memk_sb[:, :, :].rearrange("p a d -> p (a d)"), ident[:, :]
                         ).then_inc(memk_made, 1)
            pe.wait_ge(norm_chain, NORMALISED)
            for c in range(DC):
                for t in range(TOK_TILES):
                    last = pe.transpose(bank[0][:, c, t * P:(t + 1) * P], xn[:, t, c * P:(c + 1) * P], ident[:, :])
                last.then_inc(xT_made, 1)
            pe.wait_ge(xT_copied, DC)
            pe.wait_ge(w_in, 48)
            pe.wait_ge(memk_copied, BATCH)
            for n, (kind, m) in enumerate(projections):
                if n >= 4:
                    pe.wait_ge(proj_copied[n % 2], (n - 4) // 2 + 1)
                for c in range(DC):
                    if kind == Q:
                        w, a = wq_sb[:, c, m * P:(m + 1) * P], xnT[:, c, :]
                    elif kind == K:
                        w, a = wkv_sb[:, c, m * P:(m + 1) * P], xnT[:, c, :]
                    else:
                        at = INNER + (m % 2) * 512
                        w, a = xnT[:, c, (m // 2) * P:(m // 2 + 1) * P], wkv_sb[:, c, at:at + 512]
                    last = mm(bank[n % 4][:, 0, :], w, a, start=(c == 0), stop=(c == DC - 1))
                last.then_inc(proj_made, 1)

            def dots(n):
                t, b, pair = n // PAIRS % QT, n // PAIRS // QT, n % PAIRS
                keys = dot_keys(t)
                if n >= 2:
                    pe.wait_ge(dots_copied[n % 2], (n - 2) // 2 + 1)
                for half in range(2):
                    tokens = (b * QT + t) * P
                    last = mm(bank[n % 2][:, half, 0:keys], q_padded[:, 2 * pair + half, tokens:tokens + P],
                              kT[:, pair, b, 0:keys], start=True, stop=True)
                last.then_inc(dots_made, 1)

            def mix(n):
                b, s = n // SA_STEPS, n % SA_STEPS
                keys = step_keys(s)
                pe.wait_ge(regrouped, 16 * HEADS * (b * QT + s // (SA_STEPS // QT) + 1))
                if n >= RING:
                    pe.wait_ge(exp_done, GPS * (n - RING + 1))
                for g in range(GPS):
                    group = s * GPS + g
                    last = mm(bank[1 + n % RING][:, g, 0:keys], kron[:, 0, :, :].rearrange("p k r -> p (k r)"),
                              grouped[:, group // (P // ROWS), group % (P // ROWS), 0:keys], start=True, stop=True)
                last.then_inc(mix_made, 1)

            def post(n):
                b, s = n // SA_STEPS, n % SA_STEPS
                pe.wait_ge(kron_done, GPS * (n + 1))
                pe.wait_ge(tail_zero, b * RING + min(s + 1, RING))
                if n >= 1:
                    pe.wait_ge(mixed_by_act, n)
                    pe.wait_ge(mixed_by_dve, n)
                for g in range(GPS):
                    e, k = expd[:, n % RING, g, :], kron_scaled[:, n % RING, g, :]
                    mm(bank[0][0:MEM, 1, (GPS + g) * P:(GPS + g + 1) * P], e[:, 0:MEM], k, start=True, stop=True)
                    last = mm(bank[0][:, 0, g * P:(g + 1) * P], e[:, MEM:MEM + P], k, start=True, stop=True)
                    if s >= SA_STEPS // QT:
                        last = mm(bank[0][:, 1, g * P:(g + 1) * P], e[:, MEM + P:KEYS], k, start=True, stop=True)
                last.then_inc(post_made, 1)

            def product_with_v(n):
                b, pair = n // PAIRS, n % PAIRS
                if n % PAIRS >= 2 :
                    pe.wait_ge(out_copied, n - 1)
                for half in range(2):
                    k = 2 * pair + half
                    out = bank[2 + n % 2][half * DH:(half + 1) * DH, 0, :]
                    mm(out[:, 0:SEQ], memv_sb[:, k, :], mixed_mem[:, k, :], start=True, stop=False)
                    mm(out[:, 0:SEQ], v_sb[:, b * QT, k * DH:(k + 1) * DH], mixed[0][:, k, :], start=False, stop=False)
                    last = mm(out[:, P:SEQ], v_sb[:, b * QT + 1, k * DH:(k + 1) * DH], mixed[1][:, k, P:SEQ],
                              start=False, stop=True)
                last.then_inc(out_made, 1)

            def output(n):
                for pair in range(PAIRS):
                    last = mm(bank[2 + n % 2][:, 1, 0:D], outT[:, pair, n % QT * P:(n % QT + 1) * P], wo_sb[:, pair, :],
                              start=(pair == 0), stop=(pair == PAIRS - 1))
                last.then_inc(y_made, 1)

            for eng in range(2):
                pe.wait_ge(proj_copied[eng], NPROJ // 2)
            def all_dots(b):
                for n in range(b * QT * PAIRS, (b + 1) * QT * PAIRS):
                    dots(n)

            all_dots(0)
            for b in range(BATCH):
                first = b * SA_STEPS
                for eng in range(2):
                    pe.wait_ge(dots_copied[eng], (b + 1) * QT * PAIRS // 2)
                if b > 0:
                    pe.wait_ge(y_added, b * QT)
                for n in range(first, first + SA_STEPS + RING - 1):
                    if n < first + SA_STEPS:
                        mix(n)
                    if n >= first + RING - 1:
                        post(n - RING + 1)
                pe.wait_ge(mixed_by_act, first + SA_STEPS)
                pe.wait_ge(mixed_by_dve, first + SA_STEPS)
                if b < BATCH - 1:
                    all_dots(b + 1)
                for n in range(b * PAIRS, (b + 1) * PAIRS):
                    product_with_v(n)
                pe.wait_ge(out_copied, (b + 1) * PAIRS)
                for n in range(b * QT, (b + 1) * QT):
                    output(n)


FF = 768
FC = FF // P
BLOCK = 32
W_MAX = 2.0 ** 3 - 1.0
A_MAX = 2.0 ** 15 - 1.0
U_STEPS = 65536.0
ROUND = 1.5 * 2.0 ** 23
TINY = 1e-12


def gated_ffn(nc, w_gate, w_up, w_down, x_res, out, ident):
    with ExitStack() as stack:
        r = Resources(nc, stack)
        NB = FF * D // P // BLOCK
        UP, GATE, DOWN = range(3)
        w_sb = [r.sbuf(f"w_sb{n}", [P, NB, BLOCK]) for n in range(3)]
        w_top = r.sbuf("w_top", [P, 3, NB])
        w_bottom = r.sbuf("w_bottom", [P, 3, NB])
        w_scale = r.sbuf("w_scale", [P, 3, NB])
        w_inverse = r.sbuf("w_inverse", [P, 3, NB])
        wT = [r.sbuf(f"wT{n}", [P, FF * D // P]) for n in range(3)]
        upT, gateT = (wT[n][:, :].rearrange("p (c f) -> p c f", c=DC) for n in (UP, GATE))
        downT = wT[DOWN][:, :].rearrange("p (c d) -> p c d", c=FC)
        xn = r.sbuf("xn3", [P, TOK_TILES, D])
        xqT = r.sbuf("xqT", [P, DC, BATCH * SEQ])
        stats = r.sbuf("stats3", [P, TOK_TILES, 6])
        moments = r.sbuf("moments3", [P, TOK_TILES, 2])
        power = r.sbuf("power3", [P, TOK_TILES])
        up = r.sbuf("up", [P, FC, BATCH * SEQ])
        gate = r.sbuf("gate", [P, FC, BATCH * SEQ])
        sig = r.sbuf("sig", [P, FC, BATCH * SEQ])
        limits = r.sbuf("limits", [P, 5, 8])
        bank = [r.psum(f"ffn_bank{n}", [P, 512]) for n in range(8)]

        w_in = r.sem("w_in3")
        norm_chain = r.sem("norm_chain3")
        inverse_std = r.sem("inverse_std3")
        w_chain = r.sem("w_chain")
        q_chain = r.sem("q_chain")
        peak = r.sem("peak")
        xq_ready = r.sem("xq_ready")
        xqT_made = r.sem("xqT_made")
        xqT_copied = r.sem("xqT_copied")
        wT_made = r.sem("wT_made")
        wT_copied = r.sem("wT_copied")
        hidden_made = r.sem("hidden_made")
        hidden_copied = r.sem("hidden_copied")
        sig_ready = r.sem("sig_ready")
        product_ready = r.sem("product_ready")
        y_made = r.sem("y_made3")
        y_added = r.sem("y_added3")
        stored = r.sem("stored")
        Q_OPS = 8
        WT_BANKS = FF * D // P // 512
        block = stack.enter_context(nc.Block())

        @block.sync
        def _(sp):
            for n, w in ((UP, w_up), (GATE, w_gate), (DOWN, w_down)):
                t = w.shape[0] // P
                sp.dma_start(w_sb[n][:, :, :].rearrange("p b k -> p (b k)").rearrange("p (t i) -> p t i", t=t),
                             w.rearrange("(t p) i -> p t i", p=P)).then_inc(w_in, 16)
            for t in range(TOK_TILES):
                sp.wait_ge(y_added, t + 1)
                sp.dma_start(out.rearrange("b (t p) d -> p (b t) d", p=P)[:, t, :], x_res[:, t, :]).then_inc(stored, 16)
            sp.wait_ge(stored, 16 * TOK_TILES)

        @block.gpsimd
        def _(pool):
            invert_std(pool, moments, power, norm_chain, inverse_std)
            for n in range(5):
                pool.wait_ge(q_chain, Q_OPS * n + 3)
                pool.partition_all_reduce(limits[:, n, 3:4], limits[:, n, 2:3], P, bass.bass_isa.ReduceOp.max
                                          ).then_inc(peak, 1)

        @block.scalar
        def _(act):
            for n in range(3 * WT_BANKS):
                m, c = n // WT_BANKS, n % WT_BANKS
                act.wait_ge(wT_made, n + 1)
                act.activation(wT[m][:, c * 512:(c + 1) * 512], bank[n % 4][:, :], ACT.Copy).then_inc(wT_copied, 1)
            for n in range(2 * FC):
                act.wait_ge(hidden_made, n + 1)
                act.activation((up if n < FC else gate)[:, n % FC, :], bank[n % 8][:, :], ACT.Copy
                               ).then_inc(hidden_copied, 1)
            act.wait_ge(q_chain, 3 * Q_OPS)
            act.activation(sig[:, :, :], gate[:, :, :], ACT.Sigmoid).then_inc(sig_ready, 1)

        @block.vector
        def _(dve):
            def quantise(n, t):
                a = limits[:, n, :]
                base = Q_OPS * n
                dve.tensor_reduce(a[:, 0:1], t, X, ALU.max).then_inc(q_chain, 1)
                dve.tensor_reduce(a[:, 1:2], t, X, ALU.min).then_inc(q_chain, 1)
                dve.wait_ge(q_chain, base + 2)
                dve.scalar_tensor_tensor(a[:, 2:3], a[:, 1:2], -1.0, a[:, 0:1], ALU.mult, ALU.max).then_inc(q_chain, 1)
                dve.wait_ge(peak, n + 1)
                dve.tensor_scalar(a[:, 4:5], a[:, 3:4], 1.0 / A_MAX, TINY, ALU.mult, ALU.max).then_inc(q_chain, 1)
                dve.wait_ge(q_chain, base + 4)
                dve.reciprocal(a[:, 5:6], a[:, 4:5]).then_inc(q_chain, 1)
                dve.wait_ge(q_chain, base + 5)
                dve.tensor_scalar(t, t, a[:, 5:6], ROUND, ALU.mult, ALU.add).then_inc(q_chain, 1)
                dve.wait_ge(q_chain, base + 6)
                dve.tensor_scalar(t, t, ROUND, A_MAX, ALU.subtract, ALU.min).then_inc(q_chain, 1)
                dve.wait_ge(q_chain, base + 7)
                dve.tensor_scalar(t, t, -A_MAX - 1.0, a[:, 4:5], ALU.max, ALU.mult).then_inc(q_chain, 1)
                dve.wait_ge(q_chain, base + Q_OPS)

            normalise_rows(dve, x_res, xn, stats, moments, norm_chain, inverse_std)
            dve.wait_ge(norm_chain, NORMALISED)
            xflat = xn[:, :, :].rearrange("p t d -> p (t d)")
            quantise(0, xflat)
            dve.wait_ge(w_in, 48)
            for n in range(3):
                w = w_sb[n]
                base = 9 * n
                blocks = [P, NB, BLOCK]
                dve.tensor_reduce(w_top[:, n, :], w[:, :, :], X, ALU.max).then_inc(w_chain, 1)
                dve.tensor_reduce(w_bottom[:, n, :], w[:, :, :], X, ALU.min).then_inc(w_chain, 1)
                dve.wait_ge(w_chain, base + 2)
                dve.scalar_tensor_tensor(w_top[:, n, :], w_bottom[:, n, :], -1.0, w_top[:, n, :], ALU.mult, ALU.max
                                         ).then_inc(w_chain, 1)
                dve.wait_ge(w_chain, base + 3)
                dve.tensor_scalar(w_scale[:, n, :], w_top[:, n, :], 1.0 / W_MAX, TINY, ALU.mult, ALU.max
                                  ).then_inc(w_chain, 1)
                dve.wait_ge(w_chain, base + 4)
                dve.reciprocal(w_inverse[:, n, :], w_scale[:, n, :]).then_inc(w_chain, 1)
                dve.wait_ge(w_chain, base + 5)
                dve.tensor_tensor(w[:, :, :], w[:, :, :], w_inverse[:, n, :].unsqueeze(2).to_broadcast(blocks),
                                  ALU.mult).then_inc(w_chain, 1)
                dve.wait_ge(w_chain, base + 6)
                dve.tensor_scalar(w[:, :, :], w[:, :, :], ROUND, ROUND, ALU.add, ALU.subtract).then_inc(w_chain, 1)
                dve.wait_ge(w_chain, base + 7)
                dve.tensor_scalar(w[:, :, :], w[:, :, :], W_MAX, -W_MAX - 1.0, ALU.min, ALU.max).then_inc(w_chain, 1)
                dve.wait_ge(w_chain, base + 8)
                dve.tensor_tensor(w[:, :, :], w[:, :, :], w_scale[:, n, :].unsqueeze(2).to_broadcast(blocks),
                                  ALU.mult).then_inc(w_chain, 1)
            for c in range(DC):
                dve.wait_ge(xqT_made, c + 1)
                dve.tensor_copy(xqT[:, c, :], bank[6 + c][:, :]).then_inc(xqT_copied, 1)

            def flat(t):
                return t[:, :, :].rearrange("p c n -> p (c n)")
            dve.wait_ge(hidden_copied, FC)
            quantise(1, flat(up))
            dve.wait_ge(hidden_copied, 2 * FC)
            quantise(2, flat(gate))
            dve.wait_ge(sig_ready, 1)
            s = flat(sig)
            dve.tensor_scalar(s, s, U_STEPS, ROUND, ALU.mult, ALU.add).then_inc(product_ready, 1)
            dve.wait_ge(product_ready, 1)
            dve.tensor_scalar(s, s, ROUND, U_STEPS - 1.0, ALU.subtract, ALU.min).then_inc(product_ready, 1)
            dve.wait_ge(product_ready, 2)
            dve.tensor_scalar(s, s, 0.0, 1.0 / U_STEPS, ALU.max, ALU.mult).then_inc(product_ready, 1)
            dve.wait_ge(product_ready, 3)
            dve.tensor_tensor(s, s, flat(gate), ALU.mult).then_inc(product_ready, 1)
            dve.wait_ge(product_ready, 4)
            quantise(3, s)
            dve.tensor_tensor(s, s, flat(up), ALU.mult).then_inc(product_ready, 1)
            dve.wait_ge(product_ready, 5)
            quantise(4, s)
            for t in range(TOK_TILES):
                dve.wait_ge(y_made, t + 1)
                dve.tensor_tensor(x_res[:, t, :], x_res[:, t, :], bank[t][:, 0:D], ALU.add).then_inc(y_added, 1)

        @block.tensor
        def _(pe):
            mm = pe.matmul
            pe.wait_ge(q_chain, Q_OPS)
            for c in range(DC):
                for t in range(TOK_TILES):
                    last = pe.transpose(bank[6 + c][:, t * P:(t + 1) * P], xn[:, t, c * P:(c + 1) * P], ident[:, :])
                last.then_inc(xqT_made, 1)
            for n in range(3):
                pe.wait_ge(w_chain, 9 * (n + 1))
                w = w_sb[n][:, :, :].rearrange("p b k -> p (b k)")
                tiles = 2 if n == DOWN else FC
                width = FF * D // P // tiles
                for k in range(FF * D // P // P):
                    at = n * WT_BANKS + k // 4
                    if k % 4 == 0 and at >= 4:
                        pe.wait_ge(wT_copied, at - 3)
                    c, t = k // tiles, k % tiles
                    last = pe.transpose(bank[at % 4][:, k % 4 * P:(k % 4 + 1) * P],
                                        w[:, t * width + c * P:t * width + (c + 1) * P], ident[:, :])
                    if k % 4 == 3:
                        last.then_inc(wT_made, 1)
            pe.wait_ge(wT_copied, 3 * WT_BANKS)
            pe.wait_ge(xqT_copied, DC)
            for n in range(2 * FC):
                if n >= 8:
                    pe.wait_ge(hidden_copied, n - 7)
                w = upT if n < FC else gateT
                for c in range(DC):
                    last = mm(bank[n % 8][:, :], w[:, c, n % FC * P:(n % FC + 1) * P], xqT[:, c, :],
                              start=(c == 0), stop=(c == DC - 1))
                last.then_inc(hidden_made, 1)
            pe.wait_ge(hidden_copied, 2 * FC)
            pe.wait_ge(q_chain, 5 * Q_OPS)
            for t in range(TOK_TILES):
                for c in range(FC):
                    last = mm(bank[t][:, 0:D], sig[:, c, t * P:(t + 1) * P], downT[:, c, :],
                              start=(c == 0), stop=(c == FC - 1))
                last.then_inc(y_made, 1)


def load_identity(nc, ident):
    with ExitStack() as stack:
        r = Resources(nc, stack)
        cleared = r.sem("cleared")
        block = stack.enter_context(nc.Block())

        @block.gpsimd
        def _(pool):
            pool.memset(ident[:, :], 0.0).then_inc(cleared, 1)
            pool.wait_ge(cleared, 1)
            pool.affine_select(out=ident[:, :], in_=ident[:, :], compare_op=ALU.not_equal, fill=1.0, base=0,
                               pattern=[[-1, P]], channel_multiplier=1).then_inc(cleared, 1)
            pool.wait_ge(cleared, 2)


def perceiver_layer(nc, x, ctx_1024, x_w_q, x_w_k, x_w_v, x_w_o, a_w_q, a_w_kv, a_w_o, pre_proj, post_proj,
                    mem_k, mem_v, w_gate, w_up, w_down, out):
    with ExitStack() as stack:
        r = Resources(nc, stack)
        ident = r.sbuf("ident", [P, P])
        x_res = r.sbuf("x_res", [P, TOK_TILES, D])
        load_identity(nc, ident)
        cross_attention(nc, x, ctx_1024, x_w_q, x_w_k, x_w_v, x_w_o, x_res, ident)
        self_attention(nc, a_w_q, a_w_kv, a_w_o, pre_proj, post_proj, mem_k, mem_v, x_res, ident)
        gated_ffn(nc, w_gate, w_up, w_down, x_res, out, ident)


_INS = ['x', 'ctx_1024', 'L0_xattn_w_q', 'L0_xattn_w_k', 'L0_xattn_w_v', 'L0_xattn_w_o', 'L0_attn_Wq',
        'L0_attn_Wkv', 'L0_attn_Wo', 'L0_attn_pre_proj', 'L0_attn_post_proj', 'L0_attn_mem_k', 'L0_attn_mem_v',
        'L0_ffn_w_gate', 'L0_ffn_w_up', 'L0_ffn_w_down']
_OUTS = [((2, 256, 256), 'float32')]


def kernel(**inputs):
    import numpy as _np
    import concourse.bacc as _bacc
    from concourse import mybir as _mybir
    from concourse.bass_utils import run_bass_kernel_spmd as _run

    nc = _bacc.Bacc("TRN2", target_bir_lowering=False, num_devices=1)
    arrays, args = {}, []
    for name in _INS:
        a = _np.ascontiguousarray(inputs[name])
        arrays[f"in_{name}_dram"] = a
        args.append(nc.dram_tensor(f"in_{name}_dram", a.shape, _mybir.dt.from_np(a.dtype), kind="ExternalInput").ap())
    for i, (shape, dtype) in enumerate(_OUTS):
        dt = _mybir.dt.from_np(_np.dtype(dtype))
        args.append(nc.dram_tensor(f"out_{i}_dram", shape, dt, kind="ExternalOutput").ap())
    perceiver_layer(nc, *args)
    r = _run(nc, [arrays], core_ids=[0])
    got = tuple(r.results[0][f"out_{i}_dram"] for i in range(len(_OUTS)))
    return got[0]
```

```python
from contextlib import ExitStack

import concourse.bass as bass
from concourse import mybir

F32 = mybir.dt.float32
F32R = mybir.dt.float32r
ALU = mybir.AluOpType
ACT = mybir.ActivationFunctionType
X = mybir.AxisListType.X

P = 128
BATCH, SEQ, D = 2, 256, 256
CTX = 4096
HEADS, DH = 16, 64
INNER = HEADS * DH
TOK_TILES = BATCH * SEQ // P
QT = SEQ // P
DC = D // P
PAIRS = HEADS // 2
SCALE = DH ** -0.5
EPS = 1e-5


class Resources:

    def __init__(self, nc, stack):
        self.nc, self.stack = nc, stack

    def sbuf(self, name, shape, dtype=F32):
        return self.stack.enter_context(self.nc.sbuf_tensor(name, shape, dtype))

    def psum(self, name, shape, dtype=F32):
        return self.stack.enter_context(self.nc.psum_tensor(name, shape, dtype))

    def sem(self, name):
        return self.stack.enter_context(self.nc.semaphore(name))


def wait_past(eng, sem, value):
    if not isinstance(value, int) or value > 0:
        eng.wait_ge(sem, value)


NORMALISED = 3 * TOK_TILES


def normalise_rows(dve, x, out, stats, moments, chain, inverse_std):
    n = 0
    for t in range(TOK_TILES):
        dve.bn_stats(stats[:, t, :], x[:, t, :]).then_inc(chain, 1)
    n += TOK_TILES
    dve.wait_ge(chain, n)
    for t in range(TOK_TILES):
        dve.bn_aggr(moments[:, t, :], stats[:, t, :]).then_inc(chain, 1)
    n += TOK_TILES
    dve.wait_ge(inverse_std, 3)
    for t in range(TOK_TILES):
        dve.tensor_scalar(out[:, t, :], x[:, t, :], moments[:, t, 0:1], moments[:, t, 1:2],
                          ALU.subtract, ALU.mult).then_inc(chain, 1)
    assert n + TOK_TILES == NORMALISED


def invert_std(pool, moments, power, chain, inverse_std):
    pool.memset(power[:, :], -0.5).then_inc(inverse_std, 1)
    pool.wait_ge(chain, 2 * TOK_TILES)
    pool.tensor_scalar(moments[:, :, 1], moments[:, :, 1], EPS, None, ALU.add).then_inc(inverse_std, 1)
    pool.wait_ge(inverse_std, 2)
    pool.tensor_tensor(moments[:, :, 1], moments[:, :, 1], power[:, :], ALU.pow).then_inc(inverse_std, 1)


def cross_attention(nc, x, ctx_in, w_q, w_k, w_v, w_o, x_res, ident):
    CHUNK = 512
    STEPS = CTX // CHUNK
    KT = CHUNK // P
    LOAD = 4
    LOADS = CTX // P // LOAD
    HALF = CTX // P // 2
    PAIR = 2 * DH
    V_TILES = HALF // STEPS
    A, B = 0, 1

    with ExitStack() as stack:
        r = Resources(nc, stack)
        ctx_rows = r.sbuf("ctx_rows", [P, LOAD, D])
        ctxT_hi = r.sbuf("ctxT_hi", [P, DC, CTX], F32R)
        ctxT_lo = r.sbuf("ctxT_lo", [P, DC, CTX], F32R)
        k_split = r.sbuf("k_split", [P, 2, CTX], F32R)
        k_ones = r.sbuf("k_ones", [P, 2, CTX], F32R)
        v_near = r.sbuf("v_near", [P, HALF, PAIR])
        v_far = r.sbuf("v_far", [P, 2, HALF, PAIR])
        q_twice = r.sbuf("q_twice", [P, 2, SEQ], F32R)
        q_low_max = r.sbuf("q_low_max", [P, 2, SEQ], F32R)
        probs = r.sbuf("probs", [P, 2, 2, KT * SEQ])
        more_rows = [probs[:, n, h, :].rearrange("p (t d) -> p t d", t=LOAD) for n in range(2) for h in range(2)]
        prob_sum = r.sbuf("prob_sum", [P, 2, KT * SEQ])
        xn = prob_sum[:, 0, :].rearrange("p (t d) -> p t d", t=TOK_TILES)
        xnT = r.sbuf("xnT", [P, DC, BATCH * SEQ])
        stats = r.sbuf("stats", [P, TOK_TILES, 6])
        moments = r.sbuf("moments", [P, TOK_TILES, 2])
        power = r.sbuf("power", [P, TOK_TILES])
        w_raw = r.sbuf("w_raw", [P, DC, 4 * PAIR])
        w_hi = r.sbuf("w_hi", [P, DC, 3 * PAIR], F32R)
        w_lo = r.sbuf("w_lo", [P, DC, 3 * PAIR], F32R)
        wq_pair = r.sbuf("wq_pair", [P, DC, 2 * DH])
        wo_pair = r.sbuf("wo_pair", [P, D])
        step_max = r.sbuf("step_max", [P, QT, 2, STEPS])
        row_max = r.sbuf("row_max", [P, QT, 2])
        neg_max = r.sbuf("neg_max", [P, QT, P])
        k_staged_b = [prob_sum[DH:P, B, n * CHUNK:(n + 1) * CHUNK] for n in range(2)]
        recip = prob_sum[:, A, 2 * SEQ:3 * SEQ]
        outT = r.sbuf("outT", [P, SEQ])
        ones = r.sbuf("ones", [P, DH])

        scores = [r.psum("scores_a", [P, 2, CHUNK]), r.psum("scores_b", [P, 2, CHUNK])]
        k_ps = [r.psum("k_ps0", [P, CHUNK]), r.psum("k_ps1", [P, CHUNK])]
        v_ps = r.psum("v_ps", [P, CHUNK])
        out_ps = r.psum("out_ps", [P, CHUNK])
        flat_scores = [s[:, :, :].rearrange("p a b -> p (a b)") for s in scores]

        x_loaded = r.sem("x_loaded")
        SLOTS = 1 + len(more_rows)
        ctx_loaded = [r.sem(f"ctx_loaded{slot}") for slot in range(SLOTS)]
        w_loaded = r.sem("w_loaded")
        wo_loaded = r.sem("wo_loaded")
        ones_a = r.sem("ones_a")
        consts_ready = r.sem("consts_ready")
        norm_chain = r.sem("norm_chain")
        inverse_std = r.sem("inverse_std")
        xT_made = r.sem("xT_made")
        xT_copied = r.sem("xT_copied")
        ctxT_made = r.sem("ctxT_made")
        ctx_high = r.sem("ctx_high")
        ctx_low = r.sem("ctx_low")
        w_high = r.sem("w_high")
        w_low = r.sem("w_low")
        wq_copied = r.sem("wq_copied")
        q_made = r.sem("q_made")
        q_high = r.sem("q_high")
        q_low = r.sem("q_low")
        k_made = r.sem("k_made")
        k_high = r.sem("k_high")
        k_staged = r.sem("k_staged")
        k_low = [r.sem("k_low_a"), r.sem("k_low_b")]
        k_copied = r.sem("k_copied")
        v_made = r.sem("v_made")
        v_copied = r.sem("v_copied")
        pre_made = r.sem("pre_made")
        max_done = r.sem("max_done")
        max_chain = r.sem("max_chain")
        maxT_made = r.sem("maxT_made")
        max_ready = r.sem("max_ready")
        scores_made = r.sem("scores_made")
        exp_done = r.sem("exp_done")
        sum_done = r.sem("sum_done")
        fold_done = r.sem("fold_done")
        pv_done = r.sem("pv_done")
        den_made = r.sem("den_made")
        recip_done = r.sem("recip_done")
        outT_ready = r.sem("outT_ready")
        y_made = r.sem("y_made")
        y_added = r.sem("y_added")

        def v_before(b, i):
            return b * (PAIRS + 1) * STEPS + (0 if is_first(i) else (i + 1) * STEPS)

        def v_pieces(b, i, parity, j):
            for_next = not (isinstance(i, int) and i == PAIRS - 1)
            if is_first(i):
                return [(2 * j, parity, for_next), (2 * j + 1, 1 - parity, False)]
            return [(j, parity, for_next)]

        def v_bank(m):
            return (out_ps, v_ps)[m % 2]

        def slot_of(n):
            slots = [m % SLOTS if m < LOADS else 0 for m in range(n + 1)]
            return slots[n], slots[:n].count(slots[n])

        def rows_of(n):
            slot = slot_of(n)[0]
            return ctx_rows[:, :, :] if slot == 0 else more_rows[slot - 1]

        def load_before(n):
            return max(m for m in range(n) if slot_of(m)[0] == slot_of(n)[0])

        def pairs_of_batch(eng, b, body):
            body(b * PAIRS, b, 0, 0)
            with eng.Fori(0, PAIRS // 2 - 1) as k:
                for parity in (1, 0):
                    i = k * 2 + (2 - parity)
                    body(b * PAIRS + i, b, i, parity)
            body((b + 1) * PAIRS - 1, b, PAIRS - 1, 1)

        def context_banks(n):
            return [k_ps[c][:, :] if n >= LOADS else scores[n % 2][:, c, :] for c in range(DC)]

        def context_high(act, n):
            act.wait_ge(ctxT_made, n + 1)
            for c, bank in enumerate(context_banks(n)):
                act.activation(ctxT_hi[:, c, n % LOADS * CHUNK:(n % LOADS + 1) * CHUNK], bank, ACT.Copy
                               ).then_inc(ctx_high, 1)

        def context_low(dve, n):
            keys = slice(n % LOADS * CHUNK, (n % LOADS + 1) * CHUNK)
            for c, bank in enumerate(context_banks(n)):
                dve.wait_ge(ctx_high, DC * n + c + 1)
                dve.tensor_tensor(ctxT_lo[:, c, keys], bank, ctxT_hi[:, c, keys].bitcast(F32), ALU.subtract
                                  ).then_inc(ctx_low, 1)

        def next_group(b, i, j):
            last_pair = isinstance(i, int) and i == PAIRS - 1 and b < BATCH - 1
            return (b + 1) * LOADS + j - 1 if last_pair and j > 0 else None

        def is_first(it):
            return isinstance(it, int) and it == 0

        def last_batch(b, i):
            return b - 1 if is_first(i) else b

        x_tiles = x.rearrange("b (t p) d -> p (b t) d", p=P)
        ctx_tiles = ctx_in.rearrange("b (p t) d -> b p t d", p=P)
        block = stack.enter_context(nc.Block())

        @block.sync
        def _(sp):
            def load_weights(i):
                widths = (PAIR, PAIR, PAIR if isinstance(i, int) and i == PAIRS - 1 else 2 * PAIR)
                for n, (w, width) in enumerate(zip((w_q, w_k, w_v), widths)):
                    sp.dma_start(w_raw[:, :, n * PAIR:n * PAIR + width],
                                 w[:, bass.ds(i * PAIR, width)].rearrange("(c p) n -> p c n", p=P)
                                 ).then_inc(w_loaded, 16)

            sp.dma_start(x_res[:, :, :], x_tiles).then_inc(x_loaded, 16)
            for b in range(BATCH):
                for n in range(b * LOADS, (b + 1) * LOADS):
                    slot, before = slot_of(n)
                    if before > 0:
                        sp.wait_ge(ctxT_made, load_before(n) + 1)
                    tiles = slice(n % LOADS * LOAD, (n % LOADS + 1) * LOAD)
                    sp.dma_start(rows_of(n), ctx_tiles[b, :, tiles, :]).then_inc(ctx_loaded[slot], 16)
                    if n == SLOTS - 1:
                        load_weights(0)

                def body(it, b, i, parity):
                    wait_past(sp, w_low, it)
                    wait_past(sp, wq_copied, it)
                    if not is_first(it):
                        load_weights(i)
                    wait_past(sp, y_made, it)
                    sp.dma_start(wo_pair[:, :], w_o[bass.ds(i * P, P), :]).then_inc(wo_loaded, 16)
                pairs_of_batch(sp, b, body)

        @block.gpsimd
        def _(pool):
            pool.memset(neg_max[:, :, :], 0.0).then_inc(consts_ready, 1)
            pool.memset(ones[:, :], 1.0).then_inc(consts_ready, 1)
            pool.wait_ge(consts_ready, 2)
            pool.memset(k_ones[DH:P, A, :].bitcast(F32), 0.0).then_inc(consts_ready, 1)
            pool.wait_ge(consts_ready, 3)
            invert_std(pool, moments, power, norm_chain, inverse_std)
            pool.wait_ge(inverse_std, 3)
            pool.memset(k_ones[0:DH, B, :].bitcast(F32), 0.0).then_inc(consts_ready, 1)
            pool.wait_ge(consts_ready, 4)
            pool.memset(k_ones[0:1, B, :].bitcast(F32), 1.0).then_inc(consts_ready, 1)

            def body(it, b, i, parity):
                pool.wait_ge(w_high, it + 1)
                pool.tensor_tensor(w_lo[:, :, :], w_raw[:, :, PAIR:], w_hi[:, :, :].bitcast(F32),
                                   ALU.subtract).then_inc(w_low, 1)
                pool.wait_ge(w_low, it + 1)
                for j in range(STEPS):
                    keys = slice(j * CHUNK, (j + 1) * CHUNK)
                    pool.wait_ge(k_staged, STEPS * it + j + 1)
                    pool.wait_ge(k_high, 2 * (STEPS * it + j) + 2)
                    pool.tensor_tensor(k_split[0:DH, B, keys], k_staged_b[j % 2], k_split[DH:P, B, keys].bitcast(F32),
                                       ALU.subtract).then_inc(k_low[B], 1)
                pool.wait_ge(k_low[B], STEPS * (it + 1))
            pool.wait_ge(consts_ready, 5)
            for b in range(BATCH):
                pairs_of_batch(pool, b, body)

        @block.scalar
        def _(act):
            act.wait_ge(consts_ready, 3)
            act.activation(k_ones[DH:DH + 1, A, :], ones[DH:DH + 1, 0:1].to_broadcast([1, CTX]), ACT.Copy
                           ).then_inc(ones_a, 1)

            def split_weights(it, b, i):
                act.wait_ge(w_loaded, 48 * it + 48)
                wait_past(act, v_made, v_before(b, i))
                act.activation(w_hi[:, :, :], w_raw[:, :, PAIR:], ACT.Copy).then_inc(w_high, 1)
                act.activation(wq_pair[:, :, :], w_raw[:, :, 0:PAIR], ACT.Copy).then_inc(wq_copied, 1)

            def copy_v(b, i, parity, j):
                for m, half, for_next in v_pieces(b, i, parity, j):
                    act.wait_ge(v_made, v_before(b, i) + m + 1)
                    src = v_bank(m)[:, :].rearrange("p (t d) -> p t d", t=V_TILES)
                    tiles = slice(j * V_TILES, (j + 1) * V_TILES)
                    if for_next:
                        act.activation(v_far[:, parity, tiles, :], src[:, :, PAIR:2 * PAIR], ACT.Copy)
                    own = v_near[:, tiles, :] if half == parity else v_far[:, half, tiles, :]
                    act.activation(own, src[:, :, 0:PAIR], ACT.Copy).then_inc(v_copied, 1)

            def body(it, b, i, parity):
                if not is_first(it):
                    split_weights(it, b, i)
                act.wait_ge(q_made, it + 1)
                for h in (A, B):
                    for half in (0, DH):
                        act.activation(q_twice[half:half + DH, h, :], v_ps[h * DH:(h + 1) * DH, 0:SEQ],
                                       ACT.Copy).then_inc(q_high, 1)
                for j in range(STEPS + 1):
                    if j < STEPS:
                        keys = slice(j * CHUNK, (j + 1) * CHUNK)
                        act.wait_ge(k_made, STEPS * it + j + 1)
                        ps = k_ps[j % 2]
                        act.activation(k_split[0:DH, A, keys], ps[0:DH, :], ACT.Copy).then_inc(k_high, 1)
                        act.activation(k_split[DH:P, B, keys], ps[DH:P, :], ACT.Copy).then_inc(k_high, 1)
                        if j >= 2:
                            act.wait_ge(k_low[B], STEPS * it + j - 1)
                        act.activation(k_staged_b[j % 2], ps[DH:P, :], ACT.Copy).then_inc(k_staged, 1)
                    if j > 0:
                        keys = slice((j - 1) * CHUNK, j * CHUNK)
                        act.wait_ge(k_high, 2 * (STEPS * it + j))
                        act.activation(k_ones[0:DH, A, keys], k_split[0:DH, A, keys].bitcast(F32), ACT.Copy
                                       ).then_inc(k_copied, 1)
                        act.activation(k_ones[DH:P, B, keys], k_split[DH:P, B, keys].bitcast(F32), ACT.Copy
                                       ).then_inc(k_copied, 1)
                    if j > 3:
                        copy_v(b, i, parity, j - 4)
                copy_v(b, i, parity, STEPS - 3)
                copy_v(b, i, parity, STEPS - 2)
                act.wait_ge(maxT_made, it + 1)
                act.activation(q_low_max[DH:P, A, :], k_ps[0][DH:P, 0:SEQ], ACT.Copy).then_inc(max_ready, 1)
                for j in range(STEPS):
                    for h in (A, B):
                        n = 2 * (STEPS * it + j) + h
                        act.wait_ge(scores_made, n + 1)
                        if j >= 2 or not is_first(it):
                            act.wait_ge(sum_done, n - 3)
                            act.wait_ge(pv_done, STEPS * it + j - 1)
                        act.activation(probs[:, j % 2, h, :], flat_scores[h], ACT.Exp, scale=SCALE
                                       ).then_inc(exp_done, 1)
                    if j == 0:
                        copy_v(b, i, parity, STEPS - 1)
                    if next_group(b, i, j) is not None:
                        context_high(act, next_group(b, i, j))
                if next_group(b, i, STEPS) is not None:
                    context_high(act, next_group(b, i, STEPS))
            for b in range(BATCH):
                if b == 0:
                    for n in range(LOADS):
                        context_high(act, n)
                        if n == LOADS - 3:
                            split_weights(0, 0, 0)
                    act.wait_ge(consts_ready, 5)
                pairs_of_batch(act, b, body)

        @block.vector
        def _(dve):
            dve.wait_ge(x_loaded, 16)
            normalise_rows(dve, x_res, xn, stats, moments, norm_chain, inverse_std)

            def divide(before):
                dve.wait_ge(den_made, before + 1)
                dve.reciprocal(recip, out_ps[:, 0:SEQ]).then_inc(recip_done, 1)
                dve.wait_ge(recip_done, before + 1)
                wait_past(dve, y_made, before)
                dve.tensor_tensor(outT[:, :], out_ps[:, SEQ:2 * SEQ], recip, ALU.mult).then_inc(outT_ready, 1)

            def add_output(before, b):
                dve.wait_ge(y_made, before + 1)
                dst = x_res[:, b * QT:(b + 1) * QT, :]
                dve.tensor_tensor(dst, dst, out_ps[:, :].rearrange("p (t d) -> p t d", t=QT), ALU.add
                                  ).then_inc(y_added, 1)

            def body(it, b, i, parity):
                def low_queries():
                    dve.wait_ge(q_high, 4 * it + 4)
                    dve.tensor_tensor(q_low_max[0:DH, A, :], v_ps[0:DH, 0:SEQ], q_twice[0:DH, A, :].bitcast(F32),
                                      ALU.subtract).then_inc(q_low, 1)
                    dve.tensor_tensor(q_low_max[DH:P, B, :], v_ps[DH:P, 0:SEQ], q_twice[DH:P, B, :].bitcast(F32),
                                      ALU.subtract).then_inc(q_low, 1)
                if not is_first(it):
                    divide(it - 1)
                for j in range(STEPS + 1):
                    if j < STEPS:
                        keys = slice(j * CHUNK, (j + 1) * CHUNK)
                        n = STEPS * it + j
                        ps = k_ps[j % 2]
                        dve.wait_ge(k_high, 2 * n + 1)
                        dve.tensor_tensor(k_split[DH:P, A, keys], ps[0:DH, :], k_split[0:DH, A, keys].bitcast(F32),
                                          ALU.subtract).then_inc(k_low[A], 1)
                    if j == 1 and not is_first(it):
                        add_output(it - 1, last_batch(b, i))
                    if j > 0:
                        for h in (A, B):
                            dve.wait_ge(pre_made, 2 * (STEPS * it + j - 1) + h + 1)
                            dve.tensor_reduce(step_max[:, :, 1 - h, j - 1], scores[h][:, :, :], X, ALU.max
                                              ).then_inc(max_done, 1)
                    if j == 2:
                        low_queries()
                dve.wait_ge(max_done, 2 * STEPS * (it + 1))
                dve.tensor_reduce(row_max[:, :, :], step_max[:, :, :, :], X, ALU.max).then_inc(max_chain, 1)
                dve.wait_ge(max_chain, 2 * it + 1)
                dve.tensor_scalar(neg_max[:, :, 0:P:DH], row_max[:, :, :], -1.0, None, ALU.mult
                                  ).then_inc(max_chain, 1)
                dve.wait_ge(maxT_made, it + 1)
                dve.tensor_copy(q_low_max[0:DH, B, :], k_ps[0][0:DH, 0:SEQ]).then_inc(max_ready, 1)
                for j in range(STEPS):
                    for h in (A, B):
                        n = 2 * (STEPS * it + j) + h
                        dve.wait_ge(exp_done, n + 1)
                        if j == 0:
                            dve.tensor_copy(prob_sum[:, h, :], probs[:, 0, h, :]).then_inc(sum_done, 1)
                        else:
                            dve.wait_ge(sum_done, n - 1)
                            dve.tensor_tensor(prob_sum[:, h, :], prob_sum[:, h, :], probs[:, j % 2, h, :], ALU.add
                                              ).then_inc(sum_done, 1)
                    if next_group(b, i, j) is not None:
                        context_low(dve, next_group(b, i, j))
                dve.wait_ge(sum_done, 2 * STEPS * (it + 1))
                half = KT * SEQ // 2
                dve.tensor_tensor(prob_sum[:, :, 0:half], prob_sum[:, :, 0:half], prob_sum[:, :, half:2 * half],
                                  ALU.add).then_inc(fold_done, 1)
                dve.wait_ge(fold_done, 2 * it + 1)
                dve.tensor_tensor(prob_sum[:, :, 0:SEQ], prob_sum[:, :, 0:SEQ], prob_sum[:, :, SEQ:2 * SEQ],
                                  ALU.add).then_inc(fold_done, 1)
                if next_group(b, i, STEPS) is not None:
                    context_low(dve, next_group(b, i, STEPS))
            for b in range(BATCH):
                for n in range(LOADS if b == 0 else 0):
                    context_low(dve, n)
                    if n == 3:
                        for c in range(DC):
                            dve.wait_ge(xT_made, c + 1)
                            dve.tensor_copy(xnT[:, c, :], k_ps[c][:, :]).then_inc(xT_copied, 1)
                pairs_of_batch(dve, b, body)
            divide(BATCH * PAIRS - 1)
            add_output(BATCH * PAIRS - 1, BATCH - 1)

        @block.tensor
        def _(pe):
            mm = pe.matmul

            def transpose_context(n):
                slot, before = slot_of(n)
                pe.wait_ge(ctx_loaded[slot], 16 * (before + 1))
                if n >= LOADS:
                    pe.wait_ge(ctx_low, DC * n)
                elif n >= 2:
                    pe.wait_ge(ctx_low, DC * (n - 1))
                for t in range(LOAD):
                    for c in range(DC):
                        last = pe.transpose(context_banks(n)[c][:, t * P:(t + 1) * P],
                                            rows_of(n)[:, t, c * P:(c + 1) * P], ident[:, :])
                last.then_inc(ctxT_made, 1)

            def transpose_x():
                pe.wait_ge(norm_chain, NORMALISED)
                for c in range(DC):
                    for t in range(TOK_TILES):
                        last = pe.transpose(k_ps[c][:, t * P:(t + 1) * P], xn[:, t, c * P:(c + 1) * P], ident[:, :])
                    last.then_inc(xT_made, 1)

            def project_q(it, b):
                pe.wait_ge(wq_copied, it + 1)
                for c in range(DC):
                    last = mm(v_ps[:, 0:SEQ], wq_pair[:, c, :], xnT[:, c, b * SEQ:(b + 1) * SEQ],
                              start=(c == 0), stop=(c == DC - 1))
                last.then_inc(q_made, 1)

            def passes_of():
                return [(w, s, c) for w, s in ((w_hi, ctxT_lo), (w_lo, ctxT_hi), (w_hi, ctxT_hi)) for c in range(DC)]

            def project_k(it, j):
                passes = passes_of()
                for n, (w, s, c) in enumerate(passes):
                    last = mm(k_ps[j % 2][:, :], w[:, c, 0:PAIR], s[:, c, j * CHUNK:(j + 1) * CHUNK],
                              start=(n == 0), stop=(n == len(passes) - 1))
                last.then_inc(k_made, 1)

            def project_v(it, b, i, parity, j, tiles=None):
                passes = passes_of()
                pieces = v_pieces(b, i, parity, j)
                todo = [(piece, t) for piece in pieces for t in range(V_TILES)]
                if tiles is not None:
                    todo = todo[len(todo) // 2:] if tiles else todo[:len(todo) // 2]
                for (m, half, for_next), t in todo:
                    if t == 0 and m == 0:
                        wait_past(pe, y_added, it)
                    elif t == 0 and m == 1:
                        pe.wait_ge(q_low, 2 * it + 2)
                    elif t == 0:
                        pe.wait_ge(v_copied, v_before(b, i) + m - 1)
                    width = 2 * PAIR if for_next else PAIR
                    tile = half * HALF + j * V_TILES + t
                    for n, (w, s, c) in enumerate(passes):
                        last = mm(v_bank(m)[:, t * 2 * PAIR:t * 2 * PAIR + width], s[:, c, tile * P:(tile + 1) * P],
                                  w[:, c, PAIR:PAIR + width], start=(n == 0), stop=(n == len(passes) - 1))
                    if t == V_TILES - 1:
                        last.then_inc(v_made, 1)

            def scores_for_max(it, j):
                keys = slice(j * CHUNK, (j + 1) * CHUNK)
                for h in (A, B):
                    pe.wait_ge(k_low[h], STEPS * it + j + 1)
                    if j > 0:
                        pe.wait_ge(max_done, 2 * (STEPS * it + j - 1) + h + 1)
                    else:
                        wait_past(pe, exp_done, 2 * STEPS * it)
                    for qt in range(QT):
                        last = mm(scores[h][:, qt, :], q_twice[:, h, qt * P:(qt + 1) * P], k_split[:, h, keys],
                                  start=True, stop=True)
                    last.then_inc(pre_made, 1)

            def scores_by_keys(it, j, h):
                if j > 0:
                    pe.wait_ge(exp_done, 2 * (STEPS * it + j - 1) + h + 1)
                for t in range(KT):
                    keys = slice((j * KT + t) * P, (j * KT + t + 1) * P)
                    out = flat_scores[h][:, t * SEQ:(t + 1) * SEQ]
                    mm(out, k_split[:, h, keys], q_twice[:, h, :], start=True, stop=False)
                    last = mm(out, k_ones[:, h, keys], q_low_max[:, h, :], start=False, stop=True)
                last.then_inc(scores_made, 1)

            def product_with_v(it, b, i, parity, j):
                if j == 0:
                    pe.wait_ge(v_copied, v_before(b, i) + len(v_pieces(b, i, parity, 0)) * STEPS)
                pe.wait_ge(exp_done, 2 * (STEPS * it + j) + 2)
                for t in range(KT):
                    half, tile = (j * KT + t) // HALF, (j * KT + t) % HALF
                    v = v_near[:, tile, :] if half == parity else v_far[:, 1 - parity, tile, :]
                    for h in (A, B):
                        last = mm(out_ps[h * DH:(h + 1) * DH, SEQ:2 * SEQ], v[:, h * DH:(h + 1) * DH],
                                  probs[:, j % 2, h, t * SEQ:(t + 1) * SEQ],
                                  start=(j == 0 and t == 0), stop=(j == STEPS - 1 and t == KT - 1))
                last.then_inc(pv_done, 1)

            def sum_over_keys(it):
                pe.wait_ge(fold_done, 2 * it + 2)
                for h in (A, B):
                    last = mm(out_ps[h * DH:(h + 1) * DH, 0:SEQ], ones[:, :], prob_sum[:, h, 0:SEQ],
                              start=True, stop=True)
                last.then_inc(den_made, 1)

            def project_output(it):
                pe.wait_ge(outT_ready, it + 1)
                pe.wait_ge(wo_loaded, 16 * (it + 1))
                for qt in range(QT):
                    last = mm(out_ps[:, qt * D:(qt + 1) * D], outT[:, qt * P:(qt + 1) * P], wo_pair[:, :],
                              start=True, stop=True)
                last.then_inc(y_made, 1)

            def body(it, b, i, parity):
                project_q(it, b)
                if not is_first(it):
                    sum_over_keys(it - 1)
                pe.wait_ge(w_low, it + 1)
                for j in range(STEPS):
                    if j >= 2:
                        pe.wait_ge(k_low[A], STEPS * it + j - 1)
                        pe.wait_ge(k_staged, STEPS * it + j - 1)
                    if is_first(i):
                        pe.wait_ge(ctx_low, DC * (j + 1 if b == 0 else (b + 1) * LOADS))
                    project_k(it, j)
                    if j == 1 and not is_first(it):
                        project_output(it - 1)
                    if j == 2 and is_first(i):
                        pe.wait_ge(ctx_low, DC * (b + 1) * LOADS)
                    if j > 1:
                        scores_for_max(it, j - 2)
                    if j > 3:
                        project_v(it, b, i, parity, j - 4)
                scores_for_max(it, STEPS - 2)
                project_v(it, b, i, parity, STEPS - 4)
                scores_for_max(it, STEPS - 1)
                project_v(it, b, i, parity, STEPS - 3)
                project_v(it, b, i, parity, STEPS - 2)
                pe.wait_ge(max_chain, 2 * it + 2)
                for qt in range(QT):
                    last = pe.transpose(k_ps[0][:, qt * P:(qt + 1) * P], neg_max[:, qt, :], ident[:, :])
                last.then_inc(maxT_made, 1)
                project_v(it, b, i, parity, STEPS - 1, tiles=0)
                pe.wait_ge(q_low, 2 * it + 2)
                pe.wait_ge(max_ready, 2 * it + 2)
                pe.wait_ge(k_copied, 2 * STEPS * (it + 1))
                for j in range(STEPS):
                    for h in (A, B):
                        scores_by_keys(it, j, h)
                    if j == 0:
                        project_v(it, b, i, parity, STEPS - 1, tiles=1)
                    if j > 0:
                        product_with_v(it, b, i, parity, j - 1)
                    if next_group(b, i, j) is not None:
                        transpose_context(next_group(b, i, j))
                product_with_v(it, b, i, parity, STEPS - 1)
                if next_group(b, i, STEPS) is not None:
                    transpose_context(next_group(b, i, STEPS))

            for b in range(BATCH):
                for n in range(LOADS if b == 0 else 0):
                    transpose_context(n)
                    if n == 2:
                        transpose_x()
                if b == 0:
                    pe.wait_ge(xT_copied, DC)
                    pe.wait_ge(consts_ready, 5)
                    pe.wait_ge(ones_a, 1)
                pairs_of_batch(pe, b, body)
            sum_over_keys(BATCH * PAIRS - 1)
            project_output(BATCH * PAIRS - 1)



MEM = 16
KEYS = MEM + SEQ
ROWS = P // HEADS
GPS = 2
STEP_ROWS = GPS * ROWS
SA_STEPS = SEQ // STEP_ROWS
RING = 3
LOW = -3.0e38

FF = 768
FC = FF // P
BLOCK = 32
NB = FF * D // P // BLOCK
W_MAX = 2.0 ** 3 - 1.0
ROUND = 1.5 * 2.0 ** 23
TINY = 1e-12
WT_BANKS = FF * D // P // 512
GATE, UP, DOWN = range(3)
W_OPS = 9
W_PARTS = 6


def load_ffn_weight(sp, dst, w, loaded):
    sp.dma_start(dst.rearrange("p (t i) -> p t i", t=w.shape[0] // P),
                 w.rearrange("(t p) i -> p t i", p=P)).then_inc(loaded, 16)


def quantise_weight(dve, part, w, scales, chain, done):
    blocks = [P, NB, BLOCK]
    w = w.rearrange("p (b k) -> p b k", k=BLOCK)
    top, bottom, scale, inverse = (scales[:, n, :] for n in range(4))
    if part == 0:
        dve.tensor_reduce(top, w, X, ALU.max).then_inc(chain, 1)
    elif part == 1:
        dve.tensor_reduce(bottom, w, X, ALU.min).then_inc(chain, 1)
    elif part == 2:
        dve.wait_ge(chain, done + 2)
        dve.scalar_tensor_tensor(top, bottom, -1.0, top, ALU.mult, ALU.max).then_inc(chain, 1)
        dve.wait_ge(chain, done + 3)
        dve.tensor_scalar(scale, top, 1.0 / W_MAX, TINY, ALU.mult, ALU.max).then_inc(chain, 1)
        dve.wait_ge(chain, done + 4)
        dve.reciprocal(inverse, scale).then_inc(chain, 1)
    elif part == 3:
        dve.wait_ge(chain, done + 5)
        dve.tensor_tensor(w, w, inverse.unsqueeze(2).to_broadcast(blocks), ALU.mult).then_inc(chain, 1)
    elif part == 4:
        dve.wait_ge(chain, done + 6)
        dve.tensor_scalar(w, w, ROUND, ROUND, ALU.add, ALU.subtract).then_inc(chain, 1)
        dve.wait_ge(chain, done + 7)
        dve.tensor_scalar(w, w, W_MAX, -W_MAX - 1.0, ALU.min, ALU.max).then_inc(chain, 1)
    else:
        dve.wait_ge(chain, done + 8)
        dve.tensor_tensor(w, w, scale.unsqueeze(2).to_broadcast(blocks), ALU.mult).then_inc(chain, 1)


def transpose_weight(pe, w, row_tiles, k, out, ident):
    width = FF * D // P // row_tiles
    c, t = k // row_tiles, k % row_tiles
    return pe.transpose(out, w[:, t * width + c * P:t * width + (c + 1) * P], ident[:, :])


def self_attention(nc, w_q, w_kv, w_o, pre_proj, post_proj, mem_k, mem_v, w_gate, w_up, hidden_wT,
                   x_res, ident):
    with ExitStack() as stack:
        r = Resources(nc, stack)
        shared = r.sbuf("shared", [P, 3 * HEADS * P])
        wq_sb = shared[:, 0:DC * INNER].rearrange("p (c n) -> p c n", c=DC)
        wkv_sb = shared[:, DC * INNER:3 * DC * INNER].rearrange("p (c n) -> p c n", c=DC)
        mixed = [shared[:, 0:HEADS * SEQ].rearrange("p (k i) -> p k i", k=HEADS),
                 shared[:, HEADS * SEQ:].rearrange("p (k i) -> p k i", k=HEADS)]
        wide = r.sbuf("wide", [P, HEADS * SEQ])
        hidden_w = [wide[:, n * FF * D // P:(n + 1) * FF * D // P] for n in (GATE, UP)]
        mixed_mem = wide[0:MEM, :].rearrange("p (k i) -> p k i", k=HEADS)
        w_scales = r.sbuf("w_scales", [P, 4, NB])
        wo_sb = r.sbuf("wo_sb", [P, PAIRS, D])
        normed = r.sbuf("normed", [P, PAIRS * SEQ])
        xn = normed[:, 0:TOK_TILES * D].rearrange("p (t d) -> p t d", t=TOK_TILES)
        xnT = normed[:, TOK_TILES * D:].rearrange("p (c n) -> p c n", c=DC)
        outT = normed[:, :].rearrange("p (k i) -> p k i", k=PAIRS)
        stats = r.sbuf("stats2", [P, TOK_TILES, 6])
        moments = r.sbuf("moments2", [P, TOK_TILES, 2])
        power = r.sbuf("power2", [P, TOK_TILES])
        q_padded = r.sbuf("q_padded", [P, HEADS, BATCH * SEQ])
        kT = r.sbuf("kT", [P, PAIRS, BATCH, KEYS])
        v_sb = r.sbuf("v_sb", [P, TOK_TILES, INNER])
        memk_sb = r.sbuf("memk_sb", [P, 2, DH])
        memv_sb = r.sbuf("memv_sb", [MEM, HEADS, DH])
        dots_sb = r.sbuf("dots_sb", [P, HEADS, KEYS])
        grouped = r.sbuf("grouped", [P, 2, P // ROWS, KEYS])
        expd = r.sbuf("expd", [P, RING, GPS, KEYS])
        proj_sb = r.sbuf("proj_sb", [HEADS, 2, HEADS])
        spread = r.sbuf("spread", [HEADS, P])
        same_row = r.sbuf("same_row", [P, ROWS])
        rep = r.sbuf("rep", [P, 2, HEADS])
        kron = r.sbuf("kron", [P, 2, HEADS, ROWS])
        kron_scaled = r.sbuf("kron_scaled", [P, RING, GPS, P])
        row_of = r.sbuf("row_of", [P, 1])
        columns = r.sbuf("columns", [P, GPS, STEP_ROWS])
        weighted = r.sbuf("weighted", [P, ROWS])
        causal = r.sbuf("causal", [P, GPS, STEP_ROWS])
        top = r.sbuf("top", [P, RING, GPS])
        neg_top = r.sbuf("neg_top", [P, RING, GPS])
        total = r.sbuf("total", [P, RING, GPS])
        inv_total = r.sbuf("inv_total", [P, RING, GPS])

        bank = [r.psum(f"bank{n}", [P, 2, 512]) for n in range(4)]

        wq_in = r.sem("wq_in")
        wkv_in = r.sem("wkv_in")
        wo_in = r.sem("wo_in")
        hidden_in = r.sem("hidden_in")
        hidden_chain = r.sem("hidden_chain")
        hidden_made = r.sem("hidden_made2")
        hidden_copied = r.sem("hidden_copied2")
        small_in = r.sem("small_in")
        norm_chain = r.sem("norm_chain2")
        inverse_std = r.sem("inverse_std2")
        xT_made = r.sem("xT_made2")
        xT_copied = r.sem("xT_copied2")
        consts = r.sem("consts")
        zeroed = r.sem("zeroed")
        kron_made = r.sem("kron_made")
        kron_chain = r.sem("kron_chain")
        memk_made = r.sem("memk_made")
        memk_copied = r.sem("memk_copied")
        proj_made = r.sem("proj_made")
        proj_copied = [r.sem("proj_by_act"), r.sem("proj_by_dve")]
        dots_made = r.sem("dots_made")
        dots_copied = [r.sem("dots_by_act"), r.sem("dots_by_dve")]
        regrouped = [r.sem(f"regrouped{pair}") for pair in range(PAIRS)]
        mix_made = r.sem("mix_made")
        masked = r.sem("masked")
        top_done = r.sem("top_done")
        neg_done = r.sem("neg_done")
        exp_done = r.sem("exp_done2")
        tail_zero = r.sem("tail_zero")
        inv_done = r.sem("inv_done")
        kron_done = r.sem("kron_done")
        post_made = r.sem("post_made")
        mixed_by_act = r.sem("mixed_by_act")
        mixed_by_dve = r.sem("mixed_by_dve")
        out_made = r.sem("out_made")
        out_copied = r.sem("out_copied")
        y_made = r.sem("y_made2")
        y_added = r.sem("y_added2")

        Q, K, V = range(3)
        projections = [(kind, n) for n in range(PAIRS) for kind in (Q, K)] + [(V, n) for n in range(2 * TOK_TILES)]
        NPROJ = len(projections)
        NQK = 2 * PAIRS
        NV = TOK_TILES

        def mix_places(n, at, end):
            ring = [bank[2][:, 0, :], bank[2][:, 1, :], bank[3][:, 0, :]][n % RING]
            if end <= 512 // GPS:
                return [ring.rearrange("p (g c) -> p g c", g=GPS)[:, :, at:end]]
            return [ring[:, at:end].unsqueeze(1), bank[3][:, 1, at:end].unsqueeze(1)]

        def mix_group(n, g, keys):
            places = mix_places(n, 0, keys)
            return places[0][:, g, :] if len(places) == 1 else places[g][:, 0, :]

        def places_until(n):
            return n + n // SA_STEPS

        def projection_bank(n):
            return bank[n % 4 if n < NQK else 2 + n % 2][:, 0, :]

        def hidden_bank(n):
            return bank[2 + n // 2 % 2][:, n % 2, :]

        def dot_keys(t):
            return MEM + (t + 1) * P

        def step_keys(s):
            return MEM + (s + 1) * STEP_ROWS

        block = stack.enter_context(nc.Block())

        @block.sync
        def _(sp):
            sp.dma_start(wq_sb, w_q.rearrange("(c p) n -> p c n", p=P)).then_inc(wq_in, 16)
            sp.dma_start(wkv_sb, w_kv.rearrange("(c p) n -> p c n", p=P)).then_inc(wkv_in, 16)
            sp.dma_start(proj_sb[:, 0, :], pre_proj).then_inc(small_in, 16)
            sp.dma_start(proj_sb[:, 1, :], post_proj).then_inc(small_in, 16)
            sp.dma_start(memv_sb[:, :, :], mem_v.rearrange("h m d -> m h d")).then_inc(small_in, 16)
            for pair in range(PAIRS):
                sp.dma_start(memk_sb[pair * MEM:(pair + 1) * MEM, :, :],
                             mem_k[2 * pair:2 * pair + 2].rearrange("h m d -> m h d")).then_inc(small_in, 16)
            for n, w in ((GATE, w_gate), (UP, w_up)):
                load_ffn_weight(sp, hidden_w[n], w, hidden_in)
            sp.dma_start(wo_sb[:, :, :], w_o.rearrange("(c p) n -> p c n", p=P)).then_inc(wo_in, 16)
            for b in range(BATCH):
                for t in range(QT):
                    if b > 0:
                        sp.wait_ge(mix_made, (b - 1) * SA_STEPS + (t + 1) * SA_STEPS // QT)
                    for h in range(HEADS):
                        n = (b * QT + t) * PAIRS + h // 2
                        sp.wait_ge(dots_copied[n % 2], n // 2 + 1)
                        keys = dot_keys(t)
                        sp.dma_start(grouped[h * ROWS:(h + 1) * ROWS, t, :, 0:keys],
                                     dots_sb[:, h, 0:keys]).then_inc(regrouped[h // 2], 16)

        @block.gpsimd
        def _(pool):
            pool.memset(spread[:, :], 1.0).then_inc(consts, 1)
            for n in range(GPS):
                for c in range(STEP_ROWS):
                    pool.memset(columns[:, n, c:c + 1], float(c - n * ROWS)).then_inc(consts, 1)
            pool.wait_ge(consts, 1 + GPS * STEP_ROWS)
            pool.affine_select(out=spread[:, :], in_=spread[:, :], compare_op=ALU.is_ge, fill=0.0, base=0,
                               pattern=[[1, P]], channel_multiplier=-ROWS).then_inc(consts, 1)
            pool.wait_ge(consts, 2 + GPS * STEP_ROWS)
            pool.affine_select(out=spread[:, :], in_=spread[:, :], compare_op=ALU.is_ge, fill=0.0, base=ROWS - 1,
                               pattern=[[-1, P]], channel_multiplier=ROWS).then_inc(consts, 1)
            invert_std(pool, moments, power, norm_chain, inverse_std)
            pool.wait_ge(inverse_std, 3)
            pool.memset(q_padded[DH:P, 0:HEADS:2, :], 0.0).then_inc(zeroed, 1)
            pool.wait_ge(zeroed, 1)
            pool.memset(q_padded[0:DH, 1:HEADS:2, :], 0.0).then_inc(zeroed, 1)
            pool.wait_ge(zeroed, 2)
            for b in range(BATCH):
                for s in range(RING):
                    n = b * SA_STEPS + s
                    if n >= RING:
                        pool.wait_ge(post_made, n - RING + 1)
                    pool.memset(expd[:, n % RING, :, step_keys(s):KEYS], 0.0).then_inc(tail_zero, 1)

        def copy_projection(copy, n):
            kind, m = projections[n]
            src = projection_bank(n)
            if kind == Q:
                queries = src.rearrange("p (t g r) -> p t g r", g=P // ROWS, r=ROWS)
                for half in range(2):
                    rows = slice(half * DH, (half + 1) * DH)
                    place = q_padded[rows, 2 * m + half, :].rearrange("p (t r g) -> p t g r", g=P // ROWS, r=ROWS)
                    ins = copy(place, queries[rows])
            elif kind == K:
                ins = copy(kT[:, m, :, MEM:KEYS], src.rearrange("p (b n) -> p b n", b=BATCH))
            else:
                ins = copy(v_sb[:, m // 2, (m % 2) * 512:(m % 2 + 1) * 512], src)
            ins.then_inc(proj_copied[n % 2], 1)

        def copy_dots(eng, scaled_copy, n):
            t = n // PAIRS % QT
            pair = n % PAIRS
            keys = dot_keys(t)
            eng.wait_ge(dots_made, n + 1)
            if n >= PAIRS:
                eng.wait_ge(regrouped[pair], 32 * (n // PAIRS))
            scaled_copy(dots_sb[:, 2 * pair:2 * pair + 2, 0:keys], bank[n % 2][:, :, 0:keys]
                        ).then_inc(dots_copied[n % 2], 1)

        def mixed_place(n, to, skipped=0):
            i = n % SA_STEPS * STEP_ROWS - skipped
            return to[:, :, i:i + STEP_ROWS].rearrange("p k (g r) -> p g k r", g=GPS)

        def mixed_source(n, rows, half, at):
            return bank[n % 2][0:rows, half, at:at + GPS * P].rearrange("p (g k r) -> p g k r", g=GPS, k=HEADS)

        @block.scalar
        def _(act):
            def copy(out, src):
                return act.activation(out, src, ACT.Copy)

            def scaled_copy(out, src):
                return act.activation(out, src, ACT.Copy, scale=SCALE)

            def copy_projections(first, end):
                for n in range(first, end, 2):
                    act.wait_ge(proj_made, n + 1)
                    copy_projection(copy, n)

            def exponentials(n):
                keys = step_keys(n % SA_STEPS)
                act.wait_ge(neg_done, n + 1)
                if n >= RING:
                    act.wait_ge(post_made, n - RING + 1)
                    act.wait_ge(inv_done, n - RING + 1)
                for g in range(GPS):
                    act.activation(expd[:, n % RING, g, 0:keys], mix_group(n, g, keys), ACT.Exp,
                                   bias=neg_top[:, n % RING, g:g + 1], accum_out=total[:, n % RING, g:g + 1]
                                   ).then_inc(exp_done, 1)

            def copy_mixed(n):
                act.wait_ge(post_made, n + 1)
                copy(mixed_place(n, mixed[0]), mixed_source(n, P, 0, 0)).then_inc(mixed_by_act, 1)

            def copy_scores(b, t):
                for n in range((b * QT + t) * PAIRS, (b * QT + t + 1) * PAIRS, 2):
                    copy_dots(act, scaled_copy, n)

            copy_projections(0, NQK)
            for t in range(QT):
                copy_scores(0, t)
                copy_projections(NQK + t * NV, NQK + (t + 1) * NV)
            for n in range(2 * WT_BANKS):
                act.wait_ge(hidden_made, n + 1)
                copy(hidden_wT[:, n // WT_BANKS, n % WT_BANKS * 512:(n % WT_BANKS + 1) * 512], hidden_bank(n)
                     ).then_inc(hidden_copied, 1)
            for b in range(BATCH):
                first = b * SA_STEPS
                for n in range(first, first + SA_STEPS):
                    exponentials(n)
                    if n >= first + 2:
                        copy_mixed(n - 2)
                copy_mixed(first + SA_STEPS - 2)
                copy_mixed(first + SA_STEPS - 1)
                if b < BATCH - 1:
                    for t in range(QT):
                        copy_scores(b + 1, t)
                for n in range(b * PAIRS, (b + 1) * PAIRS):
                    act.wait_ge(out_made, n + 1)
                    copy(outT[:, n % PAIRS, :], bank[2 + n % 2][:, 0, 0:SEQ]).then_inc(out_copied, 1)

        @block.vector
        def _(dve):
            normalise_rows(dve, x_res, xn, stats, moments, norm_chain, inverse_std)
            for c in range(DC):
                dve.wait_ge(xT_made, c + 1)
                dve.tensor_copy(xnT[:, c, :], bank[0][:, c, :]).then_inc(xT_copied, 1)
            dve.tensor_reduce(same_row[:, :], ident[:, :].rearrange("p (h r) -> p r h", r=ROWS), X, ALU.add
                              ).then_inc(kron_chain, 1)
            dve.wait_ge(kron_made, 1)
            dve.tensor_copy(rep[:, :, :].rearrange("p a k -> p (a k)"), bank[3][:, 0, 0:2 * HEADS]
                            ).then_inc(kron_chain, 1)
            dve.wait_ge(memk_made, 1)
            for b in range(BATCH):
                dve.tensor_copy(kT[:, :, b, 0:MEM], bank[3][:, 1, 0:P].rearrange("p (k m) -> p k m", m=MEM)
                                ).then_inc(memk_copied, 1)
            dve.wait_ge(kron_chain, 2)
            for n in range(2):
                dve.tensor_tensor(kron[:, n, :, :], rep[:, n, :].unsqueeze(2).to_broadcast([P, HEADS, ROWS]),
                                  same_row[:, :].unsqueeze(1).to_broadcast([P, HEADS, ROWS]), ALU.mult
                                  ).then_inc(kron_chain, 1)
            dve.wait_ge(consts, 3 + GPS * STEP_ROWS)
            dve.tensor_tensor(weighted[:, :], same_row[:, :], columns[:, 0, 0:ROWS], ALU.mult).then_inc(kron_chain, 1)
            dve.wait_ge(kron_chain, 5)
            dve.tensor_reduce(row_of[:, :], weighted[:, :], X, ALU.add).then_inc(kron_chain, 1)
            dve.wait_ge(kron_chain, 6)
            dve.tensor_scalar(causal[:, :, :], columns[:, :, :], row_of[:, 0:1], LOW, ALU.is_gt, ALU.mult
                              ).then_inc(kron_chain, 1)
            dve.wait_ge(kron_chain, 7)
            dve.wait_ge(hidden_in, 32)

            def copy_projections(first, end):
                for n in range(first + 1, end, 2):
                    dve.wait_ge(proj_made, n + 1)
                    copy_projection(dve.tensor_copy, n)
                    m, part = n // 2 // W_PARTS, n // 2 % W_PARTS
                    if m > 0 and part == 0:
                        dve.wait_ge(hidden_chain, m * W_OPS)
                    quantise_weight(dve, part, hidden_w[m], w_scales, hidden_chain, m * W_OPS)

            def scaled_copy(out, src):
                return dve.tensor_scalar(out, src, SCALE, None, ALU.mult)

            def maximum(n):
                keys = step_keys(n % SA_STEPS)
                dve.wait_ge(mix_made, n + 1)
                lasts, places = mix_places(n, keys - STEP_ROWS, keys), mix_places(n, 0, keys)
                per = GPS // len(places)
                for m, last in enumerate(lasts):
                    dve.tensor_tensor(last, last, causal[:, m * per:(m + 1) * per, :], ALU.add).then_inc(masked, 1)
                for m, place in enumerate(places):
                    dve.wait_ge(masked, places_until(n) + m + 1)
                    dve.tensor_reduce(top[:, n % RING, m * per:(m + 1) * per], place, X, ALU.max).then_inc(top_done, 1)
                dve.wait_ge(top_done, places_until(n + 1) if len(places) > 1 else places_until(n) + 1)
                if n >= RING:
                    dve.wait_ge(exp_done, GPS * (n - RING + 1))
                dve.tensor_scalar(neg_top[:, n % RING, :], top[:, n % RING, :], -1.0, None, ALU.mult).then_inc(neg_done, 1)

            def invert(n):
                dve.wait_ge(exp_done, GPS * (n + 1))
                dve.reciprocal(inv_total[:, n % RING, :], total[:, n % RING, :]).then_inc(inv_done, 1)
                dve.wait_ge(inv_done, n + 1)
                if n >= RING:
                    dve.wait_ge(post_made, n - RING + 1)
                for g in range(GPS):
                    dve.tensor_scalar(kron_scaled[:, n % RING, g, :], kron[:, 1, :, :], inv_total[:, n % RING, g:g + 1],
                                      None, ALU.mult).then_inc(kron_done, 1)

            def copy_mixed(n):
                dve.wait_ge(post_made, n + 1)
                ins = dve.tensor_copy(mixed_place(n, mixed_mem), mixed_source(n, MEM, 1, GPS * P))
                if n % SA_STEPS >= SA_STEPS // QT:
                    ins = dve.tensor_copy(mixed_place(n, mixed[1], P), mixed_source(n, P, 1, 0))
                ins.then_inc(mixed_by_dve, 1)

            def copy_scores(b, t):
                for n in range((b * QT + t) * PAIRS + 1, (b * QT + t + 1) * PAIRS, 2):
                    copy_dots(dve, scaled_copy, n)

            copy_projections(0, NQK)
            for t in range(QT):
                copy_scores(0, t)
                copy_projections(NQK + t * NV, NQK + (t + 1) * NV)
            for b in range(BATCH):
                first = b * SA_STEPS
                for n in range(first, first + SA_STEPS):
                    maximum(n)
                    if n >= first + 1:
                        invert(n - 1)
                    if n >= first + 2:
                        copy_mixed(n - 2)
                invert(first + SA_STEPS - 1)
                copy_mixed(first + SA_STEPS - 2)
                copy_mixed(first + SA_STEPS - 1)
                if b < BATCH - 1:
                    for t in range(QT):
                        copy_scores(b + 1, t)
                for n in range(b * QT, (b + 1) * QT):
                    dve.wait_ge(y_made, n + 1)
                    dve.tensor_tensor(x_res[:, n, :], x_res[:, n, :], bank[2 + n % 2][:, 1, 0:D], ALU.add
                                      ).then_inc(y_added, 1)

        @block.tensor
        def _(pe):
            mm = pe.matmul
            pe.wait_ge(norm_chain, NORMALISED)
            for c in range(DC):
                for t in range(TOK_TILES):
                    last = pe.transpose(bank[0][:, c, t * P:(t + 1) * P], xn[:, t, c * P:(c + 1) * P], ident[:, :])
                last.then_inc(xT_made, 1)
            pe.wait_ge(xT_copied, DC)
            pe.wait_ge(wq_in, 16)

            def small_constants():
                pe.wait_ge(small_in, 16 * (3 + PAIRS))
                pe.wait_ge(consts, 3 + GPS * STEP_ROWS)
                mm(bank[3][:, 0, 0:2 * HEADS], spread[:, :], proj_sb[:, :, :].rearrange("p a k -> p (a k)"),
                   start=True, stop=True).then_inc(kron_made, 1)
                pe.transpose(bank[3][:, 1, 0:P], memk_sb[:, :, :].rearrange("p a d -> p (a d)"), ident[:, :]
                             ).then_inc(memk_made, 1)

            def project(n):
                kind, m = projections[n]
                if n == 1:
                    pe.wait_ge(wkv_in, 16)
                if n == 3:
                    small_constants()
                    pe.wait_ge(memk_copied, BATCH)
                if n >= 4:
                    back = 4 if n < NQK else 2
                    pe.wait_ge(proj_copied[n % 2], (n - back) // 2 + 1)
                for c in range(DC):
                    if kind == Q:
                        w, a = wq_sb[:, c, m * P:(m + 1) * P], xnT[:, c, :]
                    elif kind == K:
                        w, a = wkv_sb[:, c, m * P:(m + 1) * P], xnT[:, c, :]
                    else:
                        at = INNER + (m % 2) * 512
                        w, a = xnT[:, c, (m // 2) * P:(m // 2 + 1) * P], wkv_sb[:, c, at:at + 512]
                    last = mm(projection_bank(n), w, a, start=(c == 0), stop=(c == DC - 1))
                last.then_inc(proj_made, 1)

            def dots(n):
                t, b, pair = n // PAIRS % QT, n // PAIRS // QT, n % PAIRS
                keys = dot_keys(t)
                if n >= 2:
                    pe.wait_ge(dots_copied[n % 2], (n - 2) // 2 + 1)
                for half in range(2):
                    tokens = (b * QT + t) * P
                    last = mm(bank[n % 2][:, half, 0:keys], q_padded[:, 2 * pair + half, tokens:tokens + P],
                              kT[:, pair, b, 0:keys], start=True, stop=True)
                last.then_inc(dots_made, 1)

            def mix(n):
                b, s = n // SA_STEPS, n % SA_STEPS
                keys = step_keys(s)
                if s % (SA_STEPS // QT) == 0:
                    for pair in range(PAIRS):
                        pe.wait_ge(regrouped[pair], 32 * (b * QT + s // (SA_STEPS // QT) + 1))
                if n >= RING:
                    pe.wait_ge(exp_done, GPS * (n - RING + 1))
                for g in range(GPS):
                    group = s * GPS + g
                    last = mm(mix_group(n, g, keys), kron[:, 0, :, :].rearrange("p k r -> p (k r)"),
                              grouped[:, group // (P // ROWS), group % (P // ROWS), 0:keys], start=True, stop=True)
                last.then_inc(mix_made, 1)

            def post(n):
                b, s = n // SA_STEPS, n % SA_STEPS
                pe.wait_ge(kron_done, GPS * (n + 1))
                pe.wait_ge(tail_zero, b * RING + min(s + 1, RING))
                if n >= 2:
                    pe.wait_ge(mixed_by_act, n - 1)
                    pe.wait_ge(mixed_by_dve, n - 1)
                for g in range(GPS):
                    e, k = expd[:, n % RING, g, :], kron_scaled[:, n % RING, g, :]
                    mm(bank[n % 2][0:MEM, 1, (GPS + g) * P:(GPS + g + 1) * P], e[:, 0:MEM], k, start=True, stop=True)
                    last = mm(bank[n % 2][:, 0, g * P:(g + 1) * P], e[:, MEM:MEM + P], k, start=True, stop=True)
                    if s >= SA_STEPS // QT:
                        last = mm(bank[n % 2][:, 1, g * P:(g + 1) * P], e[:, MEM + P:KEYS], k, start=True, stop=True)
                last.then_inc(post_made, 1)

            def product_with_v(n):
                b, pair = n // PAIRS, n % PAIRS
                if n % PAIRS >= 2 :
                    pe.wait_ge(out_copied, n - 1)
                for half in range(2):
                    k = 2 * pair + half
                    out = bank[2 + n % 2][half * DH:(half + 1) * DH, 0, :]
                    mm(out[:, 0:SEQ], memv_sb[:, k, :], mixed_mem[:, k, :], start=True, stop=False)
                    mm(out[:, 0:SEQ], v_sb[:, b * QT, k * DH:(k + 1) * DH], mixed[0][:, k, :], start=False, stop=False)
                    last = mm(out[:, P:SEQ], v_sb[:, b * QT + 1, k * DH:(k + 1) * DH], mixed[1][:, k, :],
                              start=False, stop=True)
                last.then_inc(out_made, 1)

            def output(n):
                for pair in range(PAIRS):
                    last = mm(bank[2 + n % 2][:, 1, 0:D], outT[:, pair, n % QT * P:(n % QT + 1) * P], wo_sb[:, pair, :],
                              start=(pair == 0), stop=(pair == PAIRS - 1))
                last.then_inc(y_made, 1)

            def all_dots(b, t):
                for n in range((b * QT + t) * PAIRS, (b * QT + t + 1) * PAIRS):
                    dots(n)

            for n in range(NQK):
                project(n)
            for eng in range(2):
                pe.wait_ge(proj_copied[eng], NQK // 2)
            pe.wait_ge(zeroed, 2)
            for t in range(QT):
                all_dots(0, t)
                for n in range(NQK + t * NV, NQK + (t + 1) * NV):
                    project(n)
            for eng in range(2):
                pe.wait_ge(proj_copied[eng], NPROJ // 2)
            for m in (GATE, UP):
                pe.wait_ge(hidden_chain, (m + 1) * W_OPS)
                for k in range(4 * WT_BANKS):
                    at = m * WT_BANKS + k // 4
                    if k % 4 == 0 and at >= 4:
                        pe.wait_ge(hidden_copied, at - 3)
                    last = transpose_weight(pe, hidden_w[m], FC, k, hidden_bank(at)[:, k % 4 * P:(k % 4 + 1) * P], ident)
                    if k % 4 == 3:
                        last.then_inc(hidden_made, 1)
            pe.wait_ge(hidden_copied, 2 * WT_BANKS)
            pe.wait_ge(wo_in, 16)
            for b in range(BATCH):
                first = b * SA_STEPS
                for eng in range(2):
                    pe.wait_ge(dots_copied[eng], (b + 1) * QT * PAIRS // 2)
                if b > 0:
                    pe.wait_ge(y_added, b * QT)
                for n in range(first, first + SA_STEPS + RING - 1):
                    if n < first + SA_STEPS:
                        mix(n)
                    if n >= first + RING - 1:
                        post(n - RING + 1)
                pe.wait_ge(mixed_by_act, first + SA_STEPS)
                pe.wait_ge(mixed_by_dve, first + SA_STEPS)
                if b < BATCH - 1:
                    for t in range(QT):
                        all_dots(b + 1, t)
                for n in range(b * PAIRS, (b + 1) * PAIRS):
                    product_with_v(n)
                pe.wait_ge(out_copied, (b + 1) * PAIRS)
                for n in range(b * QT, (b + 1) * QT):
                    output(n)


def gated_ffn(nc, w_down, hidden_wT, x_res, out, ident):
    A_MAX = 2.0 ** 15 - 1.0
    U_STEPS = 65536.0
    N = BATCH * SEQ
    TOP, BOTH, SCL, INV = FC, FC + 1, FC + 2, FC + 3

    with ExitStack() as stack:
        r = Resources(nc, stack)
        w_down_sb = r.sbuf("w_down_sb", [P, FF * D // P])
        w_scales = r.sbuf("w_scales3", [P, 4, NB])
        downT = r.sbuf("downT", [P, FC, D])
        xn = r.sbuf("xn3", [P, TOK_TILES, D])
        xqT = r.sbuf("xqT", [P, DC, N])
        stats = r.sbuf("stats3", [P, TOK_TILES, 6])
        moments = r.sbuf("moments3", [P, TOK_TILES, 2])
        power = r.sbuf("power3", [P, TOK_TILES])
        gate = r.sbuf("gate", [P, FC, N])
        up = r.sbuf("up", [P, FC, N])
        sig = r.sbuf("sig", [P, FC, N])
        magnitude = r.sbuf("magnitude", [P, 4, N])
        limits = r.sbuf("limits", [P, 5, FC + 4])
        round_bias = r.sbuf("round_bias", [P, 1])
        bank = [r.psum(f"ffn_bank{n}", [P, 512]) for n in range(8)]

        w_in = r.sem("w_in3")
        norm_chain = r.sem("norm_chain3")
        inverse_std = r.sem("inverse_std3")
        w_chain = r.sem("w_chain")
        magnitude_made = r.sem("magnitude_made")
        magnitude_read = r.sem("magnitude_read")
        top_found = r.sem("top_found")
        peak = r.sem("peak")
        scaled = r.sem("scaled")
        q_chain = r.sem("q_chain")
        up_chain = r.sem("up_chain")
        bias_ready = r.sem("bias_ready")
        first_pass = r.sem("first_pass")
        sig_scaled = r.sem("sig_scaled")
        xqT_made = r.sem("xqT_made")
        xqT_copied = r.sem("xqT_copied")
        wT_made = r.sem("wT_made")
        wT_copied = r.sem("wT_copied")
        hidden_made = r.sem("hidden_made")
        hidden_copied = r.sem("hidden_copied")
        sig_made = r.sem("sig_made")
        sig_chain = r.sem("sig_chain")
        multiplied = r.sem("multiplied")
        y_made = r.sem("y_made3")
        y_added = r.sem("y_added3")
        stored = r.sem("stored")

        INPUT, GATES, UPS, GATED, PRODUCT = range(5)
        CHUNKS = [TOK_TILES * D // 512, FC, FC, FC, FC]
        BEFORE = [sum(CHUNKS[:n]) for n in range(6)]
        PIECES = [1, 3, 0, 3, TOK_TILES]
        PASSES = 3

        def order(which):
            n = PIECES[which]
            if which in (INPUT, GATES, UPS):
                return [(m, k) for m in range(PASSES) for k in range(n)]
            rest = [(m, k) for k in range(1, n) for m, k in ((1, k), (2, k - 1)) if k > 0]
            return [(0, 0), (1, 0), (2, 0)] + rest + [(2, n - 1)]

        ROUNDED = [sum(len(order(m)) for m in range(n + 1)) for n in range(5)]

        def pass_count(which, m, k):
            return ROUNDED[which] - len(order(which)) + order(which).index((m, k)) + 1

        thirds = [slice(k * FC // 3, (k + 1) * FC // 3) for k in range(3)]

        def round_pass(eng, which, m, t):
            inverse, scale = limits[:, which, INV:INV + 1], limits[:, which, SCL:SCL + 1]
            one, two, op_one, op_two = ((inverse, ROUND, ALU.mult, ALU.add),
                                        (ROUND, A_MAX, ALU.subtract, ALU.min),
                                        (-A_MAX - 1.0, scale, ALU.max, ALU.mult))[m]
            return eng.tensor_scalar(t, t, one, two, op_one, op_two)

        def pieces(which):
            if which == INPUT:
                return [xn[:, :, :].rearrange("p t d -> p (t d)")]
            if which == PRODUCT:
                return [sig[:, :, t * P:(t + 1) * P] for t in range(TOK_TILES)]
            tensor = {GATES: gate, UPS: up, GATED: sig}[which]
            return [tensor[:, piece, :] for piece in thirds]

        def hidden_bank(n):
            return bank[n % 6]

        block = stack.enter_context(nc.Block())

        @block.sync
        def _(sp):
            load_ffn_weight(sp, w_down_sb[:, :], w_down, w_in)
            for t in range(TOK_TILES):
                sp.wait_ge(y_added, t + 1)
                sp.dma_start(out.rearrange("b (t p) d -> p (b t) d", p=P)[:, t, :], x_res[:, t, :]).then_inc(stored, 16)
            sp.wait_ge(stored, 16 * TOK_TILES)

        @block.gpsimd
        def _(pool):
            pool.memset(round_bias[:, :], ROUND).then_inc(bias_ready, 1)
            invert_std(pool, moments, power, norm_chain, inverse_std)
            for n in range(5):
                pool.wait_ge(top_found, n + 1)
                pool.partition_all_reduce(limits[:, n, BOTH:BOTH + 1], limits[:, n, TOP:TOP + 1], P,
                                          bass.bass_isa.ReduceOp.max).then_inc(peak, 1)
                if n == UPS:
                    pool.wait_ge(hidden_copied, 2 * FC)
                    pool.wait_ge(scaled, 2 * UPS + 2)
                    round_pass(pool, UPS, 0, up[:, :, :].rearrange("p c n -> p (c n)")).then_inc(up_chain, 1)
                    pool.wait_ge(up_chain, 1)

        @block.scalar
        def _(act):
            def magnitudes(which, c, src):
                n = BEFORE[which] + c
                if n >= 4:
                    act.wait_ge(magnitude_read, n - 3)
                act.activation(magnitude[:, n % 4, :], src, ACT.Abs).then_inc(magnitude_made, 1)

            act.wait_ge(norm_chain, NORMALISED)
            xflat = xn[:, :, :].rearrange("p t d -> p (t d)")
            for c in range(CHUNKS[INPUT]):
                magnitudes(INPUT, c, xflat[:, c * 512:(c + 1) * 512])
            for which, place in ((GATES, gate), (UPS, up)):
                for c in range(FC):
                    n = (which - GATES) * FC + c
                    act.wait_ge(hidden_made, n + 1)
                    act.activation(place[:, c, :], hidden_bank(n)[:, :], ACT.Copy).then_inc(hidden_copied, 1)
                    magnitudes(which, c, hidden_bank(n)[:, :])
                    if which == UPS and c >= FC - len(thirds):
                        k = c - FC + len(thirds)
                        act.wait_ge(q_chain, pass_count(GATES, 2, k))
                        act.activation(sig[:, thirds[k], :], gate[:, thirds[k], :], ACT.Sigmoid).then_inc(sig_made, 1)
                    if which == UPS and c % 2 == 1:
                        n = c // 2
                        act.wait_ge(wT_made, n + 1)
                        act.activation(downT[:, 2 * n:2 * n + 2, :].rearrange("p c d -> p (c d)"),
                                       bank[6 + n % 2][:, :], ACT.Copy).then_inc(wT_copied, 1)
            act.wait_ge(bias_ready, 1)
            for k, piece in enumerate(thirds):
                act.wait_ge(sig_made, k + 1)
                act.activation(sig[:, piece, :], sig[:, piece, :], ACT.Identity, bias=round_bias[:, 0:1],
                               scale=U_STEPS).then_inc(sig_scaled, 1)
            for which in (GATED, PRODUCT):
                for c in range(FC):
                    act.wait_ge(multiplied, (which - GATED) * FC + c + 1)
                    magnitudes(which, c, sig[:, c, :])
                act.wait_ge(scaled, 2 * which + 2)
                for t in pieces(which)[1:]:
                    act.activation(t, t, ACT.Identity, bias=round_bias[:, 0:1], scale=limits[:, which, INV:INV + 1]
                                   ).then_inc(first_pass, 1)

        @block.vector
        def _(dve):
            def maximum(which, c):
                n = BEFORE[which] + c
                dve.wait_ge(magnitude_made, n + 1)
                dve.tensor_reduce(limits[:, which, c:c + 1], magnitude[:, n % 4, :], X, ALU.max
                                  ).then_inc(magnitude_read, 1)

            def find_scale(which):
                a = limits[:, which, :]
                dve.wait_ge(magnitude_read, BEFORE[which + 1])
                dve.tensor_reduce(a[:, TOP:TOP + 1], a[:, 0:CHUNKS[which]], X, ALU.max).then_inc(top_found, 1)
                dve.wait_ge(peak, which + 1)
                dve.tensor_scalar(a[:, SCL:SCL + 1], a[:, BOTH:BOTH + 1], 1.0 / A_MAX, TINY, ALU.mult, ALU.max
                                  ).then_inc(scaled, 1)
                dve.wait_ge(scaled, 2 * which + 1)
                dve.reciprocal(a[:, INV:INV + 1], a[:, SCL:SCL + 1]).then_inc(scaled, 1)
                dve.wait_ge(scaled, 2 * which + 2)

            def round_pieces(which):
                for m, k in order(which):
                    if m == 1 and k > 0 and which in (GATED, PRODUCT):
                        before = PIECES[GATED] - 1 if which == PRODUCT else 0
                        dve.wait_ge(first_pass, before + k)
                    elif m > 0:
                        dve.wait_ge(q_chain, pass_count(which, m - 1, k))
                    round_pass(dve, which, m, pieces(which)[k]).then_inc(q_chain, 1)

            def multiply(which, factor):
                for c in range(FC):
                    dve.tensor_tensor(sig[:, c, :], sig[:, c, :], factor[:, c, :], ALU.mult).then_inc(multiplied, 1)
                    if c >= 2:
                        maximum(which, c - 2)
                maximum(which, FC - 2)
                maximum(which, FC - 1)

            normalise_rows(dve, x_res, xn, stats, moments, norm_chain, inverse_std)
            for c in range(CHUNKS[INPUT]):
                maximum(INPUT, c)
            dve.wait_ge(norm_chain, NORMALISED)
            find_scale(INPUT)
            round_pieces(INPUT)
            for c in range(DC):
                dve.wait_ge(xqT_made, c + 1)
                dve.tensor_copy(xqT[:, c, :], bank[6 + c][:, :]).then_inc(xqT_copied, 1)
            dve.wait_ge(w_in, 16)
            for part in range(W_PARTS // 2):
                quantise_weight(dve, part, w_down_sb[:, :], w_scales, w_chain, 0)
            for c in range(FC):
                maximum(GATES, c)
                if c < W_PARTS // 2:
                    quantise_weight(dve, W_PARTS // 2 + c, w_down_sb[:, :], w_scales, w_chain, 0)
            dve.wait_ge(hidden_copied, FC)
            find_scale(GATES)
            round_pieces(GATES)
            for c in range(FC):
                maximum(UPS, c)
            find_scale(UPS)
            passes = ((ROUND, U_STEPS - 1.0, ALU.subtract, ALU.min),
                      (0.0, 1.0 / U_STEPS, ALU.max, ALU.mult))
            for m, (one, two, op_one, op_two) in enumerate(passes):
                for k, piece in enumerate(thirds):
                    if m == 0:
                        dve.wait_ge(sig_scaled, k + 1)
                    else:
                        dve.wait_ge(sig_chain, k + 1)
                    t = sig[:, piece, :]
                    dve.tensor_scalar(t, t, one, two, op_one, op_two).then_inc(sig_chain, 1)
            for m in (1, 2):
                for k, piece in enumerate(thirds):
                    dve.wait_ge(up_chain, 1 if m == 1 else 2 + k)
                    round_pass(dve, UPS, m, up[:, piece, :]).then_inc(up_chain, 1)
            dve.wait_ge(sig_chain, 2 * len(thirds))
            dve.wait_ge(q_chain, ROUNDED[GATES])
            multiply(GATED, gate)
            dve.wait_ge(multiplied, FC)
            find_scale(GATED)
            round_pieces(GATED)
            dve.wait_ge(q_chain, ROUNDED[GATED])
            dve.wait_ge(up_chain, 1 + 2 * len(thirds))
            multiply(PRODUCT, up)
            dve.wait_ge(multiplied, 2 * FC)
            find_scale(PRODUCT)
            round_pieces(PRODUCT)
            for t in range(TOK_TILES):
                dve.wait_ge(y_made, t + 1)
                dve.tensor_tensor(x_res[:, t, :], x_res[:, t, :], bank[t][:, 0:D], ALU.add).then_inc(y_added, 1)

        @block.tensor
        def _(pe):
            mm = pe.matmul
            pe.wait_ge(q_chain, ROUNDED[INPUT])
            for c in range(DC):
                for t in range(TOK_TILES):
                    last = pe.transpose(bank[6 + c][:, t * P:(t + 1) * P], xn[:, t, c * P:(c + 1) * P], ident[:, :])
                last.then_inc(xqT_made, 1)
            pe.wait_ge(xqT_copied, DC)
            for n in range(2 * FC):
                if n >= 6:
                    pe.wait_ge(hidden_copied, n - 5)
                    pe.wait_ge(magnitude_made, BEFORE[GATES] + n - 5)
                w = hidden_wT[:, n // FC, :].rearrange("p (c f) -> p c f", c=DC)
                for c in range(DC):
                    last = mm(hidden_bank(n)[:, :], w[:, c, n % FC * P:(n % FC + 1) * P], xqT[:, c, :],
                              start=(c == 0), stop=(c == DC - 1))
                last.then_inc(hidden_made, 1)
                if n >= FC and n % 2 == 1:
                    at = (n - FC) // 2
                    pe.wait_ge(w_chain, W_OPS)
                    if at >= 2:
                        pe.wait_ge(wT_copied, at - 1)
                    for k in range(4):
                        last = transpose_weight(pe, w_down_sb[:, :], DC, at * 4 + k,
                                                bank[6 + at % 2][:, k * P:(k + 1) * P], ident)
                    last.then_inc(wT_made, 1)
            pe.wait_ge(wT_copied, WT_BANKS)
            pe.wait_ge(hidden_copied, 2 * FC)
            pe.wait_ge(magnitude_made, BEFORE[GATED])
            for t in range(TOK_TILES):
                pe.wait_ge(q_chain, pass_count(PRODUCT, 2, t))
                for c in range(FC):
                    last = mm(bank[t][:, 0:D], sig[:, c, t * P:(t + 1) * P], downT[:, c, :],
                              start=(c == 0), stop=(c == FC - 1))
                last.then_inc(y_made, 1)


def load_identity(nc, ident):
    with ExitStack() as stack:
        r = Resources(nc, stack)
        cleared = r.sem("cleared")
        block = stack.enter_context(nc.Block())

        @block.gpsimd
        def _(pool):
            pool.memset(ident[:, :], 0.0).then_inc(cleared, 1)
            pool.wait_ge(cleared, 1)
            pool.affine_select(out=ident[:, :], in_=ident[:, :], compare_op=ALU.not_equal, fill=1.0, base=0,
                               pattern=[[-1, P]], channel_multiplier=1).then_inc(cleared, 1)
            pool.wait_ge(cleared, 2)


def perceiver_layer(nc, x, ctx_1024, x_w_q, x_w_k, x_w_v, x_w_o, a_w_q, a_w_kv, a_w_o, pre_proj, post_proj,
                    mem_k, mem_v, w_gate, w_up, w_down, out):
    with ExitStack() as stack:
        r = Resources(nc, stack)
        ident = r.sbuf("ident", [P, P])
        x_res = r.sbuf("x_res", [P, TOK_TILES, D])
        load_identity(nc, ident)
        cross_attention(nc, x, ctx_1024, x_w_q, x_w_k, x_w_v, x_w_o, x_res, ident)
        hidden_wT = r.sbuf("hidden_wT", [P, 2, FF * D // P])
        self_attention(nc, a_w_q, a_w_kv, a_w_o, pre_proj, post_proj, mem_k, mem_v, w_gate, w_up, hidden_wT,
                       x_res, ident)
        gated_ffn(nc, w_down, hidden_wT, x_res, out, ident)


_INS = ['x', 'ctx_1024', 'L0_xattn_w_q', 'L0_xattn_w_k', 'L0_xattn_w_v', 'L0_xattn_w_o', 'L0_attn_Wq',
        'L0_attn_Wkv', 'L0_attn_Wo', 'L0_attn_pre_proj', 'L0_attn_post_proj', 'L0_attn_mem_k', 'L0_attn_mem_v',
        'L0_ffn_w_gate', 'L0_ffn_w_up', 'L0_ffn_w_down']
_OUTS = [((2, 256, 256), 'float32')]


def kernel(**inputs):
    import numpy as _np
    import concourse.bacc as _bacc
    from concourse import mybir as _mybir
    from concourse.bass_utils import run_bass_kernel_spmd as _run

    nc = _bacc.Bacc("TRN2", target_bir_lowering=False, num_devices=1)
    arrays, args = {}, []
    for name in _INS:
        a = _np.ascontiguousarray(inputs[name])
        arrays[f"in_{name}_dram"] = a
        args.append(nc.dram_tensor(f"in_{name}_dram", a.shape, _mybir.dt.from_np(a.dtype), kind="ExternalInput").ap())
    for i, (shape, dtype) in enumerate(_OUTS):
        dt = _mybir.dt.from_np(_np.dtype(dtype))
        args.append(nc.dram_tensor(f"out_{i}_dram", shape, dt, kind="ExternalOutput").ap())
    perceiver_layer(nc, *args)
    r = _run(nc, [arrays], core_ids=[0])
    got = tuple(r.results[0][f"out_{i}_dram"] for i in range(len(_OUTS)))
    return got[0]
```
